# Optimizing a Trainium2 kernel written in Bass

```python
import numpy as np
import jax
import jax.numpy as jnp

def _softmax(x, axis=-1):
    return jax.nn.softmax(x, axis=axis)

def _gelu(x):
    return jax.nn.gelu(x, approximate=True)

def _silu(x):
    return jax.nn.silu(x)

def _sigmoid(x):
    return jax.nn.sigmoid(x)

def _layernorm(x, axis=-1, eps=1e-05):
    m = jnp.mean(x, axis=axis, keepdims=True)
    v = jnp.var(x, axis=axis, keepdims=True)
    return (x - m) / jnp.sqrt(v + eps)

def _scatter_add(tgt, idx, src, axis=0):
    return tgt.at[idx].add(src)

def _segment_sum(src, seg, n):
    return jax.ops.segment_sum(src, seg, n)
kernel_name = 'mk_gps_d2_gnn_r16_37ac4c'

def setup_inputs(seed: int=0):
    np.random.seed(seed)
    _w = jnp.asarray

    def _rec_inputs():
        import jax
        import jax.numpy as jnp
        _gk = jax.random.key(seed)
        x = -0.0006008 + 1.001 * jax.random.normal(jax.random.fold_in(_gk, 1), (3125, 256), jnp.float32)
        _s = jax.random.randint(jax.random.fold_in(_gk, 2), (50000,), 0, 3125, jnp.int32)
        _d = jax.random.randint(jax.random.fold_in(_gk, 3), (50000,), 0, 3125, jnp.int32)
        _loop = jnp.arange(3125, dtype=jnp.int32)
        src = jnp.concatenate([_s, _d, _loop])
        dst = jnp.concatenate([_d, _s, _loop])
        _o = jnp.argsort(dst, stable=True)
        src = src[_o]
        dst = dst[_o]
        edge_type_8 = jax.random.randint(jax.random.fold_in(_gk, 12), (103125,), 0, 8, jnp.int32)
        return (x, src, dst, edge_type_8)
    x, src, dst, edge_type_8 = _rec_inputs()

    def _L0_gnn_setup():
        import jax, jax.numpy as jnp
        import numpy as np
        N_NODES = 625
        N_EDGES = 20000
        D = 256
        key = jax.random.key(seed)
        k1, k2, k3, k4, k5 = jax.random.split(key, 5)
        x = jax.random.normal(k1, (N_NODES, D), dtype=jnp.float32)
        src = jax.random.randint(k2, (N_EDGES,), 0, N_NODES, dtype=jnp.int32)
        dst = jax.random.randint(k3, (N_EDGES,), 0, N_NODES, dtype=jnp.int32)
        s = 1.0 / np.sqrt(D)
        theta_w = jax.random.uniform(k4, (D, D), jnp.float32, -s, s)
        theta_b = jnp.zeros((D,), jnp.float32)
        phi_w = jax.random.uniform(k5, (D, D), jnp.float32, -s, s)
        phi_b = jnp.zeros((D,), jnp.float32)
        return {'x': x, 'src': src, 'dst': dst, 'theta_w': theta_w, 'theta_b': theta_b, 'phi_w': phi_w, 'phi_b': phi_b}
    _L0_gnn_all = _L0_gnn_setup()
    _L0_gnn_in = {k: v for k, v in _L0_gnn_all.items() if k in ('theta_w', 'theta_b', 'phi_w', 'phi_b')}
    del _L0_gnn_all

    def _L0_mix_setup():
        import math
        import jax, jax.numpy as jnp
        import numpy as np
        EPS_DIV = 1e-07
        EPS_NORM = 1e-12

        def _l2_normalize(x, axis):
            n = jnp.sqrt(jnp.sum(x * x, axis=axis, keepdims=True))
            return x / jnp.maximum(n, EPS_NORM)
        key = jax.random.key(seed)
        ks = jax.random.split(key, 5)
        b, N, C = (8, 256, 256)
        x = jax.random.normal(ks[0], (b, N, C), dtype=jnp.float32)
        W_qkv = jax.random.normal(ks[1], (C, 3 * C), dtype=jnp.float32) * (1.0 / math.sqrt(C))
        b_qkv = jax.random.normal(ks[2], (3 * C,), dtype=jnp.float32) * 0.02
        W_out = jax.random.normal(ks[3], (C, C), dtype=jnp.float32) * (1.0 / math.sqrt(C))
        b_out = jax.random.normal(ks[4], (C,), dtype=jnp.float32) * 0.02
        return {'x': x, 'W_qkv': W_qkv, 'b_qkv': b_qkv, 'W_out': W_out, 'b_out': b_out}
    _L0_mix_all = _L0_mix_setup()
    _L0_mix_in = {k: v for k, v in _L0_mix_all.items() if k in ('W_qkv', 'b_qkv', 'W_out', 'b_out')}
    del _L0_mix_all

    def _L0_ffn_setup():
        import math
        import jax, jax.numpy as jnp
        import numpy as np
        CAPACITY_FACTOR = 1.25
        TOP_K = 2
        LN_EPS = 1e-05

        def _layer_norm(x, gamma, beta):
            mu = jnp.mean(x, axis=-1, keepdims=True)
            var = jnp.var(x, axis=-1, keepdims=True)
            return (x - mu) * jax.lax.rsqrt(var + LN_EPS) * gamma + beta
        key = jax.random.key(seed)
        ks = jax.random.split(key, 4)
        B, S, D, F, E = (8, 256, 256, 512, 8)
        x = jax.random.normal(ks[0], (B, S, D), dtype=jnp.float32)
        Wr = jax.random.normal(ks[1], (D, E), dtype=jnp.float32) / np.sqrt(D)
        br = jnp.zeros((E,), jnp.float32)
        W1 = jax.random.normal(ks[2], (E, D, F), dtype=jnp.float32) / np.sqrt(D)
        b1 = jnp.zeros((E, F), jnp.float32)
        W2 = jax.random.normal(ks[3], (E, F, D), dtype=jnp.float32) / np.sqrt(F)
        b2 = jnp.zeros((E, D), jnp.float32)
        gamma = jnp.ones((D,), jnp.float32)
        beta = jnp.zeros((D,), jnp.float32)
        return {'x': x, 'Wr': Wr, 'br': br, 'W1': W1, 'b1': b1, 'W2': W2, 'b2': b2, 'gamma': gamma, 'beta': beta}
    _L0_ffn_all = _L0_ffn_setup()
    _L0_ffn_in = {k: v for k, v in _L0_ffn_all.items() if k in ('Wr', 'br', 'W1', 'b1', 'W2', 'b2', 'gamma', 'beta')}
    del _L0_ffn_all

    def _L1_gnn_setup():
        import jax, jax.numpy as jnp
        import numpy as np
        N_NODES = 1250
        N_EDGES = 40000
        D = 256
        N_RELS = 8
        N_BASES = 4
        LN_EPS = 1e-05
        key = jax.random.key(seed)
        ks = jax.random.split(key, 8)
        node_feats = jax.random.normal(ks[0], (N_NODES, D), dtype=jnp.float32)
        src = jax.random.randint(ks[1], (N_EDGES,), 0, N_NODES, dtype=jnp.int32)
        dst = jax.random.randint(ks[2], (N_EDGES,), 0, N_NODES, dtype=jnp.int32)
        edge_types = jax.random.randint(ks[3], (N_EDGES,), 0, N_RELS, dtype=jnp.int32)
        basis = jax.random.normal(ks[4], (N_BASES, D, D), dtype=jnp.float32) * (1.0 / np.sqrt(D))
        comp = jax.random.normal(ks[5], (N_RELS, N_BASES), dtype=jnp.float32) * (1.0 / np.sqrt(N_BASES))
        loop_w = jax.random.normal(ks[6], (D, D), dtype=jnp.float32) * (1.0 / np.sqrt(D))
        h_bias = jnp.zeros((D,), dtype=jnp.float32)
        ln_gamma = jnp.ones((D,), dtype=jnp.float32)
        ln_beta = jnp.zeros((D,), dtype=jnp.float32)
        return {'node_feats': node_feats, 'src': src, 'dst': dst, 'edge_types': edge_types, 'basis': basis, 'comp': comp, 'loop_w': loop_w, 'h_bias': h_bias, 'ln_gamma': ln_gamma, 'ln_beta': ln_beta}
    _L1_gnn_all = _L1_gnn_setup()
    _L1_gnn_in = {k: v for k, v in _L1_gnn_all.items() if k in ('basis', 'comp', 'loop_w', 'h_bias', 'ln_gamma', 'ln_beta')}
    del _L1_gnn_all

    def _L1_mix_setup():
        import jax, jax.numpy as jnp
        import numpy as np
        HEADS = 4
        DIM_HEAD = 32
        key = jax.random.key(seed)
        k1, k2, k3 = jax.random.split(key, 3)
        B, L, D = (16, 512, 256)
        hidden = HEADS * DIM_HEAD
        x = jax.random.normal(k1, (B, L, D), dtype=jnp.float32)
        W_qkv = jax.random.normal(k2, (D, 3 * hidden), dtype=jnp.float32) * D ** (-0.5)
        W_out = jax.random.normal(k3, (hidden, D), dtype=jnp.float32) * hidden ** (-0.5)
        b_out = jnp.zeros((D,), dtype=jnp.float32)
        return {'x': x, 'W_qkv': W_qkv, 'W_out': W_out, 'b_out': b_out}
    _L1_mix_all = _L1_mix_setup()
    _L1_mix_in = {k: v for k, v in _L1_mix_all.items() if k in ('W_qkv', 'W_out', 'b_out')}
    del _L1_mix_all

    def _L1_ffn_setup():
        import jax, jax.numpy as jnp
        import numpy as np
        E = 8
        K = 2
        D = 256
        H = 512
        DOUT = 256
        EPS = 1e-05
        key = jax.random.key(seed)
        ks = jax.random.split(key, 9)
        s = 0.02
        return {'x': jax.random.normal(ks[0], (4, 512, D), jnp.float32), 'gamma': 1.0 + 0.05 * jax.random.normal(ks[1], (D,), jnp.float32), 'beta': 0.05 * jax.random.normal(ks[2], (D,), jnp.float32), 'Wr': 0.01 * jax.random.normal(ks[3], (D, E), jnp.float32), 'br': jnp.zeros((E,), jnp.float32), 'W1': s * jax.random.normal(ks[4], (E, D, H), jnp.float32), 'b1': s * jax.random.normal(ks[5], (E, H), jnp.float32), 'W2': s * jax.random.normal(ks[6], (E, H, DOUT), jnp.float32), 'b2': s * jax.random.normal(ks[7], (E, DOUT), jnp.float32)}
    _L1_ffn_all = _L1_ffn_setup()
    _L1_ffn_in = {k: v for k, v in _L1_ffn_all.items() if k in ('gamma', 'beta', 'Wr', 'br', 'W1', 'b1', 'W2', 'b2')}
    del _L1_ffn_all
    return {'x': x, 'src': src, 'dst': dst, 'edge_type_8': edge_type_8, 'L0_gnn_theta_w': _L0_gnn_in['theta_w'], 'L0_gnn_theta_b': _L0_gnn_in['theta_b'], 'L0_gnn_phi_w': _L0_gnn_in['phi_w'], 'L0_gnn_phi_b': _L0_gnn_in['phi_b'], 'L0_mix_W_qkv': _L0_mix_in['W_qkv'], 'L0_mix_b_qkv': _L0_mix_in['b_qkv'], 'L0_mix_W_out': _L0_mix_in['W_out'], 'L0_mix_b_out': _L0_mix_in['b_out'], 'L0_ffn_Wr': _L0_ffn_in['Wr'], 'L0_ffn_br': _L0_ffn_in['br'], 'L0_ffn_W1': _L0_ffn_in['W1'], 'L0_ffn_b1': _L0_ffn_in['b1'], 'L0_ffn_W2': _L0_ffn_in['W2'], 'L0_ffn_b2': _L0_ffn_in['b2'], 'L0_ffn_gamma': _L0_ffn_in['gamma'], 'L0_ffn_beta': _L0_ffn_in['beta'], 'L1_gnn_basis': _L1_gnn_in['basis'], 'L1_gnn_comp': _L1_gnn_in['comp'], 'L1_gnn_loop_w': _L1_gnn_in['loop_w'], 'L1_gnn_h_bias': _L1_gnn_in['h_bias'], 'L1_gnn_ln_gamma': _L1_gnn_in['ln_gamma'], 'L1_gnn_ln_beta': _L1_gnn_in['ln_beta'], 'L1_mix_W_qkv': _L1_mix_in['W_qkv'], 'L1_mix_W_out': _L1_mix_in['W_out'], 'L1_mix_b_out': _L1_mix_in['b_out'], 'L1_ffn_gamma': _L1_ffn_in['gamma'], 'L1_ffn_beta': _L1_ffn_in['beta'], 'L1_ffn_Wr': _L1_ffn_in['Wr'], 'L1_ffn_br': _L1_ffn_in['br'], 'L1_ffn_W1': _L1_ffn_in['W1'], 'L1_ffn_b1': _L1_ffn_in['b1'], 'L1_ffn_W2': _L1_ffn_in['W2'], 'L1_ffn_b2': _L1_ffn_in['b2']}

def reference(x, src, dst, edge_type_8, L0_gnn_theta_w, L0_gnn_theta_b, L0_gnn_phi_w, L0_gnn_phi_b, L0_mix_W_qkv, L0_mix_b_qkv, L0_mix_W_out, L0_mix_b_out, L0_ffn_Wr, L0_ffn_br, L0_ffn_W1, L0_ffn_b1, L0_ffn_W2, L0_ffn_b2, L0_ffn_gamma, L0_ffn_beta, L1_gnn_basis, L1_gnn_comp, L1_gnn_loop_w, L1_gnn_h_bias, L1_gnn_ln_gamma, L1_gnn_ln_beta, L1_mix_W_qkv, L1_mix_W_out, L1_mix_b_out, L1_ffn_gamma, L1_ffn_beta, L1_ffn_Wr, L1_ffn_br, L1_ffn_W1, L1_ffn_b1, L1_ffn_W2, L1_ffn_b2):
    import jax
    import jax.numpy as jnp

    def _L0_gnn_ref(x, src, dst, theta_w, theta_b, phi_w, phi_b):
        import jax, jax.numpy as jnp
        import numpy as np
        N_NODES = 625
        N_EDGES = 20000
        D = 256
        x_src = x[src]
        x_dst = x[dst]
        theta_x = (x_dst - x_src) @ theta_w.T + theta_b
        phi_x = x_src @ phi_w.T + phi_b
        e = jax.nn.relu(theta_x + phi_x)
        out = jax.ops.segment_max(e, dst, num_segments=x.shape[0])
        return jnp.where(jnp.isfinite(out), out, 0.0)

    def _L0_mix_ref(x, W_qkv, b_qkv, W_out, b_out):
        import math
        import jax, jax.numpy as jnp
        import numpy as np
        EPS_DIV = 1e-07
        EPS_NORM = 1e-12

        def _l2_normalize(x, axis):
            n = jnp.sqrt(jnp.sum(x * x, axis=axis, keepdims=True))
            return x / jnp.maximum(n, EPS_NORM)
        b, N, C = x.shape
        qkv = x @ W_qkv + b_qkv
        q, k, v = jnp.split(qkv, 3, axis=2)
        q = q - jnp.mean(q, axis=2, keepdims=True)
        k = k - jnp.mean(k, axis=2, keepdims=True)
        q2 = q * q
        k2 = k * k
        q2s = jnp.sum(q2, axis=2, keepdims=True)
        k2s = jnp.sum(k2, axis=2, keepdims=True)
        k2 = _l2_normalize(k2 / (k2s + EPS_DIV), axis=-2)
        q2 = _l2_normalize(q2 / (q2s + EPS_DIV), axis=-1)
        kv = jnp.einsum('bnc,bnd->bcd', k2, v)
        t2 = jnp.einsum('bnc,bcd->bnd', q2, kv) / math.sqrt(N)
        attn = v + t2
        return attn @ W_out + b_out

    def _L0_ffn_ref(x, Wr, br, W1, b1, W2, b2, gamma, beta):
        import math
        import jax, jax.numpy as jnp
        import numpy as np
        CAPACITY_FACTOR = 1.25
        TOP_K = 2
        LN_EPS = 1e-05

        def _layer_norm(x, gamma, beta):
            mu = jnp.mean(x, axis=-1, keepdims=True)
            var = jnp.var(x, axis=-1, keepdims=True)
            return (x - mu) * jax.lax.rsqrt(var + LN_EPS) * gamma + beta
        B, S, D = x.shape
        E = Wr.shape[1]
        N = B * S
        K = TOP_K
        logits = jnp.mean(x, axis=1) @ Wr + br
        routing_weights = jax.nn.softmax(logits, axis=-1)
        capacity = float(math.ceil(N * CAPACITY_FACTOR / E))
        expected_loads = routing_weights.sum(axis=0) * (N / B)
        scale = jnp.where(expected_loads > capacity, capacity / expected_loads, 1.0)
        routing_weights = jax.nn.softmax(routing_weights * scale, axis=-1)
        rw_tok = jnp.broadcast_to(routing_weights[:, None, :], (B, S, E)).reshape(N, E)
        top_w, top_i = jax.lax.top_k(rw_tok, K)
        top_w = jax.nn.softmax(top_w, axis=-1)
        xf = x.reshape(N, D)
        h = jax.nn.gelu(jnp.einsum('nd,edf->enf', xf, W1) + b1[:, None, :], approximate=False)
        y = jnp.einsum('enf,efd->end', h, W2) + b2[:, None, :]
        w_dense = jnp.zeros((N, E), x.dtype).at[jnp.arange(N)[:, None], top_i].add(top_w)
        out = jnp.einsum('ne,end->nd', w_dense, y).reshape(B, S, D)
        out = _layer_norm(out + x, gamma, beta)
        return out

    def _L1_gnn_ref(node_feats, src, dst, edge_types, basis, comp, loop_w, h_bias, ln_gamma, ln_beta):
        import jax, jax.numpy as jnp
        import numpy as np
        N_NODES = 1250
        N_EDGES = 40000
        D = 256
        N_RELS = 8
        N_BASES = 4
        LN_EPS = 1e-05
        W = jnp.einsum('rb,bio->rio', comp, basis)
        h_all = jnp.einsum('ni,rio->nro', node_feats, W)
        msgs = h_all[src, edge_types]
        agg = jax.ops.segment_sum(msgs, dst, num_segments=node_feats.shape[0])
        rgcn_out = agg + node_feats @ loop_w + h_bias
        h = jax.nn.gelu(rgcn_out + node_feats, approximate=False)
        mu = jnp.mean(h, axis=-1, keepdims=True)
        var = jnp.mean(jnp.square(h - mu), axis=-1, keepdims=True)
        return (h - mu) * jax.lax.rsqrt(var + LN_EPS) * ln_gamma + ln_beta

    def _L1_mix_ref(x, W_qkv, W_out, b_out):
        import jax, jax.numpy as jnp
        import numpy as np
        HEADS = 4
        DIM_HEAD = 32
        B, L, D = x.shape
        scale = DIM_HEAD ** (-0.5)
        qkv = jnp.einsum('bld,df->blf', x, W_qkv)
        qkv = qkv.reshape(B, L, 3, HEADS, DIM_HEAD)
        q = jnp.transpose(qkv[:, :, 0], (0, 2, 1, 3)) * scale
        k = jax.nn.softmax(jnp.transpose(qkv[:, :, 1], (0, 2, 1, 3)), axis=2)
        v = jnp.transpose(qkv[:, :, 2], (0, 2, 1, 3))
        context = jnp.einsum('bhld,bhle->bhde', k, v)
        out = jnp.einsum('bhde,bhld->bhle', context, q)
        out = jnp.transpose(out, (0, 2, 1, 3)).reshape(B, L, HEADS * DIM_HEAD)
        return jnp.einsum('blf,fd->bld', out, W_out) + b_out

    def _L1_ffn_ref(x, gamma, beta, Wr, br, W1, b1, W2, b2):
        import jax, jax.numpy as jnp
        import numpy as np
        E = 8
        K = 2
        D = 256
        H = 512
        DOUT = 256
        EPS = 1e-05
        mu = jnp.mean(x, axis=-1, keepdims=True)
        var = jnp.mean(jnp.square(x - mu), axis=-1, keepdims=True)
        xn = (x - mu) * jax.lax.rsqrt(var + EPS) * gamma + beta
        logits = jnp.einsum('bsd,de->bse', xn, Wr) + br
        top_vals, top_idx = jax.lax.top_k(logits, K)
        w = jax.nn.softmax(top_vals, axis=-1)
        w_full = jnp.einsum('bsk,bske->bse', w, jax.nn.one_hot(top_idx, E, dtype=w.dtype))
        y = jnp.zeros(x.shape[:-1] + (DOUT,), x.dtype)
        for e in range(E):
            h = jax.nn.gelu(jnp.einsum('bsd,dh->bsh', xn, W1[e]) + b1[e], approximate=False)
            y_e = jnp.einsum('bsh,hd->bsd', h, W2[e]) + b2[e]
            y = y + y_e * w_full[..., e, None]
        return y
    xn = _layernorm(x, axis=-1)
    x = x + _L0_gnn_ref(xn, src, dst, L0_gnn_theta_w, L0_gnn_theta_b, L0_gnn_phi_w, L0_gnn_phi_b) + _L0_mix_ref(xn[None], L0_mix_W_qkv, L0_mix_b_qkv, L0_mix_W_out, L0_mix_b_out)[0]
    x = x + _L0_ffn_ref(_layernorm(x, axis=-1)[None], L0_ffn_Wr, L0_ffn_br, L0_ffn_W1, L0_ffn_b1, L0_ffn_W2, L0_ffn_b2, L0_ffn_gamma, L0_ffn_beta)[0]
    xn = _layernorm(x, axis=-1)
    x = x + _L1_gnn_ref(xn, src, dst, edge_type_8, L1_gnn_basis, L1_gnn_comp, L1_gnn_loop_w, L1_gnn_h_bias, L1_gnn_ln_gamma, L1_gnn_ln_beta) + _L1_mix_ref(xn[None], L1_mix_W_qkv, L1_mix_W_out, L1_mix_b_out)[0]
    x = x + _L1_ffn_ref(_layernorm(x, axis=-1)[None], L1_ffn_gamma, L1_ffn_beta, L1_ffn_Wr, L1_ffn_br, L1_ffn_W1, L1_ffn_b1, L1_ffn_W2, L1_ffn_b2)[0]
    return x

_drawn_inputs = setup_inputs


def setup_inputs(seed=0):
    import zlib

    import numpy as np

    out = dict(_drawn_inputs(seed))
    spreads = {'L0_gnn_theta_b': (0.0, 0.1),
     'L0_gnn_phi_b': (0.0, 0.1),
     'L0_ffn_br': (0.0, 0.1),
     'L0_ffn_b1': (0.0, 0.468),
     'L0_ffn_b2': (0.0, 0.292),
     'L0_ffn_gamma': (1.0, 0.2),
     'L0_ffn_beta': (0.0, 0.1),
     'L1_gnn_h_bias': (0.0, 0.8),
     'L1_gnn_ln_gamma': (1.0, 0.2),
     'L1_gnn_ln_beta': (0.0, 0.276),
     'L1_mix_b_out': (0.0, 0.1),
     'L1_ffn_br': (0.0, 0.656)}
    factors = {'L0_mix_b_out': 4.218,
     'L1_ffn_gamma': 8.0,
     'L1_ffn_beta': 8.0,
     'L1_ffn_Wr': 3.946,
     'L1_ffn_W1': 3.512,
     'L1_ffn_b1': 26.486,
     'L1_ffn_W2': 3.405,
     'L1_ffn_b2': 29.615}
    for name, (base, spread) in spreads.items():
        noise = np.random.default_rng([zlib.crc32(name.encode()), seed]).standard_normal(out[name].shape)
        drawn = base * np.exp(spread * noise) if base else spread * noise
        out[name] = jnp.asarray(drawn.astype(out[name].dtype))
    for name, factor in factors.items():
        out[name] = (out[name] * factor).astype(out[name].dtype)
    return out
```

```python
import concourse.bass as bass
from concourse import mybir
from contextlib import ExitStack

F32 = mybir.dt.float32
I32 = mybir.dt.int32
U32 = mybir.dt.uint32
ALU = mybir.AluOpType
ACT = mybir.ActivationFunctionType
AX = mybir.AxisListType.X

N, D = 3125, 256
NODE_P, NT = 125, 25
GRP = 5
NG = NT // GRP
DK = D // 128
EDGES = 103125
LANES = 128
RING = 16
HB = 4
STEPS = 808
TAIL = STEPS % RING
ROUNDS = STEPS // RING
EMPTY = LANES * STEPS
E8, F = 8, 512
FK = F // 128
BIG = 1e30
LN_EPS = 1e-5
assert NODE_P * NT == N and LANES * STEPS > EDGES and TAIL == RING // 2


class Own:

    def __init__(self, eng, sem):
        self.eng, self.sem, self.done = eng, sem, 0

    def step(self, ins):
        ins.then_inc(self.sem, 1)
        self.done = self.done + 1

    def settle(self):
        self.eng.wait_ge(self.sem, self.done)

    def link(self, ins):
        self.step(ins)
        self.settle()

    def loop(self, i, start, per):
        self.base, self.per = self.done, per
        self.done = (i - start) * per + self.base

    def left(self, turns):
        self.done = self.base + turns * self.per


def free(g, u, slots):
    before = slots if u >= slots else GRP - max(w for w in range(GRP) if w % slots == u) + u
    return g * GRP + u + 1 + GRP - before


class Names:
    pass


def hold(eng, K, sem, value):
    eng.wait_ge(sem, value).then_inc(K.waits_passed, 1)


def norm_stats(nc, K, v, own, act_asks, act_gives):
    S, P = K.S, NODE_P
    own.link(nc.vector.tensor_tensor(K.t1[:P], S[:P, :, 1], S[:P, :, 4], ALU.add))
    own.link(nc.vector.tensor_tensor(K.t2[:P], S[:P, :, 1], S[:P, :, 4], ALU.subtract))
    own.link(nc.vector.tensor_tensor(K.t3[:P], S[:P, :, 2], S[:P, :, 5], ALU.add))
    own.link(nc.vector.tensor_tensor(K.t2[:P], K.t2[:P], K.t2[:P], ALU.mult))
    own.link(nc.vector.tensor_scalar(K.t2[:P], K.t2[:P], 0.25, LN_EPS, ALU.mult, ALU.add))
    nc.vector.scalar_tensor_tensor(K.t3[:P], K.t3[:P], 1.0 / D, K.t2[:P], ALU.mult, ALU.add).then_inc(act_asks, 1)
    v.wait_ge(act_gives, 1)
    own.link(nc.vector.reciprocal(K.rstd[:P], K.std[:P]))
    own.link(nc.vector.scalar_tensor_tensor(K.nmr[:P], K.t1[:P], -0.5, K.rstd[:P], ALU.mult, ALU.mult))


def setup(nc, K, sem):
    loaded_x, loaded_w, loaded_e = sem("loaded_x"), sem("loaded_w"), sem("loaded_e")
    ident_zero, ident_done, consts = sem("ident_zero"), sem("ident_done"), sem("consts")
    stats_asks, stats_gives = sem("stats_asks"), sem("stats_gives")
    xs_ready, xs_free, xt_psum, xt_free, xt_copied = (sem(n) for n in ("xs_ready", "xs_free", "xt_psum", "xt_free", "xt_copied"))
    b_psum, b_free, b_stored = sem("b_psum"), sem("b_free"), sem("b_stored")
    wdiff, edge_diag, edge_rows, lanes_of = sem("wdiff"), sem("edge_diag"), sem("edge_rows"), sem("lanes_of")
    dstf_ready, dstf_stored, cnt_used, cnt_ready, cnt_stored, cnt_back = (
        sem(n) for n in ("dstf_ready", "dstf_stored", "cnt_used", "cnt_ready", "cnt_stored", "cnt_back"))
    seg_ready, row_bias, row_done = sem("seg_ready"), sem("row_bias"), sem("row_done")
    P = NODE_P
    PS, A = K.PS, K.arena
    Ball = A[:P, 0:NT * D].rearrange("p (t d) -> p t d", d=D)
    cmp_ = A[:P, NT * D:NT * D + NT * LANES].rearrange("p (t l) -> p t l", l=LANES)
    dsti = A[:, 2 * NT * D:2 * NT * D + STEPS].bitcast(I32)
    diag = A[:, 2 * NT * D + STEPS:2 * NT * D + STEPS + 256].rearrange("p (a l) -> p a l", a=2)
    dstf = K.keep
    rows = K.G[:, 0:15, :].rearrange("p s d -> p (s d)")[:P, 0:GRP * 768]
    cg = K.arena[:P, 2 * NT * D + STEPS + 256:2 * NT * D + STEPS + 256 + GRP * STEPS].rearrange("p (s k) -> p s k", s=GRP)

    with nc.Block() as block:
        @block.sync
        def _(sp):
            sp.dma_start(dsti, K.in_dst).then_inc(loaded_e, 16)
            sp.dma_start(K.X[:P], K.in_x.rearrange("(p t) d -> p t d", t=NT)).then_inc(loaded_x, 16)
            for dst, src in K.early_loads:
                sp.dma_start(dst, src).then_inc(loaded_w, 16)
            sp.wait_ge(dstf_ready, 1)
            sp.dma_start(K.dstf_dram, dstf[:]).then_inc(dstf_stored, 16)
            for g in range(NG):
                sp.wait_ge(b_free, GRP * (g + 1) + GRP)
                sp.dma_start(K.btab[:, g * GRP:(g + 1) * GRP, :], Ball[:, g * GRP:(g + 1) * GRP, :]).then_inc(b_stored, 16)
            sp.wait_ge(cnt_ready, 1)
            sp.dma_start(K.cnt_dram[1:N + 1].rearrange("(p t) -> p t", t=NT), K.cnt_le[:P]).then_inc(cnt_stored, 16)
            sp.dma_start(K.cnt_dram[0:1].rearrange("(a b) -> a b", a=1), K.zero[0:1, 0:1]).then_inc(cnt_stored, 16)
            sp.wait_ge(cnt_stored, 32)
            sp.dma_start(K.cnt_lt[:P], K.cnt_dram[0:N].rearrange("(p t) -> p t", t=NT)).then_inc(cnt_back, 16)
            sp.wait_ge(b_stored, 16 * NG)

        @block.gpsimd
        def _(pool):
            nc.gpsimd.memset(K.ident[:], 0.0).then_inc(ident_zero, 1)
            pool.wait_ge(ident_zero, 1)
            nc.gpsimd.affine_select(out=K.ident[:], in_=K.ident[:], compare_op=ALU.not_equal, fill=1.0, base=0,
                                    pattern=[[-1, 128]], channel_multiplier=1).then_inc(ident_done, 1)
            nc.gpsimd.iota(K.nodei[:P], pattern=[[1, NT]], base=0, channel_multiplier=NT).then_inc(consts, 1)
            nc.gpsimd.iota(K.parti[:], pattern=[[0, 1]], base=0, channel_multiplier=1).then_inc(consts, 1)
            nc.gpsimd.memset(K.zero[:], 0.0).then_inc(consts, 1)
            nc.gpsimd.memset(K.ones[:], 1.0).then_inc(consts, 1)
            nc.gpsimd.memset(K.eps[:], LN_EPS).then_inc(consts, 1)
            pool.wait_ge(lanes_of, 1)
            pool.wait_ge(dstf_stored, 16)
            for t in range(NT):
                if t >= GRP:
                    pool.wait_ge(cnt_used, t - GRP + 1)
                nc.gpsimd.indirect_dma_start(cg[:, t % GRP, :], None, K.dstf_dram,
                                             bass.IndirectOffsetOnAxis(ap=K.lane_i[:P, t:t + 1], axis=0)
                                             ).then_inc(K.landed[t % GRP], 16)

        @block.scalar
        def _(act):
            act.wait_ge(stats_asks, 1)
            nc.scalar.activation(K.std[:P], K.t3[:P], ACT.Sqrt).then_inc(stats_gives, 1)
            act.sem_inc(xt_free, GRP)
            act.sem_inc(b_free, GRP)
            with act.Fori(0, NG) as g:
                for u in range(GRP):
                    hold(act, K, xt_psum, g * GRP + u + 1)
                    nc.scalar.copy(K.xTs[:, u], K.pT(u)).then_inc(xt_copied, 1)
                    nc.scalar.copy(K.XT[:, :, bass.ds((g * GRP + u) * P, P)], K.pT(u)).then_inc(xt_free, 1)
                for u in range(GRP):
                    hold(act, K, b_psum, g * GRP + u + 1)
                    nc.scalar.copy(Ball[:, bass.ds(g * GRP + u, 1), :], K.pB(u)).then_inc(b_free, 1)

        @block.tensor
        def _(pe):
            pe.wait_ge(ident_done, 1)
            pe.wait_ge(consts, 5)
            pe.wait_ge(edge_diag, 1)
            nc.tensor.matmul(PS[:, 7, 0:256], K.ones[:, 0:128], diag.rearrange("p a l -> p (a l)"),
                             start=True, stop=True).then_inc(edge_rows, 1)
            pe.wait_ge(wdiff, 1)
            with pe.Fori(0, NG) as g:
                for u in range(GRP):
                    pe.wait_ge(xs_ready, g * GRP + u + 1)
                    pe.wait_ge(xt_free, free(g, u, 4))
                    for k in range(DK):
                        last = nc.tensor.transpose(K.pT(u)[:, k, :], K.xs[:P, u, k * 128:(k + 1) * 128], K.ident[:P, :P])
                    last.then_inc(xt_psum, 1)
                for u in range(GRP):
                    pe.wait_ge(xt_copied, g * GRP + u + 1)
                    pe.wait_ge(b_free, free(g, u, 3))
                    for k in range(DK):
                        last = nc.tensor.matmul(K.pB(u), K.xTs[:, u, k, :], K.wB[:, k, :], start=k == 0, stop=k == DK - 1)
                    last.then_inc(b_psum, 1)

        @block.vector
        def _(v):
            own = K.own_v = Own(v, K.dve_own)
            v.wait_ge(loaded_e, 16)
            own.link(nc.vector.tensor_copy(dstf[:], dsti))
            v.sem_inc(dstf_ready, 1)
            v.wait_ge(ident_done, 1)
            own.link(nc.vector.tensor_scalar(diag[:, 0, :], K.ident[:], dstf[:, 0:1], None, ALU.mult))
            nc.vector.tensor_scalar(diag[:, 1, :], K.ident[:], dstf[:, STEPS - 1:STEPS], None, ALU.mult).then_inc(edge_diag, 1)
            v.wait_ge(consts, 5)
            own.link(nc.vector.tensor_copy(K.node[:P], K.nodei[:P]))
            v.wait_ge(edge_rows, 1)
            own.link(nc.vector.tensor_copy(K.edge_rows[:].rearrange("p a l -> p (a l)"), PS[:, 7, 0:256]))
            own.link(nc.vector.tensor_tensor(cmp_, K.edge_rows[:P, 1:2, :].broadcast_to([P, NT, LANES]),
                                             K.node[:P].unsqueeze(2).broadcast_to([P, NT, LANES]), ALU.is_le))
            own.link(nc.vector.tensor_reduce(K.lane[:P], cmp_, AX, ALU.add))
            nc.vector.tensor_copy(K.lane_i[:P], K.lane[:P]).then_inc(lanes_of, 1)
            v.wait_ge(loaded_w, 16 * len(K.early_loads))
            nc.vector.tensor_tensor(K.wB[:], K.wphi[:], K.wtheta[:], ALU.subtract).then_inc(wdiff, 1)
            v.wait_ge(loaded_x, 16)
            with v.Fori(0, NT) as t:
                nc.vector.bn_stats(K.S[:P, bass.ds(t, 1), :], K.X[:P, bass.ds(t, 1), :]).then_inc(K.dve_own, 1)
            own.done += NT
            own.settle()
            norm_stats(nc, K, v, own, stats_asks, stats_gives)
            with v.Fori(0, NG) as g:
                normalise(K, nc, v, g, xt_free, xs_ready)
                for u in range(GRP):
                    hold(v, K, K.landed[u], 16 * g + 16)
                    nc.vector.tensor_scalar(cg[:, u, :], cg[:, u, :], K.node[:P, bass.ds(g * GRP + u, 1)], None,
                                            ALU.is_le, ALU.add,
                                            accum_out=K.inlane[:P, bass.ds(g * GRP + u, 1)]).then_inc(cnt_used, 1)
            v.wait_ge(cnt_used, NT)
            nc.vector.scalar_tensor_tensor(K.cnt_le[:P], K.lane[:P], float(STEPS), K.inlane[:P], ALU.mult, ALU.add).then_inc(cnt_ready, 1)
            own.link(nc.vector.tensor_scalar(K.pen[:], dstf[:], dstf[:, 0:1], None, ALU.is_equal, ALU.add, accum_out=K.goes_on[:, 2:3]))
            own.link(nc.vector.tensor_copy(K.goes_on[:, 3:4], K.parti[:]))
            own.link(nc.vector.scalar_tensor_tensor(K.goes_on[:, 3:4], K.goes_on[:, 3:4], float(STEPS), K.goes_on[:, 2:3], ALU.mult, ALU.add))
            own.link(nc.vector.tensor_scalar(K.first_i[:], K.goes_on[:, 3:4], -1.0, None, ALU.add))
            own.link(nc.vector.tensor_tensor(K.pen[:, 1:STEPS], dstf[:, 1:STEPS], dstf[:, 0:STEPS - 1], ALU.is_equal))
            v.wait_ge(dstf_stored, 16)
            own.link(nc.vector.tensor_copy(K.keep[:, 1:STEPS], K.pen[:, 1:STEPS]))
            own.link(nc.vector.memset(K.keep[:, 0:1], 0.0))
            own.link(nc.vector.tensor_scalar(K.pen[:], K.keep[:], BIG, -BIG, ALU.mult, ALU.add))
            own.link(nc.vector.memset(K.lane_keep[:], 0.0))
            own.link(nc.vector.tensor_tensor(K.lane_keep[:, 1:LANES], K.edge_rows[:, 0, 1:LANES], K.edge_rows[:, 1, 0:LANES - 1], ALU.is_equal))
            own.link(nc.vector.tensor_tensor(K.lane_pen[:], K.lane_keep[:], K.ident[:], ALU.mult))
            own.link(nc.vector.tensor_reduce(K.goes_on[:, 0:1], K.lane_pen[:], AX, ALU.add))
            own.link(nc.vector.tensor_scalar(K.goes_on[:, 1:2], K.goes_on[:, 0:1], BIG, -BIG, ALU.mult, ALU.add))
            own.link(nc.vector.tensor_tensor(K.lane_pen[:], K.edge_rows[:, 0, :], K.edge_rows[:, 1, :], ALU.is_equal))
            own.link(nc.vector.tensor_tensor(K.lane_keep[:], K.lane_keep[:], K.lane_pen[:], ALU.mult))
            own.link(nc.vector.tensor_scalar(K.lane_pen[:], K.lane_keep[:], BIG, -BIG, ALU.mult, ALU.add))
            v.wait_ge(cnt_back, 16)
            t2, t3 = K.t2[:P], K.t3[:P]
            own.link(nc.vector.tensor_tensor(t3, K.cnt_lt[:P], K.cnt_le[:P], ALU.is_equal))
            own.link(nc.vector.tensor_scalar(t2, K.cnt_le[:P], -1.0, float(EMPTY + 1), ALU.mult, ALU.add))
            own.link(nc.vector.tensor_tensor(t2, t2, t3, ALU.mult))
            own.link(nc.vector.scalar_tensor_tensor(t2, K.cnt_le[:P], -1.0, t2, ALU.add, ALU.add))
            own.link(nc.vector.tensor_copy(K.end_i[:P], t2))



class Pass:

    def __init__(self, K, sem, name, table, index, factor, op0, op1, lane_factor, neutral):
        self.table, self.index, self.factor = table, index, factor
        self.op0, self.op1, self.lane_factor, self.neutral = op0, op1, lane_factor, neutral
        self.base = K.landed_total
        self.folded = sem(name + "_folded")
        self.index_staged = [sem(f"{name}_index_staged{h}") for h in range(2)]
        self.written = [sem(f"{name}_written{b}") for b in range(RING // HB)]


def gather_rounds(eng, one):
    one(0, RING, True)
    with eng.Fori(1, ROUNDS) as i:
        one(i, RING, False)
    one(ROUNDS, TAIL, False)


def gather_sync(nc, K, sp, L):
    half = RING // 2

    def stage(i, h):
        sp.dma_start(K.index_sb[:, h * half:(h + 1) * half], L.index[:, bass.ds(i * RING + h * half, half)]
                     ).then_inc(L.index_staged[h], 16)

    def one(i, steps, first):
        for b in range(steps // HB):
            sp.wait_ge(L.folded, i * RING + HB * (b + 1))
            sp.dma_start(K.hist3[:, bass.ds(i * RING + b * HB, HB), :], K.G[:, b * HB:(b + 1) * HB, :]
                         ).then_inc(L.written[b], 16)
            if steps == RING and b % 2 == 1:
                stage(i + 1, b // 2)

    stage(0, 0)
    stage(0, 1)
    gather_rounds(sp, one)


def gather_pool(nc, K, pool, L):
    def one(i, steps, first):
        for s in range(steps):
            if s % (RING // 2) == 0:
                hold(pool, K, L.index_staged[s // (RING // 2)], i * 16 + 16)
            if s % HB == 0 and not first:
                hold(pool, K, L.written[s // HB], i * 16)
                hold(pool, K, L.folded, (i - 1) * RING + s + HB + 1)
            if first and s == RING - 1:
                pool.wait_ge(L.folded, 1)
            nc.gpsimd.indirect_dma_start(K.G[:, s, :], None, L.table,
                                         bass.IndirectOffsetOnAxis(ap=K.index_sb[:, s:s + 1], axis=0)
                                         ).then_inc(K.landed[s], 16)
    gather_rounds(pool, one)


def gather_fold(nc, K, v, L, i, steps, first):
    for s in range(steps):
        hold(v, K, K.landed[s], i * 16 + 16 + L.base[s])
        if not (first and s == 0):
            v.wait_ge(L.folded, i * RING + s)
        nc.vector.scalar_tensor_tensor(K.G[:, s, :], K.G[:, (s - 1) % RING, :], L.factor[:, bass.ds(i * RING + s, 1)],
                                       K.G[:, s, :], L.op0, L.op1).then_inc(L.folded, 1)


CARRY_SEMS = "trail_up scanned trail_back first_landed fixed fix_stored neutral_set neutral_stored".split()
FIX = RING // 2


def carry_tensor(nc, K, pe, L, c):
    pe.wait_ge(L.folded, STEPS)
    for k in range(DK):
        last = nc.tensor.transpose(K.PS[:, 0, k * 128:(k + 1) * 128], K.G[:, TAIL - 1, k * 128:(k + 1) * 128], K.ident[:])
    last.then_inc(c.trail_up, 1)
    pe.wait_ge(c.scanned, DK)
    for k in range(DK):
        last = nc.tensor.transpose(K.PS[:, 1, k * 128:(k + 1) * 128], K.trail[:, k, 0:LANES], K.ident[:])
    last.then_inc(c.trail_back, 1)


def carry_vector(nc, K, v, own, L, c):
    own.link(nc.vector.memset(K.neutral[:], L.neutral))
    v.sem_inc(c.neutral_set, 1)
    own.link(nc.vector.memset(K.trail[:, :, 0:1], 0.0))
    v.wait_ge(c.trail_up, 1)
    for k in range(DK):
        nc.vector.tensor_tensor_scan(K.trail[:, k, 1:1 + LANES], L.lane_factor[:], K.PS[:, 0, k * 128:(k + 1) * 128], 0.0,
                                     L.op0, L.op1).then_inc(c.scanned, 1)
    v.wait_ge(c.trail_back, 1)
    own.link(nc.vector.tensor_scalar(K.junk[:], K.PS[:, 1, 0:D], K.goes_on[:, 0:1],
                                     K.goes_on[:, 1:2] if L.neutral else 0.0, ALU.mult, ALU.add))
    v.wait_ge(c.first_landed, 1)
    nc.vector.tensor_tensor(K.G[:, FIX, :], K.G[:, FIX, :], K.junk[:], L.op1).then_inc(c.fixed, 1)


def carry_pool(nc, K, pool, L, c):
    for b in range(RING // HB):
        pool.wait_ge(L.written[b], 16 * (ROUNDS + (b < TAIL // HB)))
    pool.wait_ge(L.folded, STEPS)
    index = bass.IndirectOffsetOnAxis(ap=K.first_i[:, 0:1], axis=0)
    nc.gpsimd.indirect_dma_start(K.G[:, FIX, :], None, K.hist, index).then_inc(K.landed[FIX], 16)
    pool.wait_ge(K.landed[FIX], L.base[FIX] + 16 * (ROUNDS + 1))
    pool.sem_inc(c.first_landed, 1)
    pool.wait_ge(c.fixed, 1)
    nc.gpsimd.indirect_dma_start(K.hist, index, K.G[:, FIX, :], None).then_inc(K.landed[FIX], 16)
    pool.wait_ge(K.landed[FIX], L.base[FIX] + 16 * (ROUNDS + 2))


def carry_sync(nc, K, sp, L, c):
    sp.wait_ge(c.neutral_set, 1)
    sp.dma_start(K.hist[EMPTY:EMPTY + 1, :], K.neutral[0:1, :]).then_inc(c.neutral_stored, 16)
    sp.wait_ge(c.neutral_stored, 16)
    for h in range(2):
        sp.wait_ge(L.index_staged[h], 16 * (ROUNDS + 1))


def carry_names(sem, prefix):
    c = Names()
    (c.trail_up, c.scanned, c.trail_back, c.first_landed, c.fixed, c.fix_stored, c.neutral_set, c.neutral_stored) = (
        sem(prefix + n) for n in CARRY_SEMS)
    return c


def gather0_mix0(nc, K, sem):
    L = K.pass0 = Pass(K, sem, "max", K.btab2, K.in_src, K.pen, ALU.add, ALU.max, K.lane_pen, -BIG)
    names = """loaded_m centred x_staged qk_psum qk_free q2_ready q2T_psum q2T_free stats_done roots asks r_ready
               v_psum v_free vk_ready kv_done kv_copied norm_root kvw_psum kvw_ready acc_free""".split()
    (loaded_m, centred, x_staged, qk_psum, qk_free, q2_ready, q2T_psum, q2T_free, stats_done, roots, asks, r_ready,
     v_psum, v_free, vk_ready, kv_done, kv_copied, norm_root, kvw_psum, kvw_ready, acc_free) = (
        sem("m0_" + n) for n in names)
    c = carry_names(sem, "c0_")
    P, PS, A = NODE_P, K.PS, K.arena
    K2 = A[:P, 0:NT * D].rearrange("p (t d) -> p t d", d=D)
    at = NT * D
    Q2T = K.Q2T = A[:, at:at + DK * N].rearrange("p (k n) -> p k n", k=DK)
    at += DK * N

    def piece(n):
        nonlocal at
        at += n
        return A[:, at - n:at]
    wqk = piece(DK * 512).rearrange("p (k n) -> p k n", k=DK)
    wv, wvT, wout = (piece(DK * D).rearrange("p (k n) -> p k n", k=DK) for _ in range(3))
    K.KVW = KVW = piece(DK * D).rearrange("p (k n) -> p k n", k=DK)
    K.wE = wE = piece(DK * 512).rearrange("p (k n) -> p k n", k=DK)
    kvT = piece(DK * D).rearrange("p (k n) -> p k n", k=DK)
    K.trail = piece(DK * (1 + LANES)).rearrange("p (k n) -> p k n", k=DK)
    K.rowE = piece(512)[0:1, :]
    rowqkv = piece(768)[0:1, :]
    rowb = piece(512)[0:1, :]
    rowo = piece(256)[0:1, :]
    bvT = piece(2)
    assert at <= 19968
    wk = lambda name: K.ins[name].rearrange("(k p) n -> p k n", p=128)
    loads = [(wqk, wk("mix0_qk")), (wv, wk("mix0_v")), (wvT, wk("mix0_vT")), (wout, wk("mix0_out")),
             (rowqkv, K.ins["mix0_b"]), (rowb[:, 0:256], K.ins["theta_b"]), (rowb[:, 256:512], K.ins["phi_b"]),
             (rowo, K.ins["mix0_bout"]), (bvT, K.ins["mix0_bvT"])]

    with nc.Block() as block:
        @block.sync
        def _(sp):
            for dst, src in loads:
                sp.dma_start(dst, src).then_inc(loaded_m, 16)
            gather_sync(nc, K, sp, L)
            carry_sync(nc, K, sp, L, c)

        @block.gpsimd
        def _(pool):
            gather_pool(nc, K, pool, L)
            carry_pool(nc, K, pool, L, c)

        @block.scalar
        def _(act):
            act.sem_inc(qk_free, GRP)
            act.sem_inc(q2T_free, GRP)
            act.sem_inc(v_free, GRP)
            with act.Fori(0, NG) as g:
                for u in range(GRP):
                    nc.scalar.copy(K.xTs[:, u], K.XT[:, :, bass.ds((g * GRP + u) * P, P)]).then_inc(x_staged, 1)
                for u in range(GRP):
                    t = g * GRP + u
                    hold(act, K, qk_psum, t + 1)
                    nc.scalar.activation(K.xs[:P, u], PS[:P, u, 0:D], ACT.Square,
                                         accum_out=K.q2sum[:P, bass.ds(t, 1)]).then_inc(q2_ready, 1)
                    nc.scalar.activation(K2[:, bass.ds(t, 1), :], PS[:P, u:u + 1, D:2 * D], ACT.Square,
                                         accum_out=K.k2sum[:P, bass.ds(t, 1)]).then_inc(qk_free, 1)
                    hold(act, K, q2_ready, t + 1)
                    nc.scalar.activation(K.junk[:P], K.xs[:P, u], ACT.Square,
                                         accum_out=K.q4sum[:P, bass.ds(t, 1)]).then_inc(stats_done, 1)
                for u in range(GRP):
                    t = g * GRP + u
                    hold(act, K, q2T_psum, t + 1)
                    nc.scalar.copy(Q2T[:, :, bass.ds(t * P, P)],
                                   PS[:, 5 + u % 3, 0:DK * P].rearrange("p (k n) -> p k n", k=DK)).then_inc(q2T_free, 1)
            act.wait_ge(stats_done, NT)
            nc.scalar.activation(K.std[:P], K.q4sum[:P], ACT.Sqrt).then_inc(roots, 1)
            act.wait_ge(r_ready, 1)
            with act.Fori(0, NG) as g:
                for u in range(GRP):
                    nc.scalar.copy(K.xTs[:, u], K.XT[:, :, bass.ds((g * GRP + u) * P, P)]).then_inc(x_staged, 1)
                for u in range(GRP):
                    t = g * GRP + u
                    hold(act, K, v_psum, t + 1)
                    hold(act, K, acc_free, t + 1)
                    nc.scalar.activation(K.xs[:P, u], PS[:P, u % 3, 0:D], ACT.Copy,
                                         scale=K.kscale[:P, bass.ds(t, 1)]).then_inc(v_free, 1)
                    nc.scalar.activation(K.ys[:P, u], K2[:, bass.ds(t, 1), :].rearrange("p a d -> p (a d)"), ACT.Square,
                                         scale=K.kscale[:P, bass.ds(t, 1)]).then_inc(vk_ready, 1)
            act.wait_ge(kv_copied, 2)
            nc.scalar.activation(K.nrm[:, 2:4], K.nrm[:, 0:2], ACT.Sqrt).then_inc(norm_root, 1)

        @block.tensor
        def _(pe):
            pe.wait_ge(centred, 1)
            with pe.Fori(0, NG) as g:
                for u in range(GRP):
                    t = g * GRP + u
                    pe.wait_ge(x_staged, t + 1)
                    pe.wait_ge(qk_free, t + 1)
                    for k in range(DK):
                        nc.tensor.matmul(PS[:P, u, :], K.xTs[:, u, k, :], wqk[:, k, :], start=k == 0, stop=False)
                    nc.tensor.matmul(PS[:P, u, :], K.ones[0:1, 0:P], rowqkv[:, 0:512], start=False, stop=True).then_inc(qk_psum, 1)
                for u in range(GRP):
                    t = g * GRP + u
                    pe.wait_ge(q2_ready, t + 1)
                    pe.wait_ge(q2T_free, free(g, u, 3))
                    for k in range(DK):
                        last = nc.tensor.transpose(PS[:, 5 + u % 3, k * P:(k + 1) * P], K.xs[:P, u, k * 128:(k + 1) * 128], K.ident[:P, :P])
                    last.then_inc(q2T_psum, 1)
            pe.wait_ge(q2T_free, NT + GRP)
            pe.sem_inc(acc_free, GRP)
            for bank in (5, 6):
                nc.tensor.matmul(PS[:, bank, :], K.zeros[:], wqk[:, 0, :], start=True, stop=False)
            with pe.Fori(0, NG) as g:
                for u in range(GRP):
                    t = g * GRP + u
                    pe.wait_ge(x_staged, t + 1 + NT)
                    pe.wait_ge(v_free, free(g, u, 3))
                    for k in range(DK):
                        nc.tensor.matmul(PS[:P, u % 3, 0:D], K.xTs[:, u, k, :], wv[:, k, :], start=k == 0, stop=False)
                    nc.tensor.matmul(PS[:P, u % 3, 0:D], K.ones[0:1, 0:P], rowqkv[:, 512:768], start=False, stop=True).then_inc(v_psum, 1)
                for u in range(GRP):
                    t = g * GRP + u
                    pe.wait_ge(vk_ready, t + 1)
                    for k in range(DK):
                        nc.tensor.matmul(PS[:, 5, k * D:(k + 1) * D], K.xs[:P, u, k * 128:(k + 1) * 128],
                                         K2[:, bass.ds(t, 1), :].rearrange("p a d -> p (a d)"), start=False, stop=False)
                        last = nc.tensor.matmul(PS[:, 6, k:k + 1], K.ys[:P, u, k * 128:(k + 1) * 128], K.ones[:P, 0:1],
                                                start=False, stop=False)
                    last.then_inc(acc_free, 1)
            for bank in (5, 6):
                last = nc.tensor.matmul(PS[:, bank, :], K.zeros[:], wqk[:, 0, :], start=False, stop=True)
            last.then_inc(kv_done, 1)
            for k in range(DK):
                for d in range(DK):
                    nc.tensor.matmul(PS[:, 3, k * D:(k + 1) * D], wvT[:, d, k * 128:(k + 1) * 128], wout[:, d, :], start=d == 0, stop=d == DK - 1)
            for d in range(DK):
                nc.tensor.matmul(PS[0:1, 4, 0:D], bvT[:, d:d + 1], wout[:, d, :], start=d == 0, stop=d == DK - 1)
            pe.wait_ge(kv_copied, 2)
            pe.wait_ge(v_free, NT + GRP)
            for k in range(DK):
                for d in range(DK):
                    last = nc.tensor.matmul(PS[:, 7, k * D:(k + 1) * D], kvT[:, d, k * 128:(k + 1) * 128], wout[:, d, :], start=d == 0, stop=d == DK - 1)
            last.then_inc(kvw_psum, 1)
            carry_tensor(nc, K, pe, L, c)

        @block.vector
        def _(v):
            own = K.own_v
            own.eng = v
            own.link(nc.vector.memset(K.zeros[:], 0.0))
            own.link(nc.vector.memset(K.G[:, RING - 1, :], 0.0))
            v.wait_ge(loaded_m, 16 * len(loads))
            for which in range(2):
                for w, n, p in [(wqk[:, k, which * D:(which + 1) * D], k, 128) for k in range(DK)] + [(rowqkv[:, which * D:(which + 1) * D], 2, 1)]:
                    own.link(nc.vector.tensor_reduce(K.nrm[:p, 4:5], w, AX, ALU.add))
                    own.link(nc.vector.tensor_scalar(K.nrm[:p, 5:6], K.nrm[:p, 4:5], -1.0 / D, None, ALU.mult))
                    own.link(nc.vector.tensor_scalar(w, w, K.nrm[:p, 5:6], None, ALU.add))
            v.sem_inc(centred, 1)
            gather_fold(nc, K, v, L, 0, RING, True)
            with v.Fori(1, 12) as i:
                gather_fold(nc, K, v, L, i, RING, False)
            v.wait_ge(roots, 1)
            own.link(nc.vector.tensor_scalar(K.kscale[:P], K.k2sum[:P], 1e-7, None, ALU.add))
            nc.vector.reciprocal(K.kscale[:P], K.kscale[:P]).then_inc(r_ready, 1)
            own.link(nc.vector.tensor_scalar(K.q2sum[:P], K.q2sum[:P], 1e-7, None, ALU.add))
            own.link(nc.vector.reciprocal(K.q2sum[:P], K.q2sum[:P]))
            own.link(nc.vector.tensor_tensor(K.t1[:P], K.std[:P], K.q2sum[:P], ALU.mult))
            own.link(nc.vector.tensor_scalar(K.t1[:P], K.t1[:P], 1e-12, None, ALU.max))
            own.link(nc.vector.reciprocal(K.t1[:P], K.t1[:P]))
            own.link(nc.vector.scalar_tensor_tensor(K.qscale[:P], K.q2sum[:P], N ** -0.5, K.t1[:P], ALU.mult, ALU.mult))
            with v.Fori(12, 36) as i:
                gather_fold(nc, K, v, L, i, RING, False)
            v.wait_ge(kv_done, 1)
            nc.vector.tensor_copy(kvT.rearrange("p k n -> p (k n)"), PS[:, 5, :]).then_inc(kv_copied, 1)
            nc.vector.tensor_copy(K.nrm[:, 0:2], PS[:, 6, 0:2]).then_inc(kv_copied, 1)
            v.wait_ge(norm_root, 1)
            own.link(nc.vector.tensor_scalar(K.nrm[:, 2:4], K.nrm[:, 2:4], 1e-12, None, ALU.max))
            own.link(nc.vector.reciprocal(K.nrm[:, 2:4], K.nrm[:, 2:4]))
            v.wait_ge(kvw_psum, 1)
            for k in range(DK):
                own.link(nc.vector.tensor_scalar(KVW[:, k, :], PS[:, 7, k * D:(k + 1) * D], K.nrm[:, 2 + k:3 + k], None, ALU.mult))
                own.link(nc.vector.tensor_copy(wE[:, k, 0:D], K.wtheta[:, k, :]))
                own.link(nc.vector.tensor_copy(wE[:, k, D:2 * D], PS[:, 3, k * D:(k + 1) * D]))
            own.link(nc.vector.tensor_tensor(K.rowE[:, 0:D], rowb[:, 0:D], rowb[:, D:2 * D], ALU.add))
            own.link(nc.vector.tensor_tensor(K.rowE[:, D:2 * D], PS[0:1, 4, 0:D], rowo, ALU.add))
            with v.Fori(36, ROUNDS) as i:
                gather_fold(nc, K, v, L, i, RING, False)
            gather_fold(nc, K, v, L, ROUNDS, TAIL, False)
            carry_vector(nc, K, v, own, L, c)
    for s in range(RING):
        K.landed_total[s] += 16 * (ROUNDS + (s < TAIL) + 2 * (s == FIX))


def gather_ends(nc, K, pool, L, m_used):
    for t in range(NT):
        u = t % GRP
        if t >= GRP:
            pool.wait_ge(m_used, t - GRP + 1)
        nc.gpsimd.indirect_dma_start(K.G[:NODE_P, u, :], None, K.hist,
                                     bass.IndirectOffsetOnAxis(ap=K.end_i[:NODE_P, t:t + 1], axis=0)
                                     ).then_inc(K.landed[u], 16)


def ends_taken(K):
    for s in range(GRP):
        K.landed_total[s] += 16 * NG


def tile_of(buf, t):
    return buf[:, bass.ds(t, 1), :].rearrange("p a d -> p (a d)")


def col(buf, t):
    return buf[:NODE_P, bass.ds(t, 1)]


def ends0(nc, K, sem):
    names = "x_staged q_staged ae_psum ae_free p1_psum p1_free m_used".split()
    x_staged, q_staged, ae_psum, ae_free, p1_psum, p1_free, m_used = (sem("e0_" + n) for n in names)
    P, PS, G = NODE_P, K.PS, K.G
    base = list(K.landed_total)
    X = K.X[:P]
    with nc.Block() as block:
        @block.gpsimd
        def _(pool):
            gather_ends(nc, K, pool, K.pass0, m_used)

        @block.scalar
        def _(act):
            with act.Fori(0, NG) as g:
                for u in range(GRP):
                    hold(act, K, ae_free, g * GRP + u + 1)
                    hold(act, K, p1_free, g * GRP + u + 1)
                    cols = bass.ds((g * GRP + u) * P, P)
                    nc.scalar.copy(K.xTs[:, u], K.XT[:, :, cols]).then_inc(x_staged, 1)
                    nc.scalar.copy(K.ys[:, u, 0:DK * P].rearrange("p (k n) -> p k n", k=DK), K.Q2T[:, :, cols]).then_inc(q_staged, 1)

        @block.tensor
        def _(pe):
            with pe.Fori(0, NG) as g:
                for u in range(GRP):
                    t = g * GRP + u
                    pe.wait_ge(x_staged, t + 1)
                    pe.wait_ge(ae_free, t + 1)
                    for k in range(DK):
                        nc.tensor.matmul(PS[:P, u, :], K.xTs[:, u, k, :], K.wE[:, k, :], start=k == 0, stop=False)
                    nc.tensor.matmul(PS[:P, u, :], K.ones[0:1, 0:P], K.rowE, start=False, stop=True).then_inc(ae_psum, 1)
                for u in range(GRP):
                    pe.wait_ge(q_staged, g * GRP + u + 1)
                    pe.wait_ge(p1_free, free(g, u, 3))
                    for k in range(DK):
                        last = nc.tensor.matmul(PS[:P, 5 + u % 3, 0:D], K.ys[:, u, k * P:(k + 1) * P], K.KVW[:, k, :],
                                                start=k == 0, stop=k == DK - 1)
                    last.then_inc(p1_psum, 1)

        @block.vector
        def _(v):
            own = K.own_v
            own.eng = v
            v.sem_inc(ae_free, GRP)
            v.sem_inc(p1_free, GRP)
            with v.Fori(0, NG) as g:
                own.loop(g, 0, 2 * GRP)
                mark = [0] * GRP
                for u in range(GRP):
                    v.wait_ge(K.landed[u], g * 16 + 16 + base[u])
                    v.wait_ge(ae_psum, g * GRP + u + 1)
                    nc.vector.tensor_tensor(K.xs[:P, u], G[:P, u, :], PS[:P, u, 0:D], ALU.add).then_inc(m_used, 1)
                for u in range(GRP):
                    v.wait_ge(m_used, g * GRP + u + 1)
                    own.step(nc.vector.scalar_tensor_tensor(tile_of(X, g * GRP + u), K.xs[:P, u], 0.0, tile_of(X, g * GRP + u),
                                                            ALU.max, ALU.add))
                    mark[u] = own.done
                for u in range(GRP):
                    v.wait_ge(own.sem, mark[u])
                    nc.vector.tensor_tensor(tile_of(X, g * GRP + u), tile_of(X, g * GRP + u), PS[:P, u, D:2 * D], ALU.add).then_inc(ae_free, 1)
                for u in range(GRP):
                    t = g * GRP + u
                    v.wait_ge(p1_psum, t + 1)
                    v.wait_ge(ae_free, t + 1 + GRP)
                    nc.vector.scalar_tensor_tensor(tile_of(X, t), PS[:P, 5 + u % 3, 0:D], col(K.qscale, t), tile_of(X, t),
                                                   ALU.mult, ALU.add).then_inc(p1_free, 1)
                for u in range(GRP):
                    t = g * GRP + u
                    hold(v, K, p1_free, t + 1 + GRP)
                    own.step(nc.vector.bn_stats(K.S[:P, bass.ds(t, 1), :], tile_of(X, t)))
            own.left(NG)
            own.settle()
    ends_taken(K)


def transposes(K, nc, pe, g, ready, xt_psum, xt_free, ring):
    for u in range(GRP):
        pe.wait_ge(ready, g * GRP + u + 1)
        pe.wait_ge(xt_free, free(g, u, ring))
        for k in range(DK):
            last = nc.tensor.transpose(K.PS[:, u % ring, k * NODE_P:(k + 1) * NODE_P], K.xs[:NODE_P, u, k * 128:(k + 1) * 128],
                                       K.ident[:NODE_P, :NODE_P])
        last.then_inc(xt_psum, 1)


def normalise(K, nc, v, g, xt_free, xs_ready):
    for u in range(GRP):
        t = g * GRP + u
        hold(v, K, xt_free, t + 1)
        nc.vector.tensor_scalar(K.xs[:NODE_P, u], tile_of(K.X[:NODE_P], t), col(K.rstd, t), col(K.nmr, t),
                                ALU.mult, ALU.add).then_inc(xs_ready, 1)


def add_normed(nc, K, v, own, a, gamma, beta):
    P, X = NODE_P, K.X[:NODE_P]
    with v.Fori(0, NG) as g:
        own.loop(g, 0, 5 * GRP)
        mark = [0] * GRP

        def all_tiles(first, emit):
            for u in range(GRP):
                if not first:
                    hold(v, K, own.sem, mark[u])
                own.step(emit(g * GRP + u))
                mark[u] = own.done
        all_tiles(True, lambda t: nc.vector.tensor_scalar(tile_of(a, t), tile_of(a, t), col(K.rstd, t), col(K.nmr, t), ALU.mult, ALU.add))
        all_tiles(False, lambda t: nc.vector.tensor_tensor(tile_of(a, t), tile_of(a, t), gamma, ALU.mult))
        all_tiles(False, lambda t: nc.vector.tensor_tensor(tile_of(a, t), tile_of(a, t), beta, ALU.add))
        all_tiles(False, lambda t: nc.vector.tensor_tensor(tile_of(X, t), tile_of(X, t), tile_of(a, t), ALU.add))
        all_tiles(False, lambda t: nc.vector.bn_stats(K.S[:P, bass.ds(t, 1), :], tile_of(X, t)))
    own.left(NG)
    own.settle()


def experts0(nc, K, sem):
    names = """loaded asks gives xs_ready xt_psum xt_free means_done mean_ready rows_psum logits_psum exp_asks exp_gives
               index_ready weights_ready h_psum h_ready y_psum y_free asks2 gives2""".split()
    (loaded, asks, gives, xs_ready, xt_psum, xt_free, means_done, mean_ready, rows_psum, logits_psum, exp_asks, exp_gives,
     index_ready, weights_ready, h_psum, h_ready, y_psum, y_free, asks2, gives2) = (sem("f0_" + n) for n in names)
    P, PS, A, XT = NODE_P, K.PS, K.arena, K.XT
    at = 0

    def piece(n):
        nonlocal at
        at += n
        return A[:, at - n:at]
    a = piece(NT * D)[:P].rearrange("p (t d) -> p t d", d=D)
    W1 = [piece(DK * F).rearrange("p (k f) -> p k f", k=DK) for _ in range(2)]
    W2 = [piece(FK * D).rearrange("p (f d) -> p f d", f=FK) for _ in range(2)]
    b1 = [piece(FK) for _ in range(2)]
    b2 = [piece(D)[:P] for _ in range(2)]
    HR = 5
    hs = [piece(FK * P).rearrange("p (f n) -> p f n", f=FK) for _ in range(HR)]
    gb = piece(2 * D)
    row = piece(2 * D)[0:1, :]
    wr = piece(DK * E8).rearrange("p (k e) -> p k e", k=DK)
    br = piece(E8)[0:1, :]
    spread = piece(DK * 128).rearrange("p (k n) -> p k n", k=DK)
    means = piece(DK * NT).rearrange("p (k t) -> p k t", k=DK)
    mean = piece(DK)
    lg, ex, top = piece(E8), piece(E8), piece(E8)
    m1, m2, m3 = piece(1), piece(1), piece(1)
    wts = piece(2)
    topi = piece(E8).bitcast(U32)
    ef, ix = piece(2), piece(2)
    rowi, expi = piece(2).bitcast(I32), piece(2).bitcast(I32)
    partf = piece(1)
    assert at <= 19968
    ins = K.ins
    loads = [(row[:, 0:D], ins["gamma0"]), (row[:, D:2 * D], ins["beta0"]), (wr, ins["ffn0_Wr"].rearrange("(k p) e -> p k e", p=128)),
             (br, ins["ffn0_br"])]
    base = list(K.landed_total)
    CAP = -(-N * 5 // (4 * E8))
    with nc.Block() as block:
        @block.sync
        def _(sp):
            for dst, src in loads:
                sp.dma_start(dst, src).then_inc(loaded, 16)

        @block.gpsimd
        def _(pool):
            pool.wait_ge(index_ready, 1)
            s = 0
            for e in range(2):
                for dst, table, index, parts in ((W1[e].rearrange("p k f -> p (k f)"), ins["ffn0_W1"], rowi, 128),
                                                 (W2[e].rearrange("p f d -> p (f d)"), ins["ffn0_W2"], rowi, 128),
                                                 (b1[e], ins["ffn0_b1"], rowi, 128), (b2[e], ins["ffn0_b2"], expi, P)):
                    nc.gpsimd.indirect_dma_start(dst, None, table, bass.IndirectOffsetOnAxis(ap=index[:parts, e:e + 1], axis=0)
                                                 ).then_inc(K.landed[s], 16)
                    s += 1

        @block.scalar
        def _(act):
            act.wait_ge(asks, 1)
            nc.scalar.activation(K.std[:P], K.t3[:P], ACT.Sqrt).then_inc(gives, 1)
            act.sem_inc(xt_free, GRP)
            with act.Fori(0, NG) as g:
                for u in range(GRP):
                    t = g * GRP + u
                    hold(act, K, xt_psum, t + 1)
                    for k in range(DK):
                        last = nc.scalar.activation(XT[:, k, bass.ds(t * P, P)], PS[:, u % 4, k * P:(k + 1) * P], ACT.Copy,
                                                    accum_out=means[:, k, bass.ds(t, 1)])
                    last.then_inc(xt_free, 1)
            for n in range(3):
                act.wait_ge(exp_asks, n + 1)
                src, dst = ((lg, ex), (lg, ex), (m2, m3))[n]
                nc.scalar.activation(dst, src, ACT.Exp).then_inc(exp_gives, 1)
            act.wait_ge(weights_ready, 1)
            with act.Fori(0, NG) as g:
                for u in range(GRP):
                    for e in range(2):
                        j = 2 * u + e
                        act.wait_ge(h_psum, g * (2 * GRP) + j + 1)
                        act.wait_ge(y_free, g * GRP + u + GRP - 1)
                        for f in range(FK):
                            last = nc.scalar.activation(hs[j % HR][:, f, :], PS[:, j % HR, f * P:(f + 1) * P], ACT.Gelu,
                                                        bias=b1[e][:, f:f + 1])
                        last.then_inc(h_ready, 1)
            act.wait_ge(asks2, 1)
            nc.scalar.activation(K.std[:P], K.t3[:P], ACT.Sqrt).then_inc(gives2, 1)

        @block.tensor
        def _(pe):
            pe.wait_ge(loaded, 16 * len(loads))
            nc.tensor.matmul(PS[:, 7, :], K.ones[0:1, :], row, start=True, stop=True).then_inc(rows_psum, 1)
            with pe.Fori(0, NG) as g:
                transposes(K, nc, pe, g, xs_ready, xt_psum, xt_free, 4)
            pe.wait_ge(mean_ready, 1)
            for k in range(DK):
                nc.tensor.matmul(PS[:, 6, 0:E8], spread[:, k, :], wr[:, k, :], start=k == 0, stop=False)
            nc.tensor.matmul(PS[:, 6, 0:E8], K.ones[0:1, :], br, start=False, stop=True).then_inc(logits_psum, 1)
            pe.wait_ge(weights_ready, 1)

            def hidden(g, u):
                for e in range(2):
                    j = 2 * u + e
                    pe.wait_ge(h_ready, g * (2 * GRP) + j + 1)
                    for f in range(FK):
                        for k in range(DK):
                            last = nc.tensor.matmul(PS[:, j % HR, f * P:(f + 1) * P], W1[e][:, k, f * 128:(f + 1) * 128],
                                                    XT[:, k, bass.ds((g * GRP + u) * P, P)], start=k == 0, stop=k == DK - 1)
                    last.then_inc(h_psum, 1)

            def output(g, u):
                pe.wait_ge(h_ready, g * (2 * GRP) + 2 * u + 2 + HR)
                pe.wait_ge(y_free, free(g, u, 3))
                for e in range(2):
                    for f in range(FK):
                        last = nc.tensor.matmul(PS[:P, 5 + u % 3, 0:D], hs[(2 * u + e) % HR][:, f, :], W2[e][:, f, :],
                                                start=e == 0 and f == 0, stop=e == 1 and f == FK - 1)
                last.then_inc(y_psum, 1)
            pe.sem_inc(h_ready, HR)
            with pe.Fori(0, NG) as g:
                for u in range(GRP):
                    hidden(g, u)
                    if u:
                        output(g, u - 1)
                output(g, GRP - 1)

        @block.vector
        def _(v):
            own = K.own_v
            own.eng = v
            link = own.link
            norm_stats(nc, K, v, own, asks, gives)
            v.wait_ge(rows_psum, 1)
            link(nc.vector.tensor_copy(gb, PS[:, 7, :]))
            link(nc.vector.tensor_copy(partf, K.parti[:]))
            with v.Fori(0, NG) as g:
                normalise(K, nc, v, g, xt_free, xs_ready)
            v.wait_ge(xt_free, NT + GRP)
            link(nc.vector.tensor_reduce(mean, means, AX, ALU.add))
            link(nc.vector.tensor_scalar(mean, mean, 1.0 / N, None, ALU.mult))
            for k in range(DK):
                link(nc.vector.tensor_scalar(spread[:, k, :], K.ones[:], mean[:, k:k + 1], None, ALU.mult))
            v.sem_inc(mean_ready, 1)
            v.wait_ge(logits_psum, 1)

            def softmax(n, src):
                link(nc.vector.tensor_reduce(m1, src, AX, ALU.max))
                link(nc.vector.tensor_scalar(lg, src, m1, None, ALU.subtract))
                v.sem_inc(exp_asks, 1)
                v.wait_ge(exp_gives, n)
                link(nc.vector.tensor_reduce(m1, ex, AX, ALU.add))
                link(nc.vector.reciprocal(m1, m1))
                link(nc.vector.tensor_scalar(ex, ex, m1, None, ALU.mult))
            softmax(1, PS[:, 6, 0:E8])
            link(nc.vector.tensor_scalar(top, ex, float(N), None, ALU.mult))
            link(nc.vector.reciprocal(top, top))
            link(nc.vector.tensor_scalar(top, top, float(CAP), 1.0, ALU.mult, ALU.min))
            link(nc.vector.tensor_tensor(lg, ex, top, ALU.mult))
            softmax(2, lg)
            link(nc.vector.max(top, ex))
            link(nc.vector.max_index(topi, top, ex))
            link(nc.vector.tensor_copy(ef, topi[:, 0:2]))
            link(nc.vector.tensor_copy(expi, ef))
            link(nc.vector.tensor_scalar(ix, ef, 128.0, partf, ALU.mult, ALU.add))
            link(nc.vector.tensor_copy(rowi, ix))
            v.sem_inc(index_ready, 1)
            link(nc.vector.tensor_tensor(m2, top[:, 1:2], top[:, 0:1], ALU.subtract))
            v.sem_inc(exp_asks, 1)
            v.wait_ge(exp_gives, 3)
            link(nc.vector.tensor_scalar(m1, m3, 1.0, None, ALU.add))
            link(nc.vector.reciprocal(wts[:, 0:1], m1))
            link(nc.vector.tensor_tensor(wts[:, 1:2], wts[:, 0:1], m3, ALU.mult))
            for s in range(8):
                v.wait_ge(K.landed[s], base[s] + 16)
            for e in range(2):
                link(nc.vector.tensor_scalar(W2[e], W2[e], wts[:, e:e + 1], None, ALU.mult))
                link(nc.vector.tensor_scalar(b2[e], b2[e], wts[:P, e:e + 1], None, ALU.mult))
            link(nc.vector.tensor_tensor(b2[0], b2[0], b2[1], ALU.add))
            v.sem_inc(weights_ready, 1)
            v.sem_inc(y_free, GRP)
            with v.Fori(0, NG) as g:
                own.loop(g, 0, 3 * GRP)
                mark = [0] * GRP
                for u in range(GRP):
                    t = g * GRP + u
                    own.step(nc.vector.tensor_scalar(tile_of(a, t), tile_of(K.X[:P], t), col(K.rstd, t), col(K.nmr, t), ALU.mult, ALU.add))
                    mark[u] = own.done
                for u in range(GRP):
                    t = g * GRP + u
                    v.wait_ge(own.sem, mark[u])
                    own.step(nc.vector.tensor_tensor(tile_of(a, t), tile_of(a, t), b2[0], ALU.add))
                    mark[u] = own.done
                for u in range(GRP):
                    t = g * GRP + u
                    v.wait_ge(y_psum, t + 1)
                    v.wait_ge(own.sem, mark[u])
                    nc.vector.tensor_tensor(tile_of(a, t), tile_of(a, t), PS[:P, 5 + u % 3, 0:D], ALU.add).then_inc(y_free, 1)
                for u in range(GRP):
                    t = g * GRP + u
                    hold(v, K, y_free, t + 1 + GRP)
                    own.step(nc.vector.bn_stats(K.S[:P, bass.ds(t, 1), :], tile_of(a, t)))
            own.left(NG)
            own.settle()
            norm_stats(nc, K, v, own, asks2, gives2)
            add_normed(nc, K, v, own, a, gb[:P, 0:D], gb[:P, D:2 * D])
    for s in range(8):
        K.landed_total[s] += 16


def relations(nc, K, sem):
    names = """loaded asks gives xs_ready xt_psum xt_free x_staged comp_psum w_ready act_free dve_free act_full
               index_ready index_stored staged_free""".split()
    (loaded, asks, gives, xs_ready, xt_psum, xt_free, x_staged, comp_psum, w_ready, act_free, dve_free, act_full,
     index_ready, index_stored, staged_free) = (sem("r_" + n) for n in names)
    chunk_psum = [sem(f"r_chunk_psum{c}") for c in range(4)]
    stored = [sem(f"r_stored{u}") for u in range(GRP)]
    P, PS, A, XT = NODE_P, K.PS, K.arena, K.XT
    RW = E8 * D
    at = 0

    def piece(n):
        nonlocal at
        at += n
        return A[:, at - n:at]
    W = piece(DK * RW).rearrange("p (k n) -> p k n", k=DK)
    basis = piece(4 * DK * D).rearrange("p (b k n) -> p b k n", b=4, k=DK)
    comp = piece(32)
    comp_row = piece(32)[0:1, :]
    H = piece(GRP * RW)[:P].rearrange("p (s n) -> p s n", s=GRP)
    assert at <= 19968
    IC = STEPS + RING - TAIL
    Gf = K.G[:].rearrange("p s d -> p (s d)")
    srci, typi, idx = Gf[:, 0:IC].bitcast(I32), Gf[:, IC:2 * IC].bitcast(I32), Gf[:, 2 * IC:3 * IC].bitcast(I32)
    srcf, typf = Gf[:, 3 * IC:4 * IC], Gf[:, 4 * IC:5 * IC]
    loads = [(basis[:, b], K.ins["basis"][b * D:(b + 1) * D, :].rearrange("(k p) n -> p k n", p=128)) for b in range(4)]
    loads += [(comp_row, K.ins["comp"]), (srci, K.ins["src"]), (typi, K.ins["etype"])]
    with nc.Block() as block:
        @block.sync
        def _(sp):
            for dst, src in loads:
                sp.dma_start(dst, src).then_inc(loaded, 16)
            sp.wait_ge(index_ready, 1)
            sp.dma_start(K.index1, idx).then_inc(index_stored, 16)
            with sp.Fori(0, NG) as g:
                for u in range(GRP):
                    t = g * GRP + u
                    sp.wait_ge(act_full, t + 1)
                    sp.wait_ge(dve_free, 1 + t)
                    sp.dma_start(K.htab.rearrange("(p t r) d -> p t (r d)", t=NT, r=E8)[:, bass.ds(t, 1), :].rearrange("p a n -> p (a n)"),
                                 H[:, u, :]).then_inc(stored[u], 16)
            for u in range(GRP):
                sp.wait_ge(stored[u], 16 * NG)
            sp.wait_ge(index_stored, 16)

        @block.scalar
        def _(act):
            act.wait_ge(asks, 1)
            nc.scalar.activation(K.std[:P], K.t3[:P], ACT.Sqrt).then_inc(gives, 1)
            act.sem_inc(xt_free, GRP)

            def group(g, first):
                for u in range(GRP):
                    t = g * GRP + u
                    hold(act, K, xt_psum, t + 1)
                    pt = PS[:, u % 2, 0:DK * P].rearrange("p (k n) -> p k n", k=DK)
                    nc.scalar.copy(K.xTs[:, u], pt).then_inc(x_staged, 1)
                    nc.scalar.copy(XT[:, :, bass.ds(t * P, P)], pt).then_inc(xt_free, 1)
                for u in range(GRP):
                    t = g * GRP + u
                    if not first:
                        act.wait_ge(stored[u], g * 16)
                    for c in range(2):
                        act.wait_ge(chunk_psum[c], t + 1)
                        last = nc.scalar.copy(H[:, u, c * 512:(c + 1) * 512], PS[:P, 2 + c, :])
                        last.then_inc(act_free if c == 0 else act_full, 1)
            group(0, True)
            with act.Fori(1, NG) as g:
                group(g, False)

        @block.tensor
        def _(pe):
            pe.wait_ge(loaded, 16 * len(loads))
            nc.tensor.matmul(PS[:, 7, 0:32], K.ones[0:1, :], comp_row, start=True, stop=True).then_inc(comp_psum, 1)
            pe.wait_ge(w_ready, 1)

            def group(g, first):
                transposes(K, nc, pe, g, xs_ready, xt_psum, xt_free, 2)
                for u in range(GRP):
                    t = g * GRP + u
                    pe.wait_ge(x_staged, t + 1)
                    for c in range(4):
                        if not (first and u == 0):
                            pe.wait_ge((act_free, act_full, staged_free, dve_free)[c], t)
                        for k in range(DK):
                            last = nc.tensor.matmul(PS[:P, 2 + c, :], K.xTs[:, u, k, :], W[:, k, c * 512:(c + 1) * 512], start=k == 0, stop=k == DK - 1)
                        last.then_inc(chunk_psum[c], 1)
            group(0, True)
            with pe.Fori(1, NG) as g:
                group(g, False)

        @block.vector
        def _(v):
            own = K.own_v
            own.eng = v
            link = own.link
            norm_stats(nc, K, v, own, asks, gives)
            v.wait_ge(loaded, 16 * len(loads))
            link(nc.vector.tensor_copy(srcf, srci))
            link(nc.vector.tensor_copy(typf, typi))
            link(nc.vector.scalar_tensor_tensor(srcf, srcf, float(E8), typf, ALU.mult, ALU.add))
            nc.vector.tensor_copy(idx, srcf).then_inc(index_ready, 1)
            v.wait_ge(comp_psum, 1)
            link(nc.vector.tensor_copy(comp, PS[:, 7, 0:32]))
            for b in range(4):
                for r in range(E8):
                    w, f = W[:, :, r * D:(r + 1) * D], comp[:, r * 4 + b:r * 4 + b + 1]
                    if b == 0:
                        own.step(nc.vector.tensor_scalar(w, basis[:, b], f, None, ALU.mult))
                    else:
                        own.step(nc.vector.scalar_tensor_tensor(w, basis[:, b], f, w, ALU.mult, ALU.add))
                own.settle()
            v.sem_inc(w_ready, 1)

            def group(g, first):
                normalise(K, nc, v, g, xt_free, xs_ready)
                for u in range(GRP):
                    t = g * GRP + u
                    if not first:
                        v.wait_ge(stored[u], g * 16)
                    for c in (2, 3):
                        v.wait_ge(chunk_psum[c], t + 1)
                        nc.vector.tensor_copy(H[:, u, c * 512:(c + 1) * 512], PS[:P, 2 + c, :]).then_inc(staged_free if c == 2 else dve_free, 1)
            group(0, True)
            with v.Fori(1, NG) as g:
                group(g, False)


def gather1_mix1(nc, K, sem):
    L = K.pass1 = Pass(K, sem, "sum", K.htab, K.index1, K.keep, ALU.mult, ALU.add, K.lane_keep, 0.0)
    names = """loaded x_staged kq_psum kq_free v_psum v_free kq_done max_ready exp_ready kT_psum kT_free acc_free ctx_done
               ctx_ready ctxT_psum ctxT_ready w_psum""".split()
    (loaded, x_staged, kq_psum, kq_free, v_psum, v_free, kq_done, max_ready, exp_ready, kT_psum, kT_free, acc_free, ctx_done,
     ctx_ready, ctxT_psum, ctxT_ready, w_psum) = (
        sem("m1_" + n) for n in names)
    c = carry_names(sem, "c1_")
    P, PS, A, XT = NODE_P, K.PS, K.arena, K.XT
    HEADS, HD = 4, 32
    at = 0

    def piece(n):
        nonlocal at
        at += n
        return A[:, at - n:at]
    KQ = piece(2 * N).rearrange("p (a n) -> p a n", a=2)
    K.QT = KQ[:, 0, :]
    V = piece(NT * 128)[:P].rearrange("p (t e) -> p t e", e=128)
    wqkv = piece(DK * 384).rearrange("p (k n) -> p k n", k=DK)
    wout, K.Wmix, ctx, ctxT, mask = piece(D), piece(D), piece(128), piece(128), piece(128)
    K.Wloop = piece(DK * D).rearrange("p (k n) -> p k n", k=DK)
    K.row1 = piece(2 * D)[0:1, :]
    K.trail = piece(DK * (1 + LANES)).rearrange("p (k n) -> p k n", k=DK)
    kmax, ksum, kfac = piece(1), piece(NT), piece(1)
    K.arena_free = at
    ins = K.ins
    loads = [(wqkv, ins["mix1_qkv"].rearrange("(k p) n -> p k n", p=128)), (wout, ins["mix1_out"]),
             (K.Wloop, ins["loop_w"].rearrange("(k p) n -> p k n", p=128)), (K.row1[:, 0:D], ins["h_bias"]), (K.row1[:, D:2 * D], ins["mix1_bout"])]
    with nc.Block() as block:
        @block.sync
        def _(sp):
            for dst, src in loads:
                sp.dma_start(dst, src).then_inc(loaded, 16)
            gather_sync(nc, K, sp, L)
            carry_sync(nc, K, sp, L, c)

        @block.gpsimd
        def _(pool):
            gather_pool(nc, K, pool, L)
            carry_pool(nc, K, pool, L, c)

        @block.scalar
        def _(act):
            act.sem_inc(kq_free, GRP)
            act.sem_inc(v_free, GRP)
            act.sem_inc(kT_free, GRP)
            with act.Fori(0, NG) as g:
                for u in range(GRP):
                    nc.scalar.copy(K.xTs[:, u], XT[:, :, bass.ds((g * GRP + u) * P, P)]).then_inc(x_staged, 1)
                for u in range(GRP):
                    t = g * GRP + u
                    hold(act, K, kq_psum, t + 1)
                    nc.scalar.copy(KQ[:, :, bass.ds(t * P, P)], PS[:, u, 0:2 * P].rearrange("p (a n) -> p a n", a=2)).then_inc(kq_free, 1)
                    hold(act, K, v_psum, t + 1)
                    nc.scalar.copy(tile_of(V, t), PS[:P, 5 + u % 3, 0:128]).then_inc(v_free, 1)
            act.wait_ge(max_ready, 1)
            with act.Fori(0, NG) as g:
                for u in range(GRP):
                    t = g * GRP + u
                    hold(act, K, kT_free, t + 1)
                    nc.scalar.activation(K.ys[:, u, 0:P], KQ[:, 1, bass.ds(t * P, P)], ACT.Exp, bias=kmax,
                                         accum_out=ksum[:, bass.ds(t, 1)]).then_inc(exp_ready, 1)
                for u in range(GRP):
                    t = g * GRP + u
                    act.wait_ge(kT_psum, t + 1)
                    act.wait_ge(acc_free, t + 1)
                    nc.scalar.copy(K.xs[:P, u, 0:128], PS[:P, u % 3, 0:128]).then_inc(kT_free, 1)

        @block.tensor
        def _(pe):
            pe.wait_ge(loaded, 16 * len(loads))
            with pe.Fori(0, NG) as g:
                for u in range(GRP):
                    t = g * GRP + u
                    pe.wait_ge(x_staged, t + 1)
                    pe.wait_ge(kq_free, t + 1)
                    for a in range(2):
                        for k in range(DK):
                            last = nc.tensor.matmul(PS[:, u, a * P:(a + 1) * P], wqkv[:, k, a * 128:(a + 1) * 128],
                                                    K.xTs[:, u, k, :], start=k == 0, stop=k == DK - 1)
                    last.then_inc(kq_psum, 1)
                    pe.wait_ge(v_free, free(g, u, 3))
                    for k in range(DK):
                        last = nc.tensor.matmul(PS[:P, 5 + u % 3, 0:128], K.xTs[:, u, k, :], wqkv[:, k, 256:384], start=k == 0, stop=k == DK - 1)
                    last.then_inc(v_psum, 1)
            pe.wait_ge(kq_free, NT + GRP)
            pe.sem_inc(acc_free, GRP)
            nc.tensor.matmul(PS[:, 4, 0:128], K.zeros[:], K.ones[:], start=True, stop=False)
            with pe.Fori(0, NG) as g:
                for u in range(GRP):
                    t = g * GRP + u
                    pe.wait_ge(exp_ready, t + 1)
                    pe.wait_ge(kT_free, free(g, u, 3))
                    nc.tensor.transpose(PS[:P, u % 3, 0:128], K.ys[:, u, 0:P], K.ident[:]).then_inc(kT_psum, 1)
                for u in range(GRP):
                    t = g * GRP + u
                    pe.wait_ge(kT_free, t + 1 + GRP)
                    nc.tensor.matmul(PS[:, 4, 0:128], K.xs[:P, u, 0:128], tile_of(V, t), start=False, stop=False).then_inc(acc_free, 1)
            nc.tensor.matmul(PS[:, 4, 0:128], K.zeros[:], K.ones[:], start=False, stop=True).then_inc(ctx_done, 1)
            pe.wait_ge(ctx_ready, 1)
            nc.tensor.transpose(PS[:, 5, 0:128], ctx, K.ident[:]).then_inc(ctxT_psum, 1)
            pe.wait_ge(ctxT_ready, 1)
            nc.tensor.matmul(PS[:, 6, 0:D], ctxT, wout, start=True, stop=True).then_inc(w_psum, 1)
            carry_tensor(nc, K, pe, L, c)

        @block.vector
        def _(v):
            own = K.own_v
            own.eng = v
            link = own.link
            link(nc.vector.memset(K.G[:, RING - 1, :], 0.0))
            link(nc.vector.memset(mask, 0.0))
            for h in range(HEADS):
                link(nc.vector.memset(mask[h * HD:(h + 1) * HD, h * HD:(h + 1) * HD], 1.0))
            gather_fold(nc, K, v, L, 0, RING, True)
            with v.Fori(1, 12) as i:
                gather_fold(nc, K, v, L, i, RING, False)
            v.wait_ge(kq_free, NT + GRP)
            link(nc.vector.tensor_reduce(kmax, KQ[:, 1, :], AX, ALU.max))
            nc.vector.tensor_scalar(kmax, kmax, -1.0, None, ALU.mult).then_inc(max_ready, 1)
            with v.Fori(12, 36) as i:
                gather_fold(nc, K, v, L, i, RING, False)
            v.wait_ge(ctx_done, 1)
            nc.vector.tensor_tensor(ctx, PS[:, 4, 0:128], mask, ALU.mult).then_inc(ctx_ready, 1)
            v.wait_ge(kT_free, NT + GRP)
            link(nc.vector.tensor_reduce(kfac, ksum, AX, ALU.add))
            link(nc.vector.reciprocal(kfac, kfac))
            link(nc.vector.tensor_scalar(kfac, kfac, HD ** -0.5, None, ALU.mult))
            v.wait_ge(ctxT_psum, 1)
            nc.vector.tensor_copy(ctxT, PS[:, 5, 0:128]).then_inc(ctxT_ready, 1)
            v.wait_ge(w_psum, 1)
            link(nc.vector.tensor_scalar(K.Wmix, PS[:, 6, 0:D], kfac, None, ALU.mult))
            with v.Fori(36, ROUNDS) as i:
                gather_fold(nc, K, v, L, i, RING, False)
            gather_fold(nc, K, v, L, ROUNDS, TAIL, False)
            carry_vector(nc, K, v, own, L, c)
    for s in range(RING):
        K.landed_total[s] += 16 * (ROUNDS + (s < TAIL) + 2 * (s == FIX))


def ends1(nc, K, sem):
    names = "loaded x_staged q_staged ae_psum ae_free m_used pre_ready gelu_done asks gives rows_psum".split()
    loaded, x_staged, q_staged, ae_psum, ae_free, m_used, pre_ready, gelu_done, asks, gives, rows_psum = (sem("e1_" + n) for n in names)
    P, PS, G, A = NODE_P, K.PS, K.G, K.arena
    base = list(K.landed_total)
    X = K.X[:P]
    at = K.arena_free
    a = A[:P, at:at + NT * D].rearrange("p (t d) -> p t d", d=D)
    gb = K.wphi[:].rearrange("p k n -> p (k n)")
    row = K.wtheta[0:1].rearrange("p k n -> p (k n)")
    assert at + NT * D <= 19968
    with nc.Block() as block:
        @block.sync
        def _(sp):
            sp.dma_start(row[:, 0:D], K.ins["gamma1"]).then_inc(loaded, 16)
            sp.dma_start(row[:, D:2 * D], K.ins["beta1"]).then_inc(loaded, 16)

        @block.gpsimd
        def _(pool):
            gather_ends(nc, K, pool, K.pass1, m_used)

        @block.scalar
        def _(act):
            with act.Fori(0, NG) as g:
                for u in range(GRP):
                    hold(act, K, ae_free, g * GRP + u + 1)
                    cols = bass.ds((g * GRP + u) * P, P)
                    nc.scalar.copy(K.xTs[:, u], K.XT[:, :, cols]).then_inc(x_staged, 1)
                    nc.scalar.copy(K.ys[:, u, 0:P], K.QT[:, cols]).then_inc(q_staged, 1)
                for u in range(GRP):
                    t = g * GRP + u
                    hold(act, K, pre_ready, t + 1)
                    nc.scalar.activation(tile_of(a, t), K.xs[:P, u], ACT.Gelu).then_inc(gelu_done, 1)
            act.wait_ge(asks, 1)
            nc.scalar.activation(K.std[:P], K.t3[:P], ACT.Sqrt).then_inc(gives, 1)

        @block.tensor
        def _(pe):
            pe.wait_ge(loaded, 32)
            nc.tensor.matmul(PS[:, 7, :], K.ones[0:1, :], row, start=True, stop=True).then_inc(rows_psum, 1)
            with pe.Fori(0, NG) as g:
                for u in range(GRP):
                    t = g * GRP + u
                    pe.wait_ge(ae_free, t + 1)
                    nc.tensor.matmul(PS[:P, u, :], K.ones[0:1, 0:P], K.row1, start=True, stop=False)
                    pe.wait_ge(x_staged, t + 1)
                    for k in range(DK):
                        nc.tensor.matmul(PS[:P, u, 0:D], K.xTs[:, u, k, :], K.Wloop[:, k, :], start=False, stop=False)
                    pe.wait_ge(q_staged, t + 1)
                    nc.tensor.matmul(PS[:P, u, D:2 * D], K.ys[:, u, 0:P], K.Wmix, start=False, stop=True).then_inc(ae_psum, 1)

        @block.vector
        def _(v):
            own = K.own_v
            own.eng = v
            v.sem_inc(ae_free, GRP)
            v.sem_inc(gelu_done, GRP)
            v.wait_ge(rows_psum, 1)
            own.link(nc.vector.tensor_copy(gb, PS[:, 7, :]))
            with v.Fori(0, NG) as g:
                own.loop(g, 0, 2 * GRP)
                mark = [0] * GRP
                for u in range(GRP):
                    t = g * GRP + u
                    hold(v, K, gelu_done, t + 1)
                    own.step(nc.vector.tensor_scalar(K.xs[:P, u], tile_of(X, t), col(K.rstd, t), col(K.nmr, t), ALU.mult, ALU.add))
                    mark[u] = own.done
                for u in range(GRP):
                    v.wait_ge(K.landed[u], g * 16 + 16 + base[u])
                    v.wait_ge(own.sem, mark[u])
                    nc.vector.tensor_tensor(K.xs[:P, u], G[:P, u, :], K.xs[:P, u], ALU.add).then_inc(m_used, 1)
                for u in range(GRP):
                    v.wait_ge(ae_psum, g * GRP + u + 1)
                    v.wait_ge(m_used, g * GRP + u + 1)
                    nc.vector.tensor_tensor(K.xs[:P, u], K.xs[:P, u], PS[:P, u, 0:D], ALU.add).then_inc(pre_ready, 1)
                for u in range(GRP):
                    t = g * GRP + u
                    nc.vector.tensor_tensor(tile_of(X, t), tile_of(X, t), PS[:P, u, D:2 * D], ALU.add).then_inc(ae_free, 1)
                for u in range(GRP):
                    t = g * GRP + u
                    hold(v, K, gelu_done, t + 1 + GRP)
                    own.step(nc.vector.bn_stats(K.S[:P, bass.ds(t, 1), :], tile_of(a, t)))
            own.left(NG)
            own.settle()
            norm_stats(nc, K, v, own, asks, gives)
            add_normed(nc, K, v, own, a, gb[:P, 0:D], gb[:P, D:2 * D])
    ends_taken(K)


def experts1(nc, K, sem):
    names = """loaded loaded_big asks gives xs_ready xt_psum xt_free x_staged br_psum lg_psum lg_free exp_asks exp_gives w_staged
               wT_psum wT_ready b_psum b_free h_psum h_ready y_psum y_free out_ready out_stored""".split()
    (loaded, loaded_big, asks, gives, xs_ready, xt_psum, xt_free, x_staged, br_psum, lg_psum, lg_free, exp_asks, exp_gives, w_staged,
     wT_psum, wT_ready, b_psum, b_free, h_psum, h_ready, y_psum, y_free, out_ready, out_stored) = (sem("f1_" + n) for n in names)
    P, PS, A, XT = NODE_P, K.PS, K.arena, K.XT
    at = 0

    def piece(n):
        nonlocal at
        at += n
        return A[:, at - n:at]
    W1 = piece(E8 * DK * F).rearrange("p (e k f) -> p e k f", e=E8, k=DK)
    W2 = piece(E8 * FK * D).rearrange("p (e f d) -> p e f d", e=E8, f=FK)
    b1 = piece(E8 * FK).rearrange("p (e f) -> p e f", e=E8)
    b2 = piece(D)[0:E8, :]
    wr = piece(DK * E8).rearrange("p (k e) -> p k e", k=DK)
    br = piece(E8)[0:1, :]
    gcol, bcol = piece(DK), piece(DK)
    HR = 4
    hs = [K.G[:, 2 * s:2 * s + 2, :].rearrange("p a d -> p (a d)")[:, 0:FK * P].rearrange("p (f n) -> p f n", f=FK) for s in range(HR)]
    lgs = piece(NT * E8)[:P].rearrange("p (t e) -> p t e", e=E8)
    ones8, rank, oh, wf = (piece(NT * E8)[:P].rearrange("p (t e) -> p t e", e=E8) for _ in range(4))
    brB = piece(E8)[:P]
    assert at <= 19968
    m1, m2, mi, ee = K.t1[:P], K.t2[:P], K.t3[:P], K.std[:P]
    ins = K.ins
    col_of = lambda name: ins[name].rearrange("a (k p) -> p (a k)", p=128)
    loads = [(wr, ins["ffn1_Wr"].rearrange("(k p) e -> p k e", p=128)), (br, ins["ffn1_br"]), (b2, ins["ffn1_b2"]),
             (gcol, ins["gamma2T"]), (bcol, ins["beta2T"])]
    big = [(W1[:].rearrange("p e k f -> p e (k f)"), ins["ffn1_W1"].rearrange("(e p) n -> p e n", p=128)),
           (W2[:].rearrange("p e f d -> p e (f d)"), ins["ffn1_W2"].rearrange("(e p) n -> p e n", p=128)),
           (b1, ins["ffn1_b1"].rearrange("(e p) n -> p e n", p=128))]
    spread = lambda c: c.unsqueeze(2).broadcast_to([P, NT, E8])
    with nc.Block() as block:
        @block.sync
        def _(sp):
            for dst, src in loads:
                sp.dma_start(dst, src).then_inc(loaded, 16)
            for dst, src in big:
                sp.dma_start(dst, src).then_inc(loaded_big, 16)
            for g in range(NG):
                sp.wait_ge(out_ready, GRP * (g + 1))
                sp.dma_start(K.out3[:, g * GRP:(g + 1) * GRP, :], K.X[:P, g * GRP:(g + 1) * GRP, :]).then_inc(out_stored, 16)
            sp.wait_ge(out_stored, 16 * NG)

        @block.gpsimd
        def _(pool):
            nc.gpsimd.iota(K.ranki[:P], pattern=[[0, NT], [-1, E8]], base=E8, channel_multiplier=0).then_inc(K.ranked, 1)

        @block.scalar
        def _(act):
            act.wait_ge(asks, 1)
            nc.scalar.activation(K.std[:P], K.t3[:P], ACT.Sqrt).then_inc(gives, 1)
            act.sem_inc(xt_free, GRP)
            act.wait_ge(loaded, 16 * len(loads))
            with act.Fori(0, NG) as g:
                for u in range(GRP):
                    t = g * GRP + u
                    act.wait_ge(lg_free, t + 1)
                    act.wait_ge(xt_psum, t + 1)
                    for k in range(DK):
                        last = nc.scalar.activation(K.xTs[:, u, k, :], PS[:, u % 4, k * P:(k + 1) * P], ACT.Identity,
                                                    scale=gcol[:, k:k + 1], bias=bcol[:, k:k + 1])
                    last.then_inc(x_staged, 1)
                    hold(act, K, x_staged, t + 1)
                    nc.scalar.copy(XT[:, :, bass.ds(t * P, P)], K.xTs[:, u]).then_inc(xt_free, 1)
            act.wait_ge(exp_asks, 1)
            nc.scalar.activation(ee, m2, ACT.Exp).then_inc(exp_gives, 1)
            act.sem_inc(wT_ready, 1)
            act.wait_ge(loaded_big, 16 * len(big))
            act.wait_ge(b_free, 1)
            with act.Fori(0, NT) as t:
                hold(act, K, b_psum, t + 1)
                nc.scalar.copy(K.ws[:P], wf[:, bass.ds(t, 1), :].rearrange("p a e -> p (a e)")).then_inc(w_staged, 1)
                act.wait_ge(wT_psum, t + 1)
                nc.scalar.copy(K.wT[:E8], PS[:E8, 6, 0:P]).then_inc(wT_ready, 1)
                for e in range(E8):
                    act.wait_ge(h_psum, t * E8 + e + 1)
                    act.wait_ge(y_free, t * E8 + e + 1)
                    for f in range(FK):
                        last = nc.scalar.activation(hs[e % HR][:, f, :], PS[:, e % HR, f * P:(f + 1) * P], ACT.Gelu, bias=b1[:, e, f:f + 1])
                    last.then_inc(h_ready, 1)

        @block.tensor
        def _(pe):
            pe.wait_ge(loaded, 16 * len(loads))
            nc.tensor.matmul(PS[:, 7, 0:E8], K.ones[0:1, :], br, start=True, stop=True).then_inc(br_psum, 1)
            with pe.Fori(0, NG) as g:
                transposes(K, nc, pe, g, xs_ready, xt_psum, xt_free, 4)
                for u in range(GRP):
                    t = g * GRP + u
                    pe.wait_ge(x_staged, t + 1)
                    pe.wait_ge(lg_free, free(g, u, 3))
                    for k in range(DK):
                        last = nc.tensor.matmul(PS[:P, 4 + u % 3, 0:E8], K.xTs[:, u, k, :], wr[:, k, :], start=k == 0, stop=k == DK - 1)
                    last.then_inc(lg_psum, 1)
            pe.wait_ge(loaded_big, 16 * len(big))
            pe.sem_inc(h_ready, HR)
            pe.sem_inc(b_psum, 1)
            with pe.Fori(0, NT) as t:
                pe.wait_ge(w_staged, t + 1)
                pe.wait_ge(wT_ready, t + 1)
                nc.tensor.transpose(PS[:E8, 6, 0:P], K.ws[:P], K.ident[:P, :P]).then_inc(wT_psum, 1)
                pe.wait_ge(wT_ready, t + 2)
                pe.wait_ge(b_free, t + 1)
                nc.tensor.matmul(PS[:P, 7, 0:D], K.wT[:E8], b2, start=True, stop=True).then_inc(b_psum, 1)

                def hidden(e):
                    pe.wait_ge(h_ready, t * E8 + e + 1)
                    for f in range(FK):
                        for k in range(DK):
                            last = nc.tensor.matmul(PS[:, e % HR, f * P:(f + 1) * P], W1[:, e, k, f * 128:(f + 1) * 128],
                                                    XT[:, k, bass.ds(t * P, P)], start=k == 0, stop=k == DK - 1)
                    last.then_inc(h_psum, 1)

                def output(e):
                    pe.wait_ge(h_ready, t * E8 + e + 1 + HR)
                    pe.wait_ge(y_free, t * E8 + e - 2 + 1 + HR)
                    for f in range(FK):
                        last = nc.tensor.matmul(PS[:P, 4 + e % 2, 0:D], hs[e % HR][:, f, :], W2[:, e, f, :], start=f == 0, stop=f == FK - 1)
                    last.then_inc(y_psum, 1)
                hidden(0)
                for e in range(1, E8):
                    hidden(e)
                    output(e - 1)
                output(E8 - 1)

        @block.vector
        def _(v):
            own = K.own_v
            own.eng = v
            link = own.link
            norm_stats(nc, K, v, own, asks, gives)
            v.wait_ge(br_psum, 1)
            link(nc.vector.tensor_copy(brB, PS[:P, 7, 0:E8]))
            v.wait_ge(K.ranked, 1)
            link(nc.vector.tensor_copy(rank, K.ranki[:P]))
            v.sem_inc(lg_free, GRP)
            with v.Fori(0, NG) as g:
                normalise(K, nc, v, g, xt_free, xs_ready)
                for u in range(GRP):
                    hold(v, K, lg_psum, g * GRP + u + 1)
                    nc.vector.tensor_tensor(tile_of(lgs, g * GRP + u), PS[:P, 4 + u % 3, 0:E8], brB, ALU.add).then_inc(lg_free, 1)
            v.wait_ge(lg_free, NT + GRP)

            def largest(m, pick):
                link(nc.vector.tensor_reduce(m, lgs, AX, ALU.max))
                link(nc.vector.tensor_tensor(pick, lgs, spread(m), ALU.is_equal))
                link(nc.vector.tensor_tensor(pick, pick, rank, ALU.mult))
                link(nc.vector.tensor_reduce(mi, pick, AX, ALU.max))
                link(nc.vector.tensor_tensor(pick, rank, spread(mi), ALU.is_equal))
            largest(m1, oh)
            link(nc.vector.scalar_tensor_tensor(lgs, oh, -BIG, lgs, ALU.mult, ALU.add))
            largest(m2, wf)
            link(nc.vector.tensor_tensor(m2, m2, m1, ALU.subtract))
            v.sem_inc(exp_asks, 1)
            v.wait_ge(exp_gives, 1)
            link(nc.vector.tensor_scalar(m1, ee, 1.0, None, ALU.add))
            link(nc.vector.reciprocal(m1, m1))
            link(nc.vector.tensor_tensor(m2, m1, ee, ALU.mult))
            link(nc.vector.tensor_tensor(oh, oh, spread(m1), ALU.mult))
            link(nc.vector.tensor_tensor(wf, wf, spread(m2), ALU.mult))
            link(nc.vector.tensor_tensor(wf, wf, oh, ALU.add))
            v.sem_inc(b_free, 1)
            v.sem_inc(y_free, HR)
            with v.Fori(0, NT) as t:
                X = tile_of(K.X[:P], t)
                hold(v, K, b_psum, t + 2)
                nc.vector.tensor_tensor(X, X, PS[:P, 7, 0:D], ALU.add).then_inc(b_free, 1)
                for e in range(E8):
                    hold(v, K, y_psum, t * E8 + e + 1)
                    if e == 0:
                        hold(v, K, b_free, t + 2)
                    else:
                        hold(v, K, y_free, t * E8 + e + HR)
                    nc.vector.scalar_tensor_tensor(X, PS[:P, 4 + e % 2, 0:D], wf[:, bass.ds(t, 1), e:e + 1].rearrange("p a e -> p (a e)"), X,
                                                   ALU.mult, ALU.add).then_inc(y_free, 1)
                hold(v, K, y_free, t * E8 + E8 + HR)
                v.sem_inc(out_ready, 1)


def program(nc, out, ins):
    K = Names()
    ctx = ExitStack()
    with ctx:
        def sb(name, shape, dt=F32):
            return ctx.enter_context(nc.sbuf_tensor(name, shape, dt))

        def sem(name):
            return nc.alloc_semaphore(name)

        def dram(name, shape, dt=F32):
            return nc.dram_tensor(name, shape, dt).ap()

        K.ins = ins
        K.in_x, K.in_dst = ins["x"], ins["dst"]
        K.X = sb("X", [128, NT, D])
        K.XT = sb("XT", [128, DK, N])
        K.G = sb("G", [128, RING, D])
        K.keep = sb("keep", [128, STEPS])
        K.pen = sb("pen", [128, STEPS])
        K.arena = sb("arena", [128, 19968])
        K.xs = sb("xs", [128, GRP, D])
        K.xTs = sb("xTs", [128, GRP, DK, NODE_P])
        K.S = sb("S", [128, NT, 6])
        K.t1, K.t2, K.t3, K.std, K.rstd, K.nmr = (sb(n, [128, NT]) for n in ("t1", "t2", "t3", "std", "rstd", "nmr"))
        K.node, K.lane, K.inlane, K.cnt_le, K.cnt_lt = (sb(n, [128, NT]) for n in ("node", "lane", "inlane", "cnt_le", "cnt_lt"))
        K.q2sum, K.k2sum, K.q4sum, K.kscale, K.qscale = (sb(n, [128, NT]) for n in ("q2sum", "k2sum", "q4sum", "kscale", "qscale"))
        K.nrm, K.junk, K.neutral = sb("nrm", [128, 8]), sb("junk", [128, D]), sb("neutral", [1, D])
        K.zeros, K.ys = sb("zeros", [128, 128]), sb("ys", [128, GRP, D])
        K.ranki = sb("ranki", [128, NT, E8], I32)
        K.ws, K.wT = sb("ws", [128, E8]), sb("wT", [E8, NODE_P])
        K.ranked = sem("ranked")
        K.htab = dram("htab", [N * E8, D])
        K.index1 = dram("index1", [LANES, STEPS + RING - TAIL], I32)
        K.out3 = out.rearrange("(p t) d -> p t d", t=NT)
        K.index_sb = sb("index_sb", [128, RING], I32)
        K.nodei, K.lane_i, K.end_i = (sb(n, [128, NT], I32) for n in ("nodei", "lane_i", "end_i"))
        K.goes_on, K.first_i = sb("goes_on", [128, 4]), sb("first_i", [128, 1], I32)
        K.parti = sb("parti", [128, 1], I32)
        K.zero, K.eps = sb("zero", [128, 1]), sb("eps", [128, 1])
        K.ones, K.ident = sb("ones", [128, 128]), sb("ident", [128, 128])
        K.edge_rows = sb("edge_rows_sb", [128, 2, LANES])
        K.lane_keep, K.lane_pen = sb("lane_keep", [128, LANES]), sb("lane_pen", [128, LANES])
        K.wB, K.wphi, K.wtheta = (sb(n, [128, DK, D]) for n in ("wB", "wphi", "wtheta"))
        K.PS = ctx.enter_context(nc.psum_tensor("PS", [128, 8, 512], F32))
        K.pT = lambda u: K.PS[:, u % 4, 0:DK * NODE_P].rearrange("p (k n) -> p k n", k=DK)
        K.pB = lambda u: K.PS[:NODE_P, 4 + u % 3, 0:D]
        K.landed = [sem(f"landed{s}") for s in range(RING)]
        K.landed_total = [16 * GRP if s < GRP else 0 for s in range(RING)]
        K.dve_own, K.waits_passed = sem("dve_own"), sem("waits_passed")
        K.dstf_dram = dram("dstf_dram", [LANES, STEPS])
        K.cnt_dram = dram("cnt_dram", [N + 1])
        K.btab2 = dram("btab", [N, D])
        K.btab = K.btab2.rearrange("(p t) d -> p t d", t=NT)
        wk = lambda name: ins[name].rearrange("(k p) n -> p k n", p=128)
        K.early_loads = [(K.wphi[:], wk("phi_wT")), (K.wtheta[:], wk("theta_wT"))]
        K.hist = dram("hist", [LANES * STEPS + 1, D])
        K.hist3 = K.hist[0:LANES * STEPS, :].rearrange("(p k) d -> p k d", k=STEPS)
        K.in_src = ins["src"]
        stages = (setup, gather0_mix0, ends0, experts0, relations, gather1_mix1, ends1, experts1)
        for stage in stages:
            own_sems = []

            def stage_sem(name):
                own_sems.append(sem(name))
                return own_sems[-1]
            stage(nc, K, stage_sem)
            if stage is not experts1:
                nc.clear_and_free_semaphores(own_sems)
                nc.all_engine_barrier()


def laid_out(inputs):
    import numpy as np
    a = {k: np.ascontiguousarray(v) for k, v in inputs.items()}
    lanes = lambda e, fill: np.concatenate([e, np.full(LANES * STEPS - EDGES, fill, e.dtype)]).reshape(LANES, STEPS)
    staged = lambda e: np.pad(e, ((0, 0), (0, RING - TAIL)))
    out = {
        "x": a["x"], "src": staged(lanes(a["src"], 0)), "dst": lanes(a["dst"], N), "etype": staged(lanes(a["edge_type_8"], 0)),
        "theta_wT": a["L0_gnn_theta_w"].T, "phi_wT": a["L0_gnn_phi_w"].T,
        "theta_b": a["L0_gnn_theta_b"].reshape(1, D), "phi_b": a["L0_gnn_phi_b"].reshape(1, D),
        "mix0_qk": a["L0_mix_W_qkv"][:, :2 * D], "mix0_v": a["L0_mix_W_qkv"][:, 2 * D:],
        "mix0_vT": a["L0_mix_W_qkv"][:, 2 * D:].T, "mix0_b": a["L0_mix_b_qkv"].reshape(1, 3 * D),
        "mix0_bvT": a["L0_mix_b_qkv"][2 * D:].reshape(DK, 128).T,
        "mix0_out": a["L0_mix_W_out"], "mix0_bout": a["L0_mix_b_out"].reshape(1, D),
        "ffn0_Wr": a["L0_ffn_Wr"], "ffn0_br": a["L0_ffn_br"].reshape(1, E8),
        "basis": a["L1_gnn_basis"].reshape(4 * D, D), "comp": a["L1_gnn_comp"].reshape(1, 32), "loop_w": a["L1_gnn_loop_w"],
        "h_bias": a["L1_gnn_h_bias"].reshape(1, D), "gamma1": a["L1_gnn_ln_gamma"].reshape(1, D),
        "beta1": a["L1_gnn_ln_beta"].reshape(1, D),
        "mix1_qkv": a["L1_mix_W_qkv"], "mix1_out": a["L1_mix_W_out"], "mix1_bout": a["L1_mix_b_out"].reshape(1, D),
        "ffn1_Wr": a["L1_ffn_Wr"], "ffn1_br": a["L1_ffn_br"].reshape(1, E8),
        "gamma0": a["L0_ffn_gamma"].reshape(1, D), "beta0": a["L0_ffn_beta"].reshape(1, D),
        "gamma2T": a["L1_ffn_gamma"].reshape(DK, 128).T, "beta2T": a["L1_ffn_beta"].reshape(DK, 128).T,
    }
    for n in (0, 1):
        out[f"ffn{n}_W1"] = a[f"L{n}_ffn_W1"].reshape(E8, DK, 128, F).transpose(0, 2, 1, 3).reshape(E8 * 128, DK * F)
        out[f"ffn{n}_W2"] = a[f"L{n}_ffn_W2"].reshape(E8, FK, 128, D).transpose(0, 2, 1, 3).reshape(E8 * 128, FK * D)
        out[f"ffn{n}_b1"] = a[f"L{n}_ffn_b1"].reshape(E8, FK, 128).transpose(0, 2, 1).reshape(E8 * 128, FK)
        out[f"ffn{n}_b2"] = a[f"L{n}_ffn_b2"]
    return {k: np.ascontiguousarray(v) for k, v in out.items()}


def kernel(**inputs):
    import numpy as np
    import concourse.bacc as bacc
    from concourse.bass_utils import run_bass_kernel_spmd

    nc = bacc.Bacc("TRN2", target_bir_lowering=False, num_devices=1)
    arrays = laid_out(inputs)
    aps = {k: nc.dram_tensor(f"in_{k}_dram", v.shape, mybir.dt.from_np(v.dtype), kind="ExternalInput").ap() for k, v in arrays.items()}
    out = nc.dram_tensor("out_dram", (N, D), F32, kind="ExternalOutput").ap()
    program(nc, out, aps)
    got = run_bass_kernel_spmd(nc, [{f"in_{k}_dram": v for k, v in arrays.items()}], core_ids=[0])
    return got.results[0]["out_dram"]
```

```python
import concourse.bass as bass
from concourse import mybir
from contextlib import ExitStack

F32 = mybir.dt.float32
I32 = mybir.dt.int32
U32 = mybir.dt.uint32
ALU = mybir.AluOpType
ACT = mybir.ActivationFunctionType
AX = mybir.AxisListType.X

N, D = 3125, 256
NODE_P, NT = 125, 25
GRP = 5
NG = NT // GRP
DK = D // 128
EDGES = 103125
LANES = 128
RING = 16
HB = 4
STEPS = 808
TAIL = STEPS % RING
ROUNDS = STEPS // RING
EMPTY = LANES * STEPS
E8, F = 8, 512
FK = F // 128
BLOCK = 128
TURN = 4
SLOT_BLOCKS = (2 * N + E8 * (BLOCK - 1)) // BLOCK
BIG = 1e30
ARENA = 19968
LN_EPS = 1e-5
assert NODE_P * NT == N and LANES * STEPS > EDGES and TAIL == RING // 2 and SLOT_BLOCKS % TURN == 0


class Own:

    def __init__(self, eng, sem):
        self.eng, self.sem, self.done = eng, sem, 0

    def step(self, ins):
        ins.then_inc(self.sem, 1)
        self.done = self.done + 1

    def settle(self):
        self.eng.wait_ge(self.sem, self.done)

    def link(self, ins):
        self.step(ins)
        self.settle()

    def loop(self, i, start, per):
        self.base, self.per = self.done, per
        self.done = (i - start) * per + self.base

    def left(self, turns):
        self.done = self.base + turns * self.per


def free(g, u, slots):
    before = slots if u >= slots else GRP - max(w for w in range(GRP) if w % slots == u) + u
    return g * GRP + u + 1 + GRP - before


class Names:
    pass


def hold(eng, K, sem, value):
    eng.wait_ge(sem, value).then_inc(K.waits_passed, 1)


def norm_stats(nc, K, v, own, act_asks, act_gives):
    S, P = K.S, NODE_P
    own.link(nc.vector.tensor_tensor(K.t1[:P], S[:P, :, 1], S[:P, :, 4], ALU.add))
    own.link(nc.vector.tensor_tensor(K.t2[:P], S[:P, :, 1], S[:P, :, 4], ALU.subtract))
    own.link(nc.vector.tensor_tensor(K.t3[:P], S[:P, :, 2], S[:P, :, 5], ALU.add))
    own.link(nc.vector.tensor_tensor(K.t2[:P], K.t2[:P], K.t2[:P], ALU.mult))
    own.link(nc.vector.tensor_scalar(K.t2[:P], K.t2[:P], 0.25, LN_EPS, ALU.mult, ALU.add))
    nc.vector.scalar_tensor_tensor(K.t3[:P], K.t3[:P], 1.0 / D, K.t2[:P], ALU.mult, ALU.add).then_inc(act_asks, 1)
    v.wait_ge(act_gives, 1)
    own.link(nc.vector.reciprocal(K.rstd[:P], K.std[:P]))
    own.link(nc.vector.scalar_tensor_tensor(K.nmr[:P], K.t1[:P], -0.5, K.rstd[:P], ALU.mult, ALU.mult))


def setup(nc, K, sem):
    loaded_x, loaded_w, loaded_e = sem("loaded_x"), sem("loaded_w"), sem("loaded_e")
    ident_zero, ident_done, consts = sem("ident_zero"), sem("ident_done"), sem("consts")
    stats_asks, stats_gives = sem("stats_asks"), sem("stats_gives")
    xs_ready, xs_free, xt_psum, xt_free, xt_copied = (sem(n) for n in ("xs_ready", "xs_free", "xt_psum", "xt_free", "xt_copied"))
    b_psum, b_free, b_stored = sem("b_psum"), sem("b_free"), sem("b_stored")
    wdiff, edge_diag, edge_rows, lanes_of = sem("wdiff"), sem("edge_diag"), sem("edge_rows"), sem("lanes_of")
    dstf_ready, dstf_stored, cnt_used, cnt_ready, cnt_stored, cnt_back = (
        sem(n) for n in ("dstf_ready", "dstf_stored", "cnt_used", "cnt_ready", "cnt_stored", "cnt_back"))
    seg_ready, row_bias, row_done = sem("seg_ready"), sem("row_bias"), sem("row_done")
    P = NODE_P
    PS, A = K.PS, K.arena
    Ball = A[:P, 0:NT * D].rearrange("p (t d) -> p t d", d=D)
    cmp_ = A[:P, NT * D:NT * D + NT * LANES].rearrange("p (t l) -> p t l", l=LANES)
    dsti = A[:, 2 * NT * D:2 * NT * D + STEPS].bitcast(I32)
    diag = A[:, 2 * NT * D + STEPS:2 * NT * D + STEPS + 256].rearrange("p (a l) -> p a l", a=2)
    dstf = K.keep
    rows = K.G[:, 0:15, :].rearrange("p s d -> p (s d)")[:P, 0:GRP * 768]
    cg = K.arena[:P, 2 * NT * D + STEPS + 256:2 * NT * D + STEPS + 256 + GRP * STEPS].rearrange("p (s k) -> p s k", s=GRP)

    with nc.Block() as block:
        @block.sync
        def _(sp):
            sp.dma_start(dsti, K.in_dst).then_inc(loaded_e, 16)
            sp.dma_start(K.X[:P], K.in_x.rearrange("(p t) d -> p t d", t=NT)).then_inc(loaded_x, 16)
            for dst, src in K.early_loads:
                sp.dma_start(dst, src).then_inc(loaded_w, 16)
            sp.wait_ge(dstf_ready, 1)
            sp.dma_start(K.dstf_dram, dstf[:]).then_inc(dstf_stored, 16)
            for g in range(NG):
                sp.wait_ge(b_free, GRP * (g + 1) + GRP)
                sp.dma_start(K.btab[:, g * GRP:(g + 1) * GRP, :], Ball[:, g * GRP:(g + 1) * GRP, :]).then_inc(b_stored, 16)
            sp.wait_ge(cnt_ready, 1)
            sp.dma_start(K.cnt_dram[1:N + 1].rearrange("(p t) -> p t", t=NT), K.cnt_le[:P]).then_inc(cnt_stored, 16)
            sp.dma_start(K.cnt_dram[0:1].rearrange("(a b) -> a b", a=1), K.zero[0:1, 0:1]).then_inc(cnt_stored, 16)
            sp.wait_ge(cnt_stored, 32)
            sp.dma_start(K.cnt_lt[:P], K.cnt_dram[0:N].rearrange("(p t) -> p t", t=NT)).then_inc(cnt_back, 16)
            sp.wait_ge(b_stored, 16 * NG)

        @block.gpsimd
        def _(pool):
            nc.gpsimd.memset(K.ident[:], 0.0).then_inc(ident_zero, 1)
            pool.wait_ge(ident_zero, 1)
            nc.gpsimd.affine_select(out=K.ident[:], in_=K.ident[:], compare_op=ALU.not_equal, fill=1.0, base=0,
                                    pattern=[[-1, 128]], channel_multiplier=1).then_inc(ident_done, 1)
            nc.gpsimd.iota(K.nodei[:P], pattern=[[1, NT]], base=0, channel_multiplier=NT).then_inc(consts, 1)
            nc.gpsimd.iota(K.parti[:], pattern=[[0, 1]], base=0, channel_multiplier=1).then_inc(consts, 1)
            nc.gpsimd.memset(K.zero[:], 0.0).then_inc(consts, 1)
            nc.gpsimd.memset(K.ones[:], 1.0).then_inc(consts, 1)
            nc.gpsimd.memset(K.eps[:], LN_EPS).then_inc(consts, 1)
            pool.wait_ge(lanes_of, 1)
            pool.wait_ge(dstf_stored, 16)
            for t in range(NT):
                if t >= GRP:
                    pool.wait_ge(cnt_used, t - GRP + 1)
                nc.gpsimd.indirect_dma_start(cg[:, t % GRP, :], None, K.dstf_dram,
                                             bass.IndirectOffsetOnAxis(ap=K.lane_i[:P, t:t + 1], axis=0)
                                             ).then_inc(K.landed[t % GRP], 16)

        @block.scalar
        def _(act):
            act.wait_ge(stats_asks, 1)
            nc.scalar.activation(K.std[:P], K.t3[:P], ACT.Sqrt).then_inc(stats_gives, 1)
            act.sem_inc(xt_free, GRP)
            act.sem_inc(b_free, GRP)
            with act.Fori(0, NG) as g:
                for u in range(GRP):
                    hold(act, K, xt_psum, g * GRP + u + 1)
                    nc.scalar.copy(K.xTs[:, u], K.pT(u)).then_inc(xt_copied, 1)
                    nc.scalar.copy(K.XT[:, :, bass.ds((g * GRP + u) * P, P)], K.pT(u)).then_inc(xt_free, 1)
                for u in range(GRP):
                    hold(act, K, b_psum, g * GRP + u + 1)
                    nc.scalar.copy(Ball[:, bass.ds(g * GRP + u, 1), :], K.pB(u)).then_inc(b_free, 1)

        @block.tensor
        def _(pe):
            pe.wait_ge(ident_done, 1)
            pe.wait_ge(consts, 5)
            pe.wait_ge(edge_diag, 1)
            nc.tensor.matmul(PS[:, 7, 0:256], K.ones[:, 0:128], diag.rearrange("p a l -> p (a l)"),
                             start=True, stop=True).then_inc(edge_rows, 1)
            pe.wait_ge(wdiff, 1)
            with pe.Fori(0, NG) as g:
                for u in range(GRP):
                    pe.wait_ge(xs_ready, g * GRP + u + 1)
                    pe.wait_ge(xt_free, free(g, u, 4))
                    for k in range(DK):
                        last = nc.tensor.transpose(K.pT(u)[:, k, :], K.xs[:P, u, k * 128:(k + 1) * 128], K.ident[:P, :P])
                    last.then_inc(xt_psum, 1)
                for u in range(GRP):
                    pe.wait_ge(xt_copied, g * GRP + u + 1)
                    pe.wait_ge(b_free, free(g, u, 3))
                    for k in range(DK):
                        last = nc.tensor.matmul(K.pB(u), K.xTs[:, u, k, :], K.wB[:, k, :], start=k == 0, stop=k == DK - 1)
                    last.then_inc(b_psum, 1)

        @block.vector
        def _(v):
            own = K.own_v = Own(v, K.dve_own)
            v.wait_ge(loaded_e, 16)
            own.link(nc.vector.tensor_copy(dstf[:], dsti))
            v.sem_inc(dstf_ready, 1)
            v.wait_ge(ident_done, 1)
            own.link(nc.vector.tensor_scalar(diag[:, 0, :], K.ident[:], dstf[:, 0:1], None, ALU.mult))
            nc.vector.tensor_scalar(diag[:, 1, :], K.ident[:], dstf[:, STEPS - 1:STEPS], None, ALU.mult).then_inc(edge_diag, 1)
            v.wait_ge(consts, 5)
            own.link(nc.vector.tensor_copy(K.node[:P], K.nodei[:P]))
            v.wait_ge(edge_rows, 1)
            own.link(nc.vector.tensor_copy(K.edge_rows[:].rearrange("p a l -> p (a l)"), PS[:, 7, 0:256]))
            own.link(nc.vector.tensor_tensor(cmp_, K.edge_rows[:P, 1:2, :].broadcast_to([P, NT, LANES]),
                                             K.node[:P].unsqueeze(2).broadcast_to([P, NT, LANES]), ALU.is_le))
            own.link(nc.vector.tensor_reduce(K.lane[:P], cmp_, AX, ALU.add))
            nc.vector.tensor_copy(K.lane_i[:P], K.lane[:P]).then_inc(lanes_of, 1)
            v.wait_ge(loaded_w, 16 * len(K.early_loads))
            nc.vector.tensor_tensor(K.wB[:], K.wphi[:], K.wtheta[:], ALU.subtract).then_inc(wdiff, 1)
            v.wait_ge(loaded_x, 16)
            with v.Fori(0, NT) as t:
                nc.vector.bn_stats(K.S[:P, bass.ds(t, 1), :], K.X[:P, bass.ds(t, 1), :]).then_inc(K.dve_own, 1)
            own.done += NT
            own.settle()
            norm_stats(nc, K, v, own, stats_asks, stats_gives)
            with v.Fori(0, NG) as g:
                normalise(K, nc, v, g, xt_free, xs_ready)
                for u in range(GRP):
                    hold(v, K, K.landed[u], 16 * g + 16)
                    nc.vector.tensor_scalar(cg[:, u, :], cg[:, u, :], K.node[:P, bass.ds(g * GRP + u, 1)], None,
                                            ALU.is_le, ALU.add,
                                            accum_out=K.inlane[:P, bass.ds(g * GRP + u, 1)]).then_inc(cnt_used, 1)
            v.wait_ge(cnt_used, NT)
            nc.vector.scalar_tensor_tensor(K.cnt_le[:P], K.lane[:P], float(STEPS), K.inlane[:P], ALU.mult, ALU.add).then_inc(cnt_ready, 1)
            own.link(nc.vector.tensor_scalar(K.pen[:], dstf[:], dstf[:, 0:1], None, ALU.is_equal, ALU.add, accum_out=K.goes_on[:, 2:3]))
            own.link(nc.vector.tensor_copy(K.goes_on[:, 3:4], K.parti[:]))
            own.link(nc.vector.scalar_tensor_tensor(K.goes_on[:, 3:4], K.goes_on[:, 3:4], float(STEPS), K.goes_on[:, 2:3], ALU.mult, ALU.add))
            own.link(nc.vector.tensor_scalar(K.first_i[:], K.goes_on[:, 3:4], -1.0, None, ALU.add))
            own.link(nc.vector.tensor_tensor(K.pen[:, 1:STEPS], dstf[:, 1:STEPS], dstf[:, 0:STEPS - 1], ALU.is_equal))
            v.wait_ge(dstf_stored, 16)
            own.link(nc.vector.tensor_copy(K.keep[:, 1:STEPS], K.pen[:, 1:STEPS]))
            own.link(nc.vector.memset(K.keep[:, 0:1], 0.0))
            own.link(nc.vector.tensor_scalar(K.pen[:], K.keep[:], BIG, -BIG, ALU.mult, ALU.add))
            own.link(nc.vector.memset(K.lane_keep[:], 0.0))
            own.link(nc.vector.tensor_tensor(K.lane_keep[:, 1:LANES], K.edge_rows[:, 0, 1:LANES], K.edge_rows[:, 1, 0:LANES - 1], ALU.is_equal))
            own.link(nc.vector.tensor_tensor(K.lane_pen[:], K.lane_keep[:], K.ident[:], ALU.mult))
            own.link(nc.vector.tensor_reduce(K.goes_on[:, 0:1], K.lane_pen[:], AX, ALU.add))
            own.link(nc.vector.tensor_scalar(K.goes_on[:, 1:2], K.goes_on[:, 0:1], BIG, -BIG, ALU.mult, ALU.add))
            own.link(nc.vector.tensor_tensor(K.lane_pen[:], K.edge_rows[:, 0, :], K.edge_rows[:, 1, :], ALU.is_equal))
            own.link(nc.vector.tensor_tensor(K.lane_keep[:], K.lane_keep[:], K.lane_pen[:], ALU.mult))
            own.link(nc.vector.tensor_scalar(K.lane_pen[:], K.lane_keep[:], BIG, -BIG, ALU.mult, ALU.add))
            v.wait_ge(cnt_back, 16)
            t2, t3 = K.t2[:P], K.t3[:P]
            own.link(nc.vector.tensor_tensor(t3, K.cnt_lt[:P], K.cnt_le[:P], ALU.is_equal))
            own.link(nc.vector.tensor_scalar(t2, K.cnt_le[:P], -1.0, float(EMPTY + 1), ALU.mult, ALU.add))
            own.link(nc.vector.tensor_tensor(t2, t2, t3, ALU.mult))
            own.link(nc.vector.scalar_tensor_tensor(t2, K.cnt_le[:P], -1.0, t2, ALU.add, ALU.add))
            own.link(nc.vector.tensor_copy(K.end_i[:P], t2))



class Pass:

    def __init__(self, K, sem, name, table, index, factor, op0, op1, lane_factor, neutral):
        self.table, self.index, self.factor = table, index, factor
        self.op0, self.op1, self.lane_factor, self.neutral = op0, op1, lane_factor, neutral
        self.base = K.landed_total
        self.folded = sem(name + "_folded")
        self.index_staged = [sem(f"{name}_index_staged{h}") for h in range(2)]
        self.written = [sem(f"{name}_written{b}") for b in range(RING // HB)]


def gather_rounds(eng, one):
    one(0, RING, True)
    with eng.Fori(1, ROUNDS) as i:
        one(i, RING, False)
    one(ROUNDS, TAIL, False)


def gather_sync(nc, K, sp, L):
    half = RING // 2

    def stage(i, h):
        sp.dma_start(K.index_sb[:, h * half:(h + 1) * half], L.index[:, bass.ds(i * RING + h * half, half)]
                     ).then_inc(L.index_staged[h], 16)

    def one(i, steps, first):
        for b in range(steps // HB):
            sp.wait_ge(L.folded, i * RING + HB * (b + 1))
            sp.dma_start(K.hist3[:, bass.ds(i * RING + b * HB, HB), :], K.G[:, b * HB:(b + 1) * HB, :]
                         ).then_inc(L.written[b], 16)
            if steps == RING and b % 2 == 1:
                stage(i + 1, b // 2)

    stage(0, 0)
    stage(0, 1)
    gather_rounds(sp, one)


def gather_pool(nc, K, pool, L):
    def one(i, steps, first):
        for s in range(steps):
            if s % (RING // 2) == 0:
                hold(pool, K, L.index_staged[s // (RING // 2)], i * 16 + 16)
            if s % HB == 0 and not first:
                hold(pool, K, L.written[s // HB], i * 16)
                hold(pool, K, L.folded, (i - 1) * RING + s + HB + 1)
            if first and s == RING - 1:
                pool.wait_ge(L.folded, 1)
            nc.gpsimd.indirect_dma_start(K.G[:, s, :], None, L.table,
                                         bass.IndirectOffsetOnAxis(ap=K.index_sb[:, s:s + 1], axis=0)
                                         ).then_inc(K.landed[s], 16)
    gather_rounds(pool, one)


def gather_fold(nc, K, v, L, i, steps, first, beside=None):
    for s in range(steps):
        hold(v, K, K.landed[s], i * 16 + 16 + L.base[s])
        if not (first and s == 0):
            v.wait_ge(L.folded, i * RING + s)
        nc.vector.scalar_tensor_tensor(K.G[:, s, :], K.G[:, (s - 1) % RING, :], L.factor[:, bass.ds(i * RING + s, 1)],
                                       K.G[:, s, :], L.op0, L.op1).then_inc(L.folded, 1)
        if beside:
            beside(s)


BESIDE = 36


CARRY_SEMS = "trail_up scanned trail_back first_landed fixed neutral_set neutral_stored".split()
FIX = RING // 2


def carry_tensor(nc, K, pe, L, c):
    pe.wait_ge(L.folded, STEPS)
    for k in range(DK):
        last = nc.tensor.transpose(K.PS[:, 0, k * 128:(k + 1) * 128], K.G[:, TAIL - 1, k * 128:(k + 1) * 128], K.ident[:])
    last.then_inc(c.trail_up, 1)
    pe.wait_ge(c.scanned, DK)
    for k in range(DK):
        last = nc.tensor.transpose(K.PS[:, 1, k * 128:(k + 1) * 128], K.trail[:, k, 0:LANES], K.ident[:])
    last.then_inc(c.trail_back, 1)


def carry_vector(nc, K, v, own, L, c):
    own.link(nc.vector.memset(K.neutral[:], L.neutral))
    v.sem_inc(c.neutral_set, 1)
    own.link(nc.vector.memset(K.trail[:, :, 0:1], 0.0))
    v.wait_ge(c.trail_up, 1)
    for k in range(DK):
        nc.vector.tensor_tensor_scan(K.trail[:, k, 1:1 + LANES], L.lane_factor[:], K.PS[:, 0, k * 128:(k + 1) * 128], 0.0,
                                     L.op0, L.op1).then_inc(c.scanned, 1)
    v.wait_ge(c.trail_back, 1)
    own.link(nc.vector.tensor_scalar(K.junk[:], K.PS[:, 1, 0:D], K.goes_on[:, 0:1],
                                     K.goes_on[:, 1:2] if L.neutral else 0.0, ALU.mult, ALU.add))
    v.wait_ge(c.first_landed, 1)
    nc.vector.tensor_tensor(K.G[:, FIX, :], K.G[:, FIX, :], K.junk[:], L.op1).then_inc(c.fixed, 1)


def carry_pool(nc, K, pool, L, c):
    for b in range(RING // HB):
        pool.wait_ge(L.written[b], 16 * (ROUNDS + (b < TAIL // HB)))
    pool.wait_ge(L.folded, STEPS)
    index = bass.IndirectOffsetOnAxis(ap=K.first_i[:, 0:1], axis=0)
    nc.gpsimd.indirect_dma_start(K.G[:, FIX, :], None, K.hist, index).then_inc(K.landed[FIX], 16)
    pool.wait_ge(K.landed[FIX], L.base[FIX] + 16 * (ROUNDS + 1))
    pool.sem_inc(c.first_landed, 1)
    pool.wait_ge(c.fixed, 1)
    nc.gpsimd.indirect_dma_start(K.hist, index, K.G[:, FIX, :], None).then_inc(K.landed[FIX], 16)
    pool.wait_ge(K.landed[FIX], L.base[FIX] + 16 * (ROUNDS + 2))


def carry_sync(nc, K, sp, L, c):
    sp.wait_ge(c.neutral_set, 1)
    sp.dma_start(K.hist[EMPTY:EMPTY + 1, :], K.neutral[0:1, :]).then_inc(c.neutral_stored, 16)
    sp.wait_ge(c.neutral_stored, 16)
    for h in range(2):
        sp.wait_ge(L.index_staged[h], 16 * (ROUNDS + 1))


def carry_names(sem, prefix):
    c = Names()
    (c.trail_up, c.scanned, c.trail_back, c.first_landed, c.fixed, c.neutral_set, c.neutral_stored) = (
        sem(prefix + n) for n in CARRY_SEMS)
    return c


def gather0_mix0(nc, K, sem):
    L = K.pass0 = Pass(K, sem, "max", K.btab2, K.in_src, K.pen, ALU.add, ALU.max, K.lane_pen, -BIG)
    names = """loaded_m centred x_staged qk_psum qk_free q2_ready q2T_psum q2T_free stats_done roots asks r_ready
               v_psum v_free vk_ready kv_done kv_copied norm_root kvw_psum acc_free
               end_weights q_staged ae_psum ae_free mix_added p1_psum p1_free""".split()
    (loaded_m, centred, x_staged, qk_psum, qk_free, q2_ready, q2T_psum, q2T_free, stats_done, roots, asks, r_ready,
     v_psum, v_free, vk_ready, kv_done, kv_copied, norm_root, kvw_psum, acc_free,
     end_weights, q_staged, ae_psum, ae_free, mix_added, p1_psum, p1_free) = (
        sem("m0_" + n) for n in names)
    c = carry_names(sem, "c0_")
    P, PS, A = NODE_P, K.PS, K.arena
    K2 = A[:P, 0:NT * D].rearrange("p (t d) -> p t d", d=D)
    K.dst_part = K2
    at = NT * D
    Q2T = K.Q2T = A[:, at:at + DK * N].rearrange("p (k n) -> p k n", k=DK)
    at += DK * N

    def piece(n):
        nonlocal at
        at += n
        return A[:, at - n:at]
    wqk = piece(DK * 512).rearrange("p (k n) -> p k n", k=DK)
    wv, wvT, wout = (piece(DK * D).rearrange("p (k n) -> p k n", k=DK) for _ in range(3))
    K.KVW = KVW = piece(DK * D).rearrange("p (k n) -> p k n", k=DK)
    K.wE = wE = piece(DK * 512).rearrange("p (k n) -> p k n", k=DK)
    kvT = piece(DK * D).rearrange("p (k n) -> p k n", k=DK)
    K.trail = piece(DK * (1 + LANES)).rearrange("p (k n) -> p k n", k=DK)
    K.rowE = piece(512)[0:1, :]
    rowqkv = piece(768)[0:1, :]
    rowb = piece(512)[0:1, :]
    rowo = piece(256)[0:1, :]
    bvT = piece(2)
    assert at <= ARENA
    wk = lambda name: K.ins[name].rearrange("(k p) n -> p k n", p=128)
    loads = [(wqk, wk("mix0_qk")), (wv, wk("mix0_v")), (wvT, wk("mix0_vT")), (wout, wk("mix0_out")),
             (rowqkv, K.ins["mix0_b"]), (rowb[:, 0:256], K.ins["theta_b"]), (rowb[:, 256:512], K.ins["phi_b"]),
             (rowo, K.ins["mix0_bout"]), (bvT, K.ins["mix0_bvT"])]

    with nc.Block() as block:
        @block.sync
        def _(sp):
            for dst, src in loads:
                sp.dma_start(dst, src).then_inc(loaded_m, 16)
            gather_sync(nc, K, sp, L)
            carry_sync(nc, K, sp, L, c)

        @block.gpsimd
        def _(pool):
            gather_pool(nc, K, pool, L)
            carry_pool(nc, K, pool, L, c)

        @block.scalar
        def _(act):
            act.sem_inc(qk_free, GRP)
            act.sem_inc(q2T_free, GRP)
            act.sem_inc(v_free, GRP)
            with act.Fori(0, NG) as g:
                for u in range(GRP):
                    nc.scalar.copy(K.xTs[:, u], K.XT[:, :, bass.ds((g * GRP + u) * P, P)]).then_inc(x_staged, 1)
                for u in range(GRP):
                    t = g * GRP + u
                    hold(act, K, qk_psum, t + 1)
                    nc.scalar.activation(K.xs[:P, u], PS[:P, u, 0:D], ACT.Square,
                                         accum_out=K.q2sum[:P, bass.ds(t, 1)]).then_inc(q2_ready, 1)
                    nc.scalar.activation(K2[:, bass.ds(t, 1), :], PS[:P, u:u + 1, D:2 * D], ACT.Square,
                                         accum_out=K.k2sum[:P, bass.ds(t, 1)]).then_inc(qk_free, 1)
                    hold(act, K, q2_ready, t + 1)
                    nc.scalar.activation(K.junk[:P], K.xs[:P, u], ACT.Square,
                                         accum_out=K.q4sum[:P, bass.ds(t, 1)]).then_inc(stats_done, 1)
                for u in range(GRP):
                    t = g * GRP + u
                    hold(act, K, q2T_psum, t + 1)
                    nc.scalar.copy(Q2T[:, :, bass.ds(t * P, P)],
                                   PS[:, 5 + u % 3, 0:DK * P].rearrange("p (k n) -> p k n", k=DK)).then_inc(q2T_free, 1)
            act.wait_ge(stats_done, NT)
            nc.scalar.activation(K.std[:P], K.q4sum[:P], ACT.Sqrt).then_inc(roots, 1)
            act.wait_ge(r_ready, 1)
            with act.Fori(0, NG) as g:
                for u in range(GRP):
                    nc.scalar.copy(K.xTs[:, u], K.XT[:, :, bass.ds((g * GRP + u) * P, P)]).then_inc(x_staged, 1)
                for u in range(GRP):
                    t = g * GRP + u
                    hold(act, K, v_psum, t + 1)
                    hold(act, K, acc_free, t + 1)
                    nc.scalar.activation(K.xs[:P, u], PS[:P, u % 3, 0:D], ACT.Copy,
                                         scale=K.kscale[:P, bass.ds(t, 1)]).then_inc(v_free, 1)
                    nc.scalar.activation(K.ys[:P, u], K2[:, bass.ds(t, 1), :].rearrange("p a d -> p (a d)"), ACT.Square,
                                         scale=K.kscale[:P, bass.ds(t, 1)]).then_inc(vk_ready, 1)
            act.wait_ge(kv_copied, 2)
            nc.scalar.activation(K.nrm[:, 2:4], K.nrm[:, 0:2], ACT.Sqrt).then_inc(norm_root, 1)
            act.wait_ge(acc_free, NT + GRP)
            act.sem_inc(ae_free, GRP)
            with act.Fori(0, NG) as g:
                for u in range(GRP):
                    t = g * GRP + u
                    hold(act, K, ae_free, t + 1)
                    hold(act, K, p1_free, t + 1)
                    cols = bass.ds(t * P, P)
                    nc.scalar.copy(K.xTs[:, u], K.XT[:, :, cols]).then_inc(x_staged, 1)
                    nc.scalar.copy(K.ys[:, u, 0:DK * P].rearrange("p (k n) -> p k n", k=DK), K.Q2T[:, :, cols]).then_inc(q_staged, 1)
                for u in range(GRP):
                    t = g * GRP + u
                    hold(act, K, mix_added, t + 1)
                    nc.scalar.copy(tile_of(K.dst_part, t), PS[:P, u, 0:D]).then_inc(ae_free, 1)

        @block.tensor
        def _(pe):
            pe.wait_ge(centred, 1)
            with pe.Fori(0, NG) as g:
                for u in range(GRP):
                    t = g * GRP + u
                    pe.wait_ge(x_staged, t + 1)
                    pe.wait_ge(qk_free, t + 1)
                    for k in range(DK):
                        nc.tensor.matmul(PS[:P, u, :], K.xTs[:, u, k, :], wqk[:, k, :], start=k == 0, stop=False)
                    nc.tensor.matmul(PS[:P, u, :], K.ones[0:1, 0:P], rowqkv[:, 0:512], start=False, stop=True).then_inc(qk_psum, 1)
                for u in range(GRP):
                    t = g * GRP + u
                    pe.wait_ge(q2_ready, t + 1)
                    pe.wait_ge(q2T_free, free(g, u, 3))
                    for k in range(DK):
                        last = nc.tensor.transpose(PS[:, 5 + u % 3, k * P:(k + 1) * P], K.xs[:P, u, k * 128:(k + 1) * 128], K.ident[:P, :P])
                    last.then_inc(q2T_psum, 1)
            pe.wait_ge(q2T_free, NT + GRP)
            pe.sem_inc(acc_free, GRP)
            for bank in (5, 6):
                nc.tensor.matmul(PS[:, bank, :], K.zeros[:, 0:128], wqk[:, 0, :], start=True, stop=False)
            with pe.Fori(0, NG) as g:
                for u in range(GRP):
                    t = g * GRP + u
                    pe.wait_ge(x_staged, t + 1 + NT)
                    pe.wait_ge(v_free, free(g, u, 3))
                    for k in range(DK):
                        nc.tensor.matmul(PS[:P, u % 3, 0:D], K.xTs[:, u, k, :], wv[:, k, :], start=k == 0, stop=False)
                    nc.tensor.matmul(PS[:P, u % 3, 0:D], K.ones[0:1, 0:P], rowqkv[:, 512:768], start=False, stop=True).then_inc(v_psum, 1)
                for u in range(GRP):
                    t = g * GRP + u
                    pe.wait_ge(vk_ready, t + 1)
                    for k in range(DK):
                        nc.tensor.matmul(PS[:, 5, k * D:(k + 1) * D], K.xs[:P, u, k * 128:(k + 1) * 128],
                                         K2[:, bass.ds(t, 1), :].rearrange("p a d -> p (a d)"), start=False, stop=False)
                        last = nc.tensor.matmul(PS[:, 6, k:k + 1], K.ys[:P, u, k * 128:(k + 1) * 128], K.ones[:P, 0:1],
                                                start=False, stop=False)
                    last.then_inc(acc_free, 1)
            for bank in (5, 6):
                last = nc.tensor.matmul(PS[:, bank, :], K.zeros[:, 0:128], wqk[:, 0, :], start=False, stop=True)
            last.then_inc(kv_done, 1)
            for k in range(DK):
                for d in range(DK):
                    nc.tensor.matmul(PS[:, 3, k * D:(k + 1) * D], wvT[:, d, k * 128:(k + 1) * 128], wout[:, d, :], start=d == 0, stop=d == DK - 1)
            for d in range(DK):
                nc.tensor.matmul(PS[0:1, 4, 0:D], bvT[:, d:d + 1], wout[:, d, :], start=d == 0, stop=d == DK - 1)
            pe.wait_ge(kv_copied, 2)
            pe.wait_ge(v_free, NT + GRP)
            for k in range(DK):
                for d in range(DK):
                    last = nc.tensor.matmul(PS[:, 7, k * D:(k + 1) * D], kvT[:, d, k * 128:(k + 1) * 128], wout[:, d, :], start=d == 0, stop=d == DK - 1)
            last.then_inc(kvw_psum, 1)
            pe.wait_ge(end_weights, 1)
            with pe.Fori(0, NG) as g:
                for u in range(GRP):
                    t = g * GRP + u
                    pe.wait_ge(x_staged, t + 1 + 2 * NT)
                    pe.wait_ge(ae_free, t + 1)
                    for k in range(DK):
                        nc.tensor.matmul(PS[:P, u, :], K.xTs[:, u, k, :], wE[:, k, :], start=k == 0, stop=False)
                    nc.tensor.matmul(PS[:P, u, :], K.ones[0:1, 0:P], K.rowE, start=False, stop=True).then_inc(ae_psum, 1)
                for u in range(GRP):
                    pe.wait_ge(q_staged, g * GRP + u + 1)
                    pe.wait_ge(p1_free, free(g, u, 3))
                    for k in range(DK):
                        last = nc.tensor.matmul(PS[:P, 5 + u % 3, 0:D], K.ys[:, u, k * P:(k + 1) * P], KVW[:, k, :],
                                                start=k == 0, stop=k == DK - 1)
                    last.then_inc(p1_psum, 1)
            pe.wait_ge(ae_free, NT + GRP)
            carry_tensor(nc, K, pe, L, c)

        @block.vector
        def _(v):
            own = K.own_v
            own.eng = v
            own.link(nc.vector.memset(K.zeros[:], 0.0))
            own.link(nc.vector.memset(K.G[:, RING - 1, :], 0.0))
            v.wait_ge(loaded_m, 16 * len(loads))
            for which in range(2):
                for w, n, p in [(wqk[:, k, which * D:(which + 1) * D], k, 128) for k in range(DK)] + [(rowqkv[:, which * D:(which + 1) * D], 2, 1)]:
                    own.link(nc.vector.tensor_reduce(K.nrm[:p, 4:5], w, AX, ALU.add))
                    own.link(nc.vector.tensor_scalar(K.nrm[:p, 5:6], K.nrm[:p, 4:5], -1.0 / D, None, ALU.mult))
                    own.link(nc.vector.tensor_scalar(w, w, K.nrm[:p, 5:6], None, ALU.add))
            v.sem_inc(centred, 1)
            gather_fold(nc, K, v, L, 0, RING, True)
            with v.Fori(1, 12) as i:
                gather_fold(nc, K, v, L, i, RING, False)
            v.wait_ge(roots, 1)
            own.link(nc.vector.tensor_scalar(K.kscale[:P], K.k2sum[:P], 1e-7, None, ALU.add))
            nc.vector.reciprocal(K.kscale[:P], K.kscale[:P]).then_inc(r_ready, 1)
            own.link(nc.vector.tensor_scalar(K.q2sum[:P], K.q2sum[:P], 1e-7, None, ALU.add))
            own.link(nc.vector.reciprocal(K.q2sum[:P], K.q2sum[:P]))
            own.link(nc.vector.tensor_tensor(K.t1[:P], K.std[:P], K.q2sum[:P], ALU.mult))
            own.link(nc.vector.tensor_scalar(K.t1[:P], K.t1[:P], 1e-12, None, ALU.max))
            own.link(nc.vector.reciprocal(K.t1[:P], K.t1[:P]))
            own.link(nc.vector.scalar_tensor_tensor(K.qscale[:P], K.q2sum[:P], N ** -0.5, K.t1[:P], ALU.mult, ALU.mult))
            with v.Fori(12, BESIDE) as i:
                gather_fold(nc, K, v, L, i, RING, False)
            v.wait_ge(kv_done, 1)
            nc.vector.tensor_copy(kvT.rearrange("p k n -> p (k n)"), PS[:, 5, :]).then_inc(kv_copied, 1)
            nc.vector.tensor_copy(K.nrm[:, 0:2], PS[:, 6, 0:2]).then_inc(kv_copied, 1)
            v.wait_ge(norm_root, 1)
            own.link(nc.vector.tensor_scalar(K.nrm[:, 2:4], K.nrm[:, 2:4], 1e-12, None, ALU.max))
            own.link(nc.vector.reciprocal(K.nrm[:, 2:4], K.nrm[:, 2:4]))
            v.wait_ge(kvw_psum, 1)
            for k in range(DK):
                own.link(nc.vector.tensor_scalar(KVW[:, k, :], PS[:, 7, k * D:(k + 1) * D], K.nrm[:, 2 + k:3 + k], None, ALU.mult))
                own.link(nc.vector.tensor_copy(wE[:, k, 0:D], K.wtheta[:, k, :]))
                own.link(nc.vector.tensor_copy(wE[:, k, D:2 * D], PS[:, 3, k * D:(k + 1) * D]))
            own.link(nc.vector.tensor_tensor(K.rowE[:, 0:D], rowb[:, 0:D], rowb[:, D:2 * D], ALU.add))
            own.link(nc.vector.tensor_tensor(K.rowE[:, D:2 * D], PS[0:1, 4, 0:D], rowo, ALU.add))
            v.sem_inc(end_weights, 1)
            v.sem_inc(p1_free, GRP)
            with v.Fori(0, NG) as g:
                def constant_part(s):
                    u, X = s // 3, K.X[:P]
                    if s % 3 == 0 and u < GRP:
                        t = g * GRP + u
                        v.wait_ge(ae_psum, t + 1)
                        nc.vector.tensor_tensor(tile_of(X, t), tile_of(X, t), PS[:P, u, D:2 * D], ALU.add).then_inc(mix_added, 1)

                def attention_part(s):
                    u, X = s // 3, K.X[:P]
                    if s % 3 == 0 and u < GRP:
                        t = g * GRP + u
                        v.wait_ge(p1_psum, t + 1)
                        v.wait_ge(mix_added, t + 1)
                        nc.vector.scalar_tensor_tensor(tile_of(X, t), PS[:P, 5 + u % 3, 0:D], col(K.qscale, t), tile_of(X, t),
                                                       ALU.mult, ALU.add).then_inc(p1_free, 1)
                gather_fold(nc, K, v, L, g * 2 + BESIDE, RING, False, constant_part)
                gather_fold(nc, K, v, L, g * 2 + BESIDE + 1, RING, False, attention_part)
            with v.Fori(BESIDE + 2 * NG, ROUNDS) as i:
                gather_fold(nc, K, v, L, i, RING, False)
            gather_fold(nc, K, v, L, ROUNDS, TAIL, False)
            carry_vector(nc, K, v, own, L, c)
    for s in range(RING):
        K.landed_total[s] += 16 * (ROUNDS + (s < TAIL) + 2 * (s == FIX))


def gather_ends(nc, K, pool, m_used):
    for t in range(NT):
        u = t % GRP
        if t >= GRP:
            pool.wait_ge(m_used, t - GRP + 1)
        nc.gpsimd.indirect_dma_start(K.G[:NODE_P, u, :], None, K.hist,
                                     bass.IndirectOffsetOnAxis(ap=K.end_i[:NODE_P, t:t + 1], axis=0)
                                     ).then_inc(K.landed[u], 16)


def ends_taken(K):
    for s in range(GRP):
        K.landed_total[s] += 16 * NG


def tile_of(buf, t):
    return buf[:, bass.ds(t, 1), :].rearrange("p a d -> p (a d)")


def col(buf, t):
    return buf[:NODE_P, bass.ds(t, 1)]


def ends0(nc, K, sem):
    m_used, summed = sem("e0_m_used"), sem("e0_summed")
    P, G, X = NODE_P, K.G, K.X[:NODE_P]
    base = list(K.landed_total)
    with nc.Block() as block:
        @block.gpsimd
        def _(pool):
            gather_ends(nc, K, pool, m_used)

        @block.vector
        def _(v):
            own = K.own_v
            own.eng = v
            with v.Fori(0, NG) as g:
                own.loop(g, 0, GRP)
                for u in range(GRP):
                    t = g * GRP + u
                    hold(v, K, K.landed[u], g * 16 + 16 + base[u])
                    nc.vector.tensor_tensor(K.xs[:P, u], G[:P, u, :], tile_of(K.dst_part, t), ALU.add).then_inc(m_used, 1)
                for u in range(GRP):
                    t = g * GRP + u
                    hold(v, K, m_used, t + 1)
                    nc.vector.scalar_tensor_tensor(tile_of(X, t), K.xs[:P, u], 0.0, tile_of(X, t), ALU.max, ALU.add).then_inc(summed, 1)
                for u in range(GRP):
                    t = g * GRP + u
                    hold(v, K, summed, t + 1)
                    own.step(nc.vector.bn_stats(K.S[:P, bass.ds(t, 1), :], tile_of(X, t)))
            own.left(NG)
            own.settle()
    ends_taken(K)


def transposes(K, nc, pe, g, ready, xt_psum, xt_free, ring):
    for u in range(GRP):
        pe.wait_ge(ready, g * GRP + u + 1)
        pe.wait_ge(xt_free, free(g, u, ring))
        for k in range(DK):
            last = nc.tensor.transpose(K.PS[:, u % ring, k * NODE_P:(k + 1) * NODE_P], K.xs[:NODE_P, u, k * 128:(k + 1) * 128],
                                       K.ident[:NODE_P, :NODE_P])
        last.then_inc(xt_psum, 1)


def normalise(K, nc, v, g, xt_free, xs_ready):
    for u in range(GRP):
        t = g * GRP + u
        hold(v, K, xt_free, t + 1)
        nc.vector.tensor_scalar(K.xs[:NODE_P, u], tile_of(K.X[:NODE_P], t), col(K.rstd, t), col(K.nmr, t),
                                ALU.mult, ALU.add).then_inc(xs_ready, 1)


def add_normed_scalar(nc, K, act, a, stats_ready, normed):
    act.wait_ge(stats_ready, 1)
    with act.Fori(0, NT) as t:
        nc.scalar.activation(tile_of(a, t), tile_of(a, t), ACT.Identity, scale=col(K.rstd, t), bias=col(K.nmr, t)).then_inc(normed, 1)


def add_normed_vector(nc, K, v, own, a, gamma, normed):
    P, X = NODE_P, K.X[:NODE_P]
    gamma_group = gamma[:P].unsqueeze(1).broadcast_to([P, GRP, D])
    with v.Fori(0, NG) as g:
        own.loop(g, 0, 2 + GRP)
        tiles = bass.ds(g * GRP, GRP)
        hold(v, K, normed, g * GRP + GRP)
        own.step(nc.vector.tensor_tensor(a[:, tiles, :], a[:, tiles, :], gamma_group, ALU.mult))
        hold(v, K, own.sem, own.done)
        own.step(nc.vector.tensor_tensor(X[:, tiles, :], X[:, tiles, :], a[:, tiles, :], ALU.add))
        hold(v, K, own.sem, own.done)
        for u in range(GRP):
            own.step(nc.vector.bn_stats(K.S[:P, bass.ds(g * GRP + u, 1), :], tile_of(X, g * GRP + u)))
    own.left(NG)
    own.settle()


def experts0(nc, K, sem):
    names = """loaded asks gives xs_ready xt_psum xt_free mean_ready logits_psum exp_asks exp_gives index_ready weights_ready
               h_psum h_ready y_psum y_free asks2 gives2 stats_ready normed loaded_next comp_psum""".split()
    (loaded, asks, gives, xs_ready, xt_psum, xt_free, mean_ready, logits_psum, exp_asks, exp_gives, index_ready, weights_ready,
     h_psum, h_ready, y_psum, y_free, asks2, gives2, stats_ready, normed, loaded_next, comp_psum) = (sem("f0_" + n) for n in names)
    P, PS, A, XT = NODE_P, K.PS, K.arena, K.XT
    at = 0

    def piece(n):
        nonlocal at
        at += n
        return A[:, at - n:at]
    a = piece(NT * D)[:P].rearrange("p (t d) -> p t d", d=D)
    W1 = [piece(DK * F).rearrange("p (k f) -> p k f", k=DK) for _ in range(2)]
    W2 = [piece(FK * D).rearrange("p (f d) -> p f d", f=FK) for _ in range(2)]
    b1 = [piece(FK) for _ in range(2)]
    b2 = [piece(D)[:P] for _ in range(2)]
    HR = 5
    hs = [piece(FK * P).rearrange("p (f n) -> p f n", f=FK) for _ in range(HR)]
    gb = piece(2 * D)
    wr = piece(DK * E8).rearrange("p (k e) -> p k e", k=DK)
    br = piece(E8)[0:1, :]
    spread = piece(DK * 128).rearrange("p (k n) -> p k n", k=DK)
    means = piece(DK * NT).rearrange("p (k t) -> p k t", k=DK)
    mean = piece(DK)
    lg, ex, top = piece(E8), piece(E8), piece(E8)
    m1, m2, m3 = piece(1), piece(1), piece(1)
    wts = piece(2)
    topi = piece(E8).bitcast(U32)
    ef, ix = piece(2), piece(2)
    rowi, expi = piece(2).bitcast(I32), piece(2).bitcast(I32)
    partf = piece(1)
    K.relW = A[:, ARENA - DK * E8 * D:ARENA].rearrange("p (k n) -> p k n", k=DK)
    assert at <= ARENA - DK * E8 * D
    IC = STEPS + RING - TAIL
    Gf = K.G[:].rearrange("p s d -> p (s d)")
    basis = Gf[:, 0:4 * DK * D].rearrange("p (b k n) -> p b k n", b=4, k=DK)
    K.srcf = srcf = Gf[:, 4 * DK * D:4 * DK * D + IC]
    comp, comp_row = Gf[:, 4 * DK * D + IC:4 * DK * D + IC + 32], Gf[0:1, 4 * DK * D + IC + 32:4 * DK * D + IC + 64]
    typf = K.ys[:].rearrange("p s d -> p (s d)")[:, 0:IC]
    ins = K.ins
    loads_next = [(basis[:, b], ins["basis"][b * D:(b + 1) * D, :].rearrange("(k p) n -> p k n", p=128)) for b in range(4)]
    loads_next += [(comp_row, ins["comp"]), (srcf.bitcast(I32), ins["src"]), (typf.bitcast(I32), ins["etype"])]
    loads = [(gb, ins["gamma_beta0"].broadcast_to([128, 2 * D])), (wr, ins["ffn0_Wr"].rearrange("(k p) e -> p k e", p=128)),
             (br, ins["ffn0_br"])]
    base = list(K.landed_total)
    CAP = -(-N * 5 // (4 * E8))
    with nc.Block() as block:
        @block.sync
        def _(sp):
            for dst, src in loads:
                sp.dma_start(dst, src).then_inc(loaded, 16)
            for dst, src in loads_next:
                sp.dma_start(dst, src).then_inc(loaded_next, 16)

        @block.gpsimd
        def _(pool):
            pool.wait_ge(index_ready, 1)
            s = 0
            for e in range(2):
                for dst, table, index, parts in ((W1[e].rearrange("p k f -> p (k f)"), ins["ffn0_W1"], rowi, 128),
                                                 (W2[e].rearrange("p f d -> p (f d)"), ins["ffn0_W2"], rowi, 128),
                                                 (b1[e], ins["ffn0_b1"], rowi, 128), (b2[e], ins["ffn0_b2"], expi, P)):
                    nc.gpsimd.indirect_dma_start(dst, None, table, bass.IndirectOffsetOnAxis(ap=index[:parts, e:e + 1], axis=0)
                                                 ).then_inc(K.landed[s], 16)
                    s += 1

        @block.scalar
        def _(act):
            act.wait_ge(asks, 1)
            nc.scalar.activation(K.std[:P], K.t3[:P], ACT.Sqrt).then_inc(gives, 1)
            act.sem_inc(xt_free, GRP)
            with act.Fori(0, NG) as g:
                for u in range(GRP):
                    t = g * GRP + u
                    hold(act, K, xt_psum, t + 1)
                    for k in range(DK):
                        last = nc.scalar.activation(XT[:, k, bass.ds(t * P, P)], PS[:, u % 4, k * P:(k + 1) * P], ACT.Copy,
                                                    accum_out=means[:, k, bass.ds(t, 1)])
                    last.then_inc(xt_free, 1)
            for n in range(3):
                act.wait_ge(exp_asks, n + 1)
                src, dst = ((lg, ex), (lg, ex), (m2, m3))[n]
                nc.scalar.activation(dst, src, ACT.Exp).then_inc(exp_gives, 1)
            act.wait_ge(weights_ready, 1)
            with act.Fori(0, NG) as g:
                for u in range(GRP):
                    for e in range(2):
                        j = 2 * u + e
                        act.wait_ge(h_psum, g * (2 * GRP) + j + 1)
                        act.wait_ge(y_free, g * GRP + u + GRP - 1)
                        for f in range(FK):
                            last = nc.scalar.activation(hs[j % HR][:, f, :], PS[:, j % HR, f * P:(f + 1) * P], ACT.Gelu,
                                                        bias=b1[e][:, f:f + 1])
                        last.then_inc(h_ready, 1)
            act.wait_ge(asks2, 1)
            nc.scalar.activation(K.std[:P], K.t3[:P], ACT.Sqrt).then_inc(gives2, 1)
            add_normed_scalar(nc, K, act, a, stats_ready, normed)

        @block.tensor
        def _(pe):
            pe.wait_ge(loaded, 16 * len(loads))
            with pe.Fori(0, NG) as g:
                transposes(K, nc, pe, g, xs_ready, xt_psum, xt_free, 4)
            pe.wait_ge(loaded_next, 16 * len(loads_next))
            nc.tensor.matmul(PS[:, 5, 0:32], K.ones[0:1, :], comp_row, start=True, stop=True).then_inc(comp_psum, 1)
            pe.wait_ge(mean_ready, 1)
            for k in range(DK):
                nc.tensor.matmul(PS[:, 6, 0:E8], spread[:, k, :], wr[:, k, :], start=k == 0, stop=False)
            nc.tensor.matmul(PS[:, 6, 0:E8], K.ones[0:1, :], br, start=False, stop=True).then_inc(logits_psum, 1)
            pe.wait_ge(weights_ready, 1)

            def hidden(g, u):
                for e in range(2):
                    j = 2 * u + e
                    pe.wait_ge(h_ready, g * (2 * GRP) + j + 1)
                    for f in range(FK):
                        for k in range(DK):
                            last = nc.tensor.matmul(PS[:, j % HR, f * P:(f + 1) * P], W1[e][:, k, f * 128:(f + 1) * 128],
                                                    XT[:, k, bass.ds((g * GRP + u) * P, P)], start=k == 0, stop=k == DK - 1)
                    last.then_inc(h_psum, 1)

            def output(g, u):
                pe.wait_ge(h_ready, g * (2 * GRP) + 2 * u + 2 + HR)
                pe.wait_ge(y_free, free(g, u, 3))
                for e in range(2):
                    for f in range(FK):
                        last = nc.tensor.matmul(PS[:P, 5 + u % 3, 0:D], hs[(2 * u + e) % HR][:, f, :], W2[e][:, f, :],
                                                start=e == 0 and f == 0, stop=e == 1 and f == FK - 1)
                last.then_inc(y_psum, 1)
            pe.sem_inc(h_ready, HR)
            with pe.Fori(0, NG) as g:
                for u in range(GRP):
                    hidden(g, u)
                    if u:
                        output(g, u - 1)
                output(g, GRP - 1)

        @block.vector
        def _(v):
            own = K.own_v
            own.eng = v
            link = own.link
            norm_stats(nc, K, v, own, asks, gives)
            link(nc.vector.tensor_copy(partf, K.parti[:]))
            with v.Fori(0, NG) as g:
                normalise(K, nc, v, g, xt_free, xs_ready)
            v.wait_ge(xt_free, NT + GRP)
            link(nc.vector.tensor_reduce(mean, means, AX, ALU.add))
            link(nc.vector.tensor_scalar(mean, mean, 1.0 / N, None, ALU.mult))
            for k in range(DK):
                link(nc.vector.tensor_scalar(spread[:, k, :], K.ones[:], mean[:, k:k + 1], None, ALU.mult))
            v.wait_ge(comp_psum, 1)
            link(nc.vector.tensor_copy(comp, PS[:, 5, 0:32]))
            v.sem_inc(mean_ready, 1)
            v.wait_ge(logits_psum, 1)

            def softmax(n, src):
                link(nc.vector.tensor_reduce(m1, src, AX, ALU.max))
                link(nc.vector.tensor_scalar(lg, src, m1, None, ALU.subtract))
                v.sem_inc(exp_asks, 1)
                v.wait_ge(exp_gives, n)
                link(nc.vector.tensor_reduce(m1, ex, AX, ALU.add))
                link(nc.vector.reciprocal(m1, m1))
                link(nc.vector.tensor_scalar(ex, ex, m1, None, ALU.mult))
            softmax(1, PS[:, 6, 0:E8])
            link(nc.vector.tensor_scalar(top, ex, float(N), None, ALU.mult))
            link(nc.vector.reciprocal(top, top))
            link(nc.vector.tensor_scalar(top, top, float(CAP), 1.0, ALU.mult, ALU.min))
            link(nc.vector.tensor_tensor(lg, ex, top, ALU.mult))
            softmax(2, lg)
            link(nc.vector.max(top, ex))
            link(nc.vector.max_index(topi, top, ex))
            link(nc.vector.tensor_copy(ef, topi[:, 0:2]))
            link(nc.vector.tensor_copy(expi, ef))
            link(nc.vector.tensor_scalar(ix, ef, 128.0, partf, ALU.mult, ALU.add))
            link(nc.vector.tensor_copy(rowi, ix))
            v.sem_inc(index_ready, 1)
            link(nc.vector.tensor_tensor(m2, top[:, 1:2], top[:, 0:1], ALU.subtract))
            v.sem_inc(exp_asks, 1)
            v.wait_ge(exp_gives, 3)
            link(nc.vector.tensor_scalar(m1, m3, 1.0, None, ALU.add))
            link(nc.vector.reciprocal(wts[:, 0:1], m1))
            link(nc.vector.tensor_tensor(wts[:, 1:2], wts[:, 0:1], m3, ALU.mult))
            for s in range(8):
                v.wait_ge(K.landed[s], base[s] + 16)
            for e in range(2):
                link(nc.vector.tensor_scalar(W2[e], W2[e], wts[:, e:e + 1], None, ALU.mult))
                link(nc.vector.tensor_scalar(b2[e], b2[e], wts[:P, e:e + 1], None, ALU.mult))
            link(nc.vector.tensor_tensor(b2[0], b2[0], b2[1], ALU.add))
            v.sem_inc(weights_ready, 1)
            v.sem_inc(y_free, GRP)
            for b in range(4):
                for r in range(E8):
                    w, f = K.relW[:, :, r * D:(r + 1) * D], comp[:, r * 4 + b:r * 4 + b + 1]
                    if b == 0:
                        own.step(nc.vector.tensor_scalar(w, basis[:, b], f, None, ALU.mult))
                    else:
                        own.step(nc.vector.scalar_tensor_tensor(w, basis[:, b], f, w, ALU.mult, ALU.add))
                own.settle()
            v.wait_ge(loaded_next, 16 * len(loads_next))
            link(nc.vector.tensor_copy(srcf, srcf.bitcast(I32)))
            link(nc.vector.tensor_copy(typf, typf.bitcast(I32)))
            link(nc.vector.scalar_tensor_tensor(srcf, srcf, float(E8), typf, ALU.mult, ALU.add))
            link(nc.vector.tensor_copy(srcf.bitcast(I32), srcf))
            group_rows = lambda r: r.unsqueeze(1).broadcast_to([P, GRP, D])
            with v.Fori(0, NG) as g:
                own.loop(g, 0, 2 * GRP + 2)
                mark = [0] * GRP
                tiles = bass.ds(g * GRP, GRP)
                for u in range(GRP):
                    t = g * GRP + u
                    own.step(nc.vector.tensor_scalar(tile_of(a, t), tile_of(K.X[:P], t), col(K.rstd, t), col(K.nmr, t), ALU.mult, ALU.add))
                hold(v, K, own.sem, own.done)
                own.step(nc.vector.tensor_tensor(a[:, tiles, :], a[:, tiles, :], group_rows(b2[0]), ALU.add))
                own.step(nc.vector.tensor_tensor(K.X[:P, tiles, :], K.X[:P, tiles, :], group_rows(gb[:P, D:2 * D]), ALU.add))
                for u in range(GRP):
                    t = g * GRP + u
                    hold(v, K, own.sem, own.done)
                    hold(v, K, y_psum, t + 1)
                    nc.vector.tensor_tensor(tile_of(a, t), tile_of(a, t), PS[:P, 5 + u % 3, 0:D], ALU.add).then_inc(y_free, 1)
                for u in range(GRP):
                    t = g * GRP + u
                    hold(v, K, y_free, t + 1 + GRP)
                    own.step(nc.vector.bn_stats(K.S[:P, bass.ds(t, 1), :], tile_of(a, t)))
            own.left(NG)
            own.settle()
            norm_stats(nc, K, v, own, asks2, gives2)
            v.sem_inc(stats_ready, 1)
            add_normed_vector(nc, K, v, own, a, gb[:, 0:D], normed)
    for s in range(8):
        K.landed_total[s] += 16


def relations(nc, K, sem):
    names = "asks gives xs_ready xt_psum xt_free x_staged act_free dve_free act_full index_stored staged_free".split()
    (asks, gives, xs_ready, xt_psum, xt_free, x_staged, act_free, dve_free, act_full, index_stored, staged_free) = (
        sem("r_" + n) for n in names)
    chunk_psum = [sem(f"r_chunk_psum{c}") for c in range(4)]
    stored = [sem(f"r_stored{u}") for u in range(GRP)]
    P, PS, A, XT = NODE_P, K.PS, K.arena, K.XT
    RW = E8 * D
    W = K.relW
    H = A[:P, 0:GRP * RW].rearrange("p (s n) -> p s n", s=GRP)
    assert GRP * RW <= ARENA - DK * RW
    with nc.Block() as block:
        @block.sync
        def _(sp):
            sp.dma_start(K.slots.rearrange("(j p) d -> p j d", p=BLOCK), K.zeros[:].unsqueeze(1).broadcast_to([BLOCK, SLOT_BLOCKS, D])
                         ).then_inc(K.slots_zeroed, 16)
            sp.dma_start(K.index1, K.srcf.bitcast(I32)).then_inc(index_stored, 16)
            with sp.Fori(0, NG) as g:
                for u in range(GRP):
                    t = g * GRP + u
                    sp.wait_ge(act_full, t + 1)
                    sp.wait_ge(dve_free, 1 + t)
                    sp.dma_start(K.htab.rearrange("(p t r) d -> p t (r d)", t=NT, r=E8)[:, bass.ds(t, 1), :].rearrange("p a n -> p (a n)"),
                                 H[:, u, :]).then_inc(stored[u], 16)
            for u in range(GRP):
                sp.wait_ge(stored[u], 16 * NG)
            sp.wait_ge(index_stored, 16)

        @block.scalar
        def _(act):
            act.wait_ge(asks, 1)
            nc.scalar.activation(K.std[:P], K.t3[:P], ACT.Sqrt).then_inc(gives, 1)
            act.sem_inc(xt_free, GRP)

            def group(g, first):
                for u in range(GRP):
                    t = g * GRP + u
                    hold(act, K, xt_psum, t + 1)
                    pt = PS[:, u % 2, 0:DK * P].rearrange("p (k n) -> p k n", k=DK)
                    nc.scalar.copy(K.xTs[:, u], pt).then_inc(x_staged, 1)
                    nc.scalar.copy(XT[:, :, bass.ds(t * P, P)], pt).then_inc(xt_free, 1)
                for u in range(GRP):
                    t = g * GRP + u
                    if not first:
                        act.wait_ge(stored[u], g * 16)
                    for c in range(2):
                        act.wait_ge(chunk_psum[c], t + 1)
                        last = nc.scalar.copy(H[:, u, c * 512:(c + 1) * 512], PS[:P, 2 + c, :])
                        last.then_inc(act_free if c == 0 else act_full, 1)
            group(0, True)
            with act.Fori(1, NG) as g:
                group(g, False)

        @block.tensor
        def _(pe):
            def group(g, first):
                transposes(K, nc, pe, g, xs_ready, xt_psum, xt_free, 2)
                for u in range(GRP):
                    t = g * GRP + u
                    pe.wait_ge(x_staged, t + 1)
                    for c in range(4):
                        if not (first and u == 0):
                            pe.wait_ge((act_free, act_full, staged_free, dve_free)[c], t)
                        for k in range(DK):
                            last = nc.tensor.matmul(PS[:P, 2 + c, :], K.xTs[:, u, k, :], W[:, k, c * 512:(c + 1) * 512], start=k == 0, stop=k == DK - 1)
                        last.then_inc(chunk_psum[c], 1)
            group(0, True)
            with pe.Fori(1, NG) as g:
                group(g, False)

        @block.vector
        def _(v):
            own = K.own_v
            own.eng = v
            norm_stats(nc, K, v, own, asks, gives)

            def group(g, first):
                normalise(K, nc, v, g, xt_free, xs_ready)
                for u in range(GRP):
                    t = g * GRP + u
                    if not first:
                        v.wait_ge(stored[u], g * 16)
                    for c in (2, 3):
                        v.wait_ge(chunk_psum[c], t + 1)
                        nc.vector.tensor_copy(H[:, u, c * 512:(c + 1) * 512], PS[:P, 2 + c, :]).then_inc(staged_free if c == 2 else dve_free, 1)
            group(0, True)
            with v.Fori(1, NG) as g:
                group(g, False)


def gather1_mix1(nc, K, sem):
    L = K.pass1 = Pass(K, sem, "sum", K.htab, K.index1, K.keep, ALU.mult, ALU.add, K.lane_keep, 0.0)
    names = """loaded x_staged kq_psum kq_free v_psum v_free kq_done max_ready exp_ready kT_psum kT_free acc_free ctx_done
               ctx_ready ctxT_psum ctxT_ready w_psum end_weights q_staged ae_psum ae_free mix_added""".split()
    (loaded, x_staged, kq_psum, kq_free, v_psum, v_free, kq_done, max_ready, exp_ready, kT_psum, kT_free, acc_free, ctx_done,
     ctx_ready, ctxT_psum, ctxT_ready, w_psum, end_weights, q_staged, ae_psum, ae_free, mix_added) = (
        sem("m1_" + n) for n in names)
    c = carry_names(sem, "c1_")
    P, PS, A, XT = NODE_P, K.PS, K.arena, K.XT
    HEADS, HD = 4, 32
    at = 0

    def piece(n):
        nonlocal at
        at += n
        return A[:, at - n:at]
    KQ = piece(2 * N).rearrange("p (a n) -> p a n", a=2)
    V = piece(NT * 128)[:P].rearrange("p (t e) -> p t e", e=128)
    wqkv = piece(DK * 384).rearrange("p (k n) -> p k n", k=DK)
    wout, Wmix, ctx, ctxT, mask = piece(D), piece(D), piece(128), piece(128), piece(128)
    Wloop = piece(DK * D).rearrange("p (k n) -> p k n", k=DK)
    row1, beta_row = piece(2 * D)[0:1, :], piece(D)[0:1, :]
    K.trail = piece(DK * (1 + LANES)).rearrange("p (k n) -> p k n", k=DK)
    kmax, ksum, kfac = piece(1), piece(NT), piece(1)
    K.own_part = piece(NT * D)[:P].rearrange("p (t d) -> p t d", d=D)
    assert at <= ARENA
    ins = K.ins
    loads = [(wqkv, ins["mix1_qkv"].rearrange("(k p) n -> p k n", p=128)), (wout, ins["mix1_out"]),
             (Wloop, ins["loop_w"].rearrange("(k p) n -> p k n", p=128)), (row1[:, 0:D], ins["h_bias"]),
             (row1[:, D:2 * D], ins["mix1_bout"]), (beta_row, ins["gamma_beta1"][:, D:2 * D])]
    with nc.Block() as block:
        @block.sync
        def _(sp):
            for dst, src in loads:
                sp.dma_start(dst, src).then_inc(loaded, 16)
            gather_sync(nc, K, sp, L)
            carry_sync(nc, K, sp, L, c)

        @block.gpsimd
        def _(pool):
            gather_pool(nc, K, pool, L)
            carry_pool(nc, K, pool, L, c)

        @block.scalar
        def _(act):
            act.sem_inc(kq_free, GRP)
            act.sem_inc(v_free, GRP)
            act.sem_inc(kT_free, GRP)
            with act.Fori(0, NG) as g:
                for u in range(GRP):
                    nc.scalar.copy(K.xTs[:, u], XT[:, :, bass.ds((g * GRP + u) * P, P)]).then_inc(x_staged, 1)
                for u in range(GRP):
                    t = g * GRP + u
                    hold(act, K, kq_psum, t + 1)
                    nc.scalar.copy(KQ[:, :, bass.ds(t * P, P)], PS[:, u, 0:2 * P].rearrange("p (a n) -> p a n", a=2)).then_inc(kq_free, 1)
                    hold(act, K, v_psum, t + 1)
                    nc.scalar.copy(tile_of(V, t), PS[:P, 5 + u % 3, 0:128]).then_inc(v_free, 1)
            act.wait_ge(max_ready, 1)
            with act.Fori(0, NG) as g:
                for u in range(GRP):
                    t = g * GRP + u
                    hold(act, K, kT_free, t + 1)
                    nc.scalar.activation(K.ys[:, u, 0:P], KQ[:, 1, bass.ds(t * P, P)], ACT.Exp, bias=kmax,
                                         accum_out=ksum[:, bass.ds(t, 1)]).then_inc(exp_ready, 1)
                for u in range(GRP):
                    t = g * GRP + u
                    act.wait_ge(kT_psum, t + 1)
                    act.wait_ge(acc_free, t + 1)
                    nc.scalar.copy(K.xs[:P, u, 0:128], PS[:P, u % 3, 0:128]).then_inc(kT_free, 1)
            act.sem_inc(ae_free, GRP)
            with act.Fori(0, NG) as g:
                for u in range(GRP):
                    t = g * GRP + u
                    hold(act, K, ae_free, t + 1)
                    nc.scalar.copy(K.xTs[:, u], XT[:, :, bass.ds(t * P, P)]).then_inc(x_staged, 1)
                    nc.scalar.copy(K.ys[:, u, 128:128 + P], KQ[:, 0, bass.ds(t * P, P)]).then_inc(q_staged, 1)
                for u in range(GRP):
                    t = g * GRP + u
                    hold(act, K, mix_added, t + 1)
                    nc.scalar.copy(tile_of(K.own_part, t), PS[:P, u, 0:D]).then_inc(ae_free, 1)

        @block.tensor
        def _(pe):
            pe.wait_ge(loaded, 16 * len(loads))
            with pe.Fori(0, NG) as g:
                for u in range(GRP):
                    t = g * GRP + u
                    pe.wait_ge(x_staged, t + 1)
                    pe.wait_ge(kq_free, t + 1)
                    for a in range(2):
                        for k in range(DK):
                            last = nc.tensor.matmul(PS[:, u, a * P:(a + 1) * P], wqkv[:, k, a * 128:(a + 1) * 128],
                                                    K.xTs[:, u, k, :], start=k == 0, stop=k == DK - 1)
                    last.then_inc(kq_psum, 1)
                    pe.wait_ge(v_free, free(g, u, 3))
                    for k in range(DK):
                        last = nc.tensor.matmul(PS[:P, 5 + u % 3, 0:128], K.xTs[:, u, k, :], wqkv[:, k, 256:384], start=k == 0, stop=k == DK - 1)
                    last.then_inc(v_psum, 1)
            pe.wait_ge(kq_free, NT + GRP)
            pe.sem_inc(acc_free, GRP)
            nc.tensor.matmul(PS[:, 4, 0:128], K.zeros[:, 0:128], K.ones[:], start=True, stop=False)
            with pe.Fori(0, NG) as g:
                for u in range(GRP):
                    t = g * GRP + u
                    pe.wait_ge(exp_ready, t + 1)
                    pe.wait_ge(kT_free, free(g, u, 3))
                    nc.tensor.transpose(PS[:P, u % 3, 0:128], K.ys[:, u, 0:P], K.ident[:]).then_inc(kT_psum, 1)
                for u in range(GRP):
                    t = g * GRP + u
                    pe.wait_ge(kT_free, t + 1 + GRP)
                    nc.tensor.matmul(PS[:, 4, 0:128], K.xs[:P, u, 0:128], tile_of(V, t), start=False, stop=False).then_inc(acc_free, 1)
            nc.tensor.matmul(PS[:, 4, 0:128], K.zeros[:, 0:128], K.ones[:], start=False, stop=True).then_inc(ctx_done, 1)
            pe.wait_ge(ctx_ready, 1)
            nc.tensor.transpose(PS[:, 5, 0:128], ctx, K.ident[:]).then_inc(ctxT_psum, 1)
            pe.wait_ge(ctxT_ready, 1)
            nc.tensor.matmul(PS[:, 6, 0:D], ctxT, wout, start=True, stop=True).then_inc(w_psum, 1)
            pe.wait_ge(end_weights, 1)
            with pe.Fori(0, NG) as g:
                for u in range(GRP):
                    t = g * GRP + u
                    pe.wait_ge(ae_free, t + 1)
                    nc.tensor.matmul(PS[:P, u, :], K.ones[0:1, 0:P], row1, start=True, stop=False)
                    pe.wait_ge(x_staged, t + 1 + NT)
                    for k in range(DK):
                        nc.tensor.matmul(PS[:P, u, 0:D], K.xTs[:, u, k, :], Wloop[:, k, :], start=False, stop=False)
                    pe.wait_ge(q_staged, t + 1)
                    nc.tensor.matmul(PS[:P, u, D:2 * D], K.ys[:, u, 128:128 + P], Wmix, start=False, stop=True).then_inc(ae_psum, 1)
            pe.wait_ge(ae_free, NT + GRP)
            carry_tensor(nc, K, pe, L, c)

        @block.vector
        def _(v):
            own = K.own_v
            own.eng = v
            link = own.link
            link(nc.vector.memset(K.G[:, RING - 1, :], 0.0))
            link(nc.vector.memset(mask, 0.0))
            for h in range(HEADS):
                link(nc.vector.memset(mask[h * HD:(h + 1) * HD, h * HD:(h + 1) * HD], 1.0))
            gather_fold(nc, K, v, L, 0, RING, True)
            with v.Fori(1, 12) as i:
                gather_fold(nc, K, v, L, i, RING, False)
            v.wait_ge(kq_free, NT + GRP)
            link(nc.vector.tensor_reduce(kmax, KQ[:, 1, :], AX, ALU.max))
            nc.vector.tensor_scalar(kmax, kmax, -1.0, None, ALU.mult).then_inc(max_ready, 1)
            with v.Fori(12, BESIDE) as i:
                gather_fold(nc, K, v, L, i, RING, False)
            v.wait_ge(ctx_done, 1)
            nc.vector.tensor_tensor(ctx, PS[:, 4, 0:128], mask, ALU.mult).then_inc(ctx_ready, 1)
            v.wait_ge(kT_free, NT + GRP)
            link(nc.vector.tensor_reduce(kfac, ksum, AX, ALU.add))
            link(nc.vector.reciprocal(kfac, kfac))
            link(nc.vector.tensor_scalar(kfac, kfac, HD ** -0.5, None, ALU.mult))
            v.wait_ge(ctxT_psum, 1)
            nc.vector.tensor_copy(ctxT, PS[:, 5, 0:128]).then_inc(ctxT_ready, 1)
            v.wait_ge(w_psum, 1)
            link(nc.vector.tensor_scalar(Wmix, PS[:, 6, 0:D], kfac, None, ALU.mult))
            for k in range(DK):
                w = Wloop[:, k, k * 128:(k + 1) * 128]
                link(nc.vector.tensor_tensor(w, w, K.ident[:], ALU.add))
            link(nc.vector.tensor_tensor(row1[:, D:2 * D], row1[:, D:2 * D], beta_row, ALU.add))
            v.sem_inc(end_weights, 1)
            with v.Fori(0, NG) as g:
                def mix_part(s):
                    u, X = s // 3, K.X[:P]
                    if s % 3 == 0 and u < GRP:
                        t = g * GRP + u
                        v.wait_ge(ae_psum, t + 1)
                        nc.vector.tensor_tensor(tile_of(X, t), tile_of(X, t), PS[:P, u, D:2 * D], ALU.add).then_inc(mix_added, 1)
                gather_fold(nc, K, v, L, g + BESIDE, RING, False, mix_part)
            with v.Fori(BESIDE + NG, ROUNDS) as i:
                gather_fold(nc, K, v, L, i, RING, False)
            gather_fold(nc, K, v, L, ROUNDS, TAIL, False)
            carry_vector(nc, K, v, own, L, c)
    for s in range(RING):
        K.landed_total[s] += 16 * (ROUNDS + (s < TAIL) + 2 * (s == FIX))


def ends1(nc, K, sem):
    names = "loaded m_used gelu_done asks gives stats_ready normed".split()
    loaded, m_used, gelu_done, asks, gives, stats_ready, normed = (sem("e1_" + n) for n in names)
    P, G, a = NODE_P, K.G, K.own_part
    base = list(K.landed_total)
    gamma = K.wphi[:, 0, :]
    with nc.Block() as block:
        @block.sync
        def _(sp):
            sp.dma_start(gamma, K.ins["gamma_beta1"][:, 0:D].broadcast_to([128, D])).then_inc(loaded, 16)

        @block.gpsimd
        def _(pool):
            gather_ends(nc, K, pool, m_used)

        @block.scalar
        def _(act):
            with act.Fori(0, NG) as g:
                for u in range(GRP):
                    t = g * GRP + u
                    hold(act, K, m_used, t + 1)
                    nc.scalar.activation(tile_of(a, t), K.xs[:P, u], ACT.Gelu).then_inc(gelu_done, 1)
            act.wait_ge(asks, 1)
            nc.scalar.activation(K.std[:P], K.t3[:P], ACT.Sqrt).then_inc(gives, 1)
            add_normed_scalar(nc, K, act, a, stats_ready, normed)

        @block.vector
        def _(v):
            own = K.own_v
            own.eng = v
            v.wait_ge(loaded, 16)
            v.sem_inc(gelu_done, GRP)
            with v.Fori(0, NG) as g:
                own.loop(g, 0, GRP)
                for u in range(GRP):
                    t = g * GRP + u
                    hold(v, K, K.landed[u], g * 16 + 16 + base[u])
                    hold(v, K, gelu_done, t + 1)
                    nc.vector.tensor_tensor(K.xs[:P, u], G[:P, u, :], tile_of(a, t), ALU.add).then_inc(m_used, 1)
                for u in range(GRP):
                    t = g * GRP + u
                    hold(v, K, gelu_done, t + 1 + GRP)
                    own.step(nc.vector.bn_stats(K.S[:P, bass.ds(t, 1), :], tile_of(a, t)))
            own.left(NG)
            own.settle()
            norm_stats(nc, K, v, own, asks, gives)
            v.sem_inc(stats_ready, 1)
            add_normed_vector(nc, K, v, own, a, gamma, normed)
    ends_taken(K)


def experts1(nc, K, sem):
    names = """loaded loaded_big consts asks gives xs_ready xt_psum xt_free x_staged br_psum lg_psum lg_free rows_kept
               exp_asks exp_gives picks_ready prefix_psum slots_ready rowT_psum rowT_ready w1_ready h_psum h_ready y_psum y_out
               first_added out_ready out_stored""".split()
    (loaded, loaded_big, consts, asks, gives, xs_ready, xt_psum, xt_free, x_staged, br_psum, lg_psum, lg_free, rows_kept,
     exp_asks, exp_gives, picks_ready, prefix_psum, slots_ready, rowT_psum, rowT_ready, w1_ready, h_psum, h_ready, y_psum, y_out,
     first_added, out_ready, out_stored) = (sem("f1_" + n) for n in names)
    rows_in = [sem(f"f1_rows_in{u}") for u in range(TURN)]
    stored = [sem(f"f1_stored{u}") for u in range(TURN)]
    P, PS = NODE_P, K.PS

    def pieces(buf):
        at = [0]

        def piece(n):
            at[0] += n
            assert at[0] <= buf.shape[1]
            return buf[:, at[0] - n:at[0]]
        return piece
    per_node = lambda a: a[:P].rearrange("p (t e) -> p t e", e=E8)
    piece = pieces(K.arena)
    W1_WORDS = DK * F + FK
    W1 = piece(E8 * W1_WORDS).rearrange("p (e n) -> p e n", e=E8)
    W2 = piece(E8 * FK * D).rearrange("p (e n) -> p e n", e=E8)
    b2 = piece(E8 * D).rearrange("p (e d) -> p e d", e=E8)
    wr = piece(DK * E8).rearrange("p (k e) -> p k e", k=DK)
    br, brB = piece(E8)[0:1, :], piece(E8)[:P]
    lgs, rank, pick1, pick2 = (per_node(piece(NT * E8)) for _ in range(4))
    block_cmp = piece(SLOT_BLOCKS * E8)[0:1].rearrange("p (j e) -> p j e", e=E8)
    piece = pieces(K.keep)
    PAD = 16
    scan = [piece((PAD + NT) * E8)[:P].rearrange("p (t e) -> p t e", e=E8) for _ in range(2)]
    rowf = piece(128)
    piece = pieces(K.pen)
    before, rowi = piece(128), piece(128).bitcast(I32)
    pos, picked = per_node(piece(NT * E8)), per_node(piece(NT * E8))
    EPAD = 4
    escan = [piece(EPAD + E8)[:P] for _ in range(2)]
    count, base_row, partf = piece(E8)[:P], piece(E8)[:P], piece(1)
    slotf = piece(NT)[:P]
    slot_i = K.ranki[:].rearrange("p t e -> p (t e)")[:P, 0:2 * NT].rearrange("p (k t) -> p k t", k=2)
    expert_f, expert_i = K.lane_pen[0:1, 0:SLOT_BLOCKS], K.edge_rows[0:1, 0, 0:SLOT_BLOCKS].bitcast(I32)
    gamma_beta = K.wphi[:].rearrange("p k n -> p (k n)")
    rows_node = K.XTraw[:P].rearrange("p (t d) -> p t d", d=D)
    ys_node = K.XTraw[:P, 0:2 * GRP * D].rearrange("p (s d) -> p s d", d=D)
    G = K.G[:].rearrange("p s d -> p (s d)")
    w1 = [G[:, s * W1_WORDS:(s + 1) * W1_WORDS] for s in range(2)]
    hs = [G[:, 2 * W1_WORDS + s * F:2 * W1_WORDS + (s + 1) * F] for s in range(2)]
    xT = [K.xTs[:].rearrange("p u k n -> p (u k n)")[:, s * D:(s + 1) * D] for s in range(TURN)]
    m1, m2, mi, ee = K.t1[:P], K.t2[:P], K.t3[:P], K.std[:P]
    scattered = K.landed[RING - 1]
    scattered_base, base = K.landed_total[RING - 1], list(K.landed_total)
    ins = K.ins
    loads = [(wr, ins["ffn1_Wr"].rearrange("(k p) e -> p k e", p=128)), (br, ins["ffn1_br"]),
             (gamma_beta, ins["gamma_beta2"].broadcast_to([128, 2 * D]))]
    big = [(W1[:, :, 0:DK * F], ins["ffn1_W1"].rearrange("(e p) n -> p e n", p=128)),
           (W1[:, :, DK * F:W1_WORDS], ins["ffn1_b1"].rearrange("(e p) n -> p e n", p=128)),
           (W2, ins["ffn1_W2"].rearrange("(e p) n -> p e n", p=128)),
           (b2.rearrange("p e d -> p (e d)"), ins["ffn1_b2"].broadcast_to([128, E8 * D]))]
    spread = lambda c: c.unsqueeze(2).broadcast_to([P, NT, E8])
    spread_rows = lambda r: r.unsqueeze(1).broadcast_to([P, NT, E8])
    spread_group = lambda r: r[:P].unsqueeze(1).broadcast_to([P, GRP, D])
    block_of = lambda table, j: table[bass.ds(j * BLOCK, BLOCK), :]
    TURNS = SLOT_BLOCKS // TURN

    def turns(eng, one, peeled=1):
        for i in range(peeled):
            one(i, i == 0, False)
        with eng.Fori(peeled, TURNS - 1) as i:
            one(i, False, False)
        one(TURNS - 1, False, True)

    with nc.Block() as block:
        @block.sync
        def _(sp):
            for dst, src in loads:
                sp.dma_start(dst, src).then_inc(loaded, 16)
            for dst, src in big:
                sp.dma_start(dst, src).then_inc(loaded_big, 16)
            sp.wait_ge(scattered, scattered_base + 16 * 2 * NT)
            with sp.Fori(0, TURNS) as i:
                for u in range(TURN):
                    sp.wait_ge(xt_psum, NT + GRP - TURN + i * TURN + u + 1)
                    sp.dma_start(K.xs[:, u, :], block_of(K.slots, i * TURN + u)).then_inc(rows_in[u], 16)
            for g in range(NG):
                sp.wait_ge(out_ready, GRP * (g + 1))
                sp.dma_start(K.out3[:, g * GRP:(g + 1) * GRP, :], K.X[:P, g * GRP:(g + 1) * GRP, :]).then_inc(out_stored, 16)
            sp.wait_ge(out_stored, 16 * NG)

        @block.gpsimd
        def _(pool):
            nc.gpsimd.iota(K.ranki[:P], pattern=[[0, NT], [-1, E8]], base=E8, channel_multiplier=0).then_inc(consts, 1)
            nc.gpsimd.iota(rowi, pattern=[[1, 128]], base=0, channel_multiplier=0).then_inc(consts, 1)
            pool.wait_ge(rows_kept, NG + 1)
            pool.wait_ge(K.slots_zeroed, 16)
            for k in range(2):
                pool.wait_ge(slots_ready, k + 1)
                for t in range(NT):
                    nc.gpsimd.indirect_dma_start(K.slots, bass.IndirectOffsetOnAxis(ap=slot_i[:, k, t:t + 1], axis=0),
                                                 rows_node[:, t, :], None).then_inc(scattered, 16)
            with pool.Fori(0, TURNS) as i:
                for u in range(TURN):
                    pool.wait_ge(y_out, i * TURN + u + 1)
                    pool.dma_start(block_of(K.slot_ys, i * TURN + u), K.ys[:, u, :]).then_inc(stored[u], 16)
            for u in range(TURN):
                pool.wait_ge(stored[u], 16 * TURNS)
            for t in range(NT):
                for k in range(2):
                    s = 2 * (t % GRP) + k
                    if t >= GRP:
                        pool.wait_ge(out_ready if k else first_added, t - GRP + 1)
                    nc.gpsimd.indirect_dma_start(ys_node[:, s, :], None, K.slot_ys,
                                                 bass.IndirectOffsetOnAxis(ap=slot_i[:, k, t:t + 1], axis=0)).then_inc(K.landed[s], 16)

        @block.scalar
        def _(act):
            act.wait_ge(asks, 1)
            nc.scalar.activation(K.std[:P], K.t3[:P], ACT.Sqrt).then_inc(gives, 1)
            act.sem_inc(xt_free, GRP)
            with act.Fori(0, NG) as g:
                for u in range(GRP):
                    t = g * GRP + u
                    act.wait_ge(lg_free, t + 1)
                    act.wait_ge(xt_psum, t + 1 + GRP)
                    nc.scalar.copy(K.xTs[:, u].rearrange("p k n -> p (k n)"), PS[:, u % 4, 0:DK * P]).then_inc(xt_free, 1)
                hold(act, K, xs_ready, g + 1)
                nc.scalar.copy(rows_node[:, bass.ds(g * GRP, GRP), :], K.xs[:P]).then_inc(rows_kept, 1)
            act.wait_ge(exp_asks, 1)
            nc.scalar.activation(ee, m2, ACT.Exp).then_inc(exp_gives, 1)
            act.wait_ge(lg_free, NT + GRP)

            def transposed(j, u):
                act.wait_ge(xt_psum, NT + GRP + j + 1)
                nc.scalar.copy(xT[u % TURN], PS[:, u % 2, 0:D]).then_inc(rowT_ready, 1)

            def one(i, first, last):
                for u in range(TURN):
                    j = i * TURN + u
                    if first and u == 0:
                        transposed(0, 0)
                    if not (last and u == TURN - 1):
                        transposed(j + 1, u + 1)
                    act.wait_ge(h_psum, j + 1)
                    if not (first and u < 2):
                        act.wait_ge(y_psum, j - 1)
                    for f in range(FK):
                        last_f = nc.scalar.activation(hs[u % 2][:, f * 128:(f + 1) * 128], PS[:, 2 + u % 2, f * 128:(f + 1) * 128], ACT.Gelu,
                                                      bias=w1[u % 2][:, DK * F + f:DK * F + f + 1])
                    last_f.then_inc(h_ready, 1)
            turns(act, one)

        @block.tensor
        def _(pe):
            pe.wait_ge(loaded, 16 * len(loads))
            nc.tensor.matmul(PS[:, 7, 0:E8], K.ones[0:1, :], br, start=True, stop=True).then_inc(br_psum, 1)
            pe.sem_inc(xt_psum, GRP)
            with pe.Fori(0, NG) as g:
                pe.wait_ge(xs_ready, g + 1)
                for u in range(GRP):
                    pe.wait_ge(xt_free, free(g, u, 4))
                    for k in range(DK):
                        last_k = nc.tensor.transpose(PS[:, u % 4, k * P:(k + 1) * P], K.xs[:P, u, k * 128:(k + 1) * 128], K.ident[:P, :P])
                    last_k.then_inc(xt_psum, 1)
                for u in range(GRP):
                    t = g * GRP + u
                    pe.wait_ge(xt_free, t + 1 + GRP)
                    pe.wait_ge(lg_free, free(g, u, 3))
                    for k in range(DK):
                        last_k = nc.tensor.matmul(PS[:P, 4 + u % 3, 0:E8], K.xTs[:, u, k, :], wr[:, k, :], start=k == 0, stop=k == DK - 1)
                    last_k.then_inc(lg_psum, 1)
            pe.wait_ge(picks_ready, 1)
            nc.tensor.matmul(PS[:P, 7, 0:NT * E8], before[:P, 0:P], picked.rearrange("p t e -> p (t e)"), start=True, stop=True)
            nc.tensor.matmul(PS[:P, 7, NT * E8:2 * NT * E8], K.ones[:P, 0:P], picked.rearrange("p t e -> p (t e)"),
                             start=True, stop=True).then_inc(prefix_psum, 1)
            pe.wait_ge(slots_ready, 3)

            def transposed(i, u):
                s = u % TURN
                pe.wait_ge(rows_in[s], 16 * (i + 1 + u // TURN))
                if i is not None and not (isinstance(i, int) and i * TURN + u < 2):
                    pe.wait_ge(rowT_ready, i * TURN + u - 1)
                for k in range(DK):
                    last_k = nc.tensor.transpose(PS[:, u % 2, k * 128:(k + 1) * 128], K.xs[:, s, k * 128:(k + 1) * 128], K.ident[:])
                last_k.then_inc(xt_psum, 1)

            def output(j, u):
                e = pe.value_load(expert_i[0:1, bass.ds(j, 1)], min_val=0, max_val=E8 - 1)
                pe.wait_ge(h_ready, j + 1)
                if not (isinstance(j, int) and j < 2):
                    pe.wait_ge(y_out, j - 1)
                for f in range(FK):
                    last_f = nc.tensor.matmul(PS[:, 4 + u % 2, 0:D], hs[u % 2][:, f * 128:(f + 1) * 128],
                                              W2[:, bass.ds(e, 1), f * D:(f + 1) * D].rearrange("p a d -> p (a d)"), start=f == 0, stop=f == FK - 1)
                last_f.then_inc(y_psum, 1)

            def one(i, first, last):
                if first:
                    transposed(0, 0)
                for u in range(TURN):
                    j = i * TURN + u
                    if not (last and u == TURN - 1):
                        transposed(i, u + 1)
                    pe.wait_ge(rowT_ready, j + 1)
                    pe.wait_ge(w1_ready, j + 1)
                    if not (first and u < 2):
                        pe.wait_ge(h_ready, j - 1)
                    for f in range(FK):
                        for k in range(DK):
                            last_k = nc.tensor.matmul(PS[:, 2 + u % 2, f * 128:(f + 1) * 128], w1[u % 2][:, k * F + f * 128:k * F + (f + 1) * 128],
                                                      xT[u][:, k * 128:(k + 1) * 128], start=k == 0, stop=k == DK - 1)
                    last_k.then_inc(h_psum, 1)
                    if not (first and u == 0):
                        output(j - 1, u + 1)
            turns(pe, one)
            output(SLOT_BLOCKS - 1, SLOT_BLOCKS - 1)

        @block.vector
        def _(v):
            own = K.own_v
            own.eng = v
            link = own.link
            norm_stats(nc, K, v, own, asks, gives)
            v.wait_ge(br_psum, 1)
            link(nc.vector.tensor_copy(brB, PS[:P, 7, 0:E8]))
            v.wait_ge(consts, 2)
            link(nc.vector.tensor_copy(rank, K.ranki[:P]))
            link(nc.vector.tensor_copy(rowf, rowi))
            link(nc.vector.tensor_copy(partf, K.parti[:]))
            link(nc.vector.tensor_scalar(before, rowf, partf, None, ALU.is_gt))
            v.wait_ge(loaded, 16 * len(loads))
            v.sem_inc(lg_free, GRP)
            v.sem_inc(rows_kept, 1)
            with v.Fori(0, NG) as g:
                own.loop(g, 0, GRP + 1)
                v.wait_ge(xt_psum, g * GRP + GRP)
                hold(v, K, rows_kept, g + 1)
                for u in range(GRP):
                    t = g * GRP + u
                    own.step(nc.vector.tensor_scalar(K.xs[:P, u], tile_of(K.X[:P], t), col(K.rstd, t), col(K.nmr, t), ALU.mult, ALU.add))
                own.settle()
                own.link(nc.vector.tensor_tensor(K.xs[:P], K.xs[:P], spread_group(gamma_beta[:, 0:D]), ALU.mult))
                nc.vector.tensor_tensor(K.xs[:P], K.xs[:P], spread_group(gamma_beta[:, D:2 * D]), ALU.add).then_inc(xs_ready, 1)
                for u in range(GRP):
                    hold(v, K, lg_psum, g * GRP + u + 1)
                    nc.vector.tensor_tensor(tile_of(lgs, g * GRP + u), PS[:P, 4 + u % 3, 0:E8], brB, ALU.add).then_inc(lg_free, 1)
            own.left(NG)
            v.wait_ge(lg_free, NT + GRP)

            def largest(m, pick):
                link(nc.vector.tensor_reduce(m, lgs, AX, ALU.max))
                link(nc.vector.tensor_tensor(pick, lgs, spread(m), ALU.is_equal))
                link(nc.vector.tensor_tensor(pick, pick, rank, ALU.mult))
                link(nc.vector.tensor_reduce(mi, pick, AX, ALU.max))
                link(nc.vector.tensor_tensor(pick, rank, spread(mi), ALU.is_equal))
            largest(m1, pick1)
            link(nc.vector.scalar_tensor_tensor(lgs, pick1, -BIG, lgs, ALU.mult, ALU.add))
            largest(m2, pick2)
            nc.vector.tensor_tensor(picked, pick1, pick2, ALU.add).then_inc(picks_ready, 1)
            link(nc.vector.tensor_tensor(m2, m2, m1, ALU.subtract))
            v.sem_inc(exp_asks, 1)
            v.wait_ge(exp_gives, 1)
            link(nc.vector.tensor_scalar(m1, ee, 1.0, None, ALU.add))
            link(nc.vector.reciprocal(m1, m1))
            link(nc.vector.tensor_tensor(m2, m1, ee, ALU.mult))
            for b in scan:
                link(nc.vector.memset(b[:, 0:PAD, :], 0.0))
            for b in escan:
                link(nc.vector.memset(b[:, 0:EPAD], 0.0))
            v.wait_ge(prefix_psum, 1)
            in_tile = PS[:P, 7, NT * E8:2 * NT * E8].rearrange("p (t e) -> p t e", e=E8)
            link(nc.vector.tensor_copy(scan[0][:, PAD:, :], in_tile))
            for n, step in enumerate((1, 2, 4, 8, 16)):
                a, b = scan[n % 2], scan[(n + 1) % 2]
                link(nc.vector.tensor_tensor(b[:, PAD:, :], a[:, PAD:, :], a[:, PAD - step:PAD + NT - step, :], ALU.add))
            upto = scan[1]
            link(nc.vector.tensor_copy(count, upto[:, PAD + NT - 1, :]))
            link(nc.vector.tensor_scalar(slotf, rowf[:P, 0:NT], float(BLOCK), None, ALU.mult))
            link(nc.vector.tensor_tensor(lgs, spread_rows(count), spread(slotf), ALU.is_gt))
            link(nc.vector.tensor_reduce(escan[0][:, EPAD:], lgs.rearrange("p t e -> p e t"), AX, ALU.add))
            link(nc.vector.tensor_copy(count, escan[0][:, EPAD:]))
            for n, step in enumerate((1, 2, 4)):
                a, b = escan[n % 2], escan[(n + 1) % 2]
                link(nc.vector.tensor_tensor(b[:, EPAD:], a[:, EPAD:], a[:, EPAD - step:EPAD + E8 - step], ALU.add))
            blocks_upto = escan[1][:, EPAD:]
            link(nc.vector.tensor_tensor(base_row, blocks_upto, count, ALU.subtract))
            link(nc.vector.tensor_scalar(base_row, base_row, float(BLOCK), None, ALU.mult))
            link(nc.vector.tensor_tensor(pos, upto[:, PAD:, :], in_tile, ALU.subtract))
            link(nc.vector.tensor_tensor(pos, pos, PS[:P, 7, 0:NT * E8].rearrange("p (t e) -> p t e", e=E8), ALU.add))
            link(nc.vector.tensor_tensor(pos, pos, spread_rows(base_row), ALU.add))
            for k, pick in enumerate((pick1, pick2)):
                link(nc.vector.tensor_tensor(pick, pick, pos, ALU.mult))
                link(nc.vector.tensor_reduce(slotf, pick, AX, ALU.add))
                nc.vector.tensor_copy(slot_i[:, k, :], slotf).then_inc(slots_ready, 1)
                v.wait_ge(slots_ready, k + 1)
            link(nc.vector.tensor_tensor(block_cmp, blocks_upto[0:1].unsqueeze(1).broadcast_to([1, SLOT_BLOCKS, E8]),
                                         rowf[0:1, 0:SLOT_BLOCKS].unsqueeze(2).broadcast_to([1, SLOT_BLOCKS, E8]), ALU.is_le))
            link(nc.vector.tensor_reduce(expert_f, block_cmp, AX, ALU.add))
            link(nc.vector.tensor_scalar(expert_f, expert_f, float(E8 - 1), None, ALU.min))
            nc.vector.tensor_copy(expert_i, expert_f).then_inc(slots_ready, 1)
            v.wait_ge(slots_ready, 3)
            v.wait_ge(loaded_big, 16 * len(big))

            def expert_of(j):
                return v.value_load(expert_i[0:1, bass.ds(j, 1)], min_val=0, max_val=E8 - 1)

            def weights(j, u):
                e = expert_of(j)
                nc.vector.tensor_copy(w1[u % 2], W1[:, bass.ds(e, 1), :].rearrange("p a n -> p (a n)")).then_inc(w1_ready, 1)

            def result(j, u):
                e = expert_of(j)
                hold(v, K, y_psum, j + 1)
                if not (isinstance(j, int) and j < TURN):
                    hold(v, K, stored[u % TURN], (j - u % TURN) * (16 // TURN))
                nc.vector.tensor_tensor(K.ys[:, u % TURN, :], PS[:, 4 + u % 2, 0:D], b2[:, bass.ds(e, 1), :].rearrange("p a d -> p (a d)"),
                                        ALU.add).then_inc(y_out, 1)

            def one(i, first, last):
                if first:
                    weights(0, 0)
                for u in range(TURN):
                    j = i * TURN + u
                    if not (last and u == TURN - 1):
                        if not (first and u == 0):
                            hold(v, K, h_ready, j)
                        weights(j + 1, u + 1)
                    if not (first and u == 0):
                        result(j - 1, TURN + u - 1)
            turns(v, one, 2)
            result(SLOT_BLOCKS - 1, SLOT_BLOCKS - 1)
            with v.Fori(0, NG) as g:
                for k, (weight, done) in enumerate(((m1, first_added), (m2, out_ready))):
                    for u in range(GRP):
                        t, s = g * GRP + u, 2 * u + k
                        X = tile_of(K.X[:P], t)
                        hold(v, K, K.landed[s], g * 16 + 16 + base[s])
                        if k:
                            hold(v, K, first_added, t + 1)
                        nc.vector.scalar_tensor_tensor(X, ys_node[:, s, :], weight[:, bass.ds(t, 1)], X, ALU.mult, ALU.add).then_inc(done, 1)


def program(nc, out, ins):
    K = Names()
    ctx = ExitStack()
    with ctx:
        def sb(name, shape, dt=F32):
            return ctx.enter_context(nc.sbuf_tensor(name, shape, dt))

        def sem(name):
            return nc.alloc_semaphore(name)

        def dram(name, shape, dt=F32):
            return nc.dram_tensor(name, shape, dt).ap()

        K.ins = ins
        K.in_x, K.in_dst = ins["x"], ins["dst"]
        K.X = sb("X", [128, NT, D])
        K.XTraw = sb("XT", [128, NT * D])
        K.XT = K.XTraw[:, 0:DK * N].rearrange("p (k n) -> p k n", k=DK)
        K.G = sb("G", [128, RING, D])
        K.keep = sb("keep", [128, STEPS])
        K.pen = sb("pen", [128, STEPS])
        K.arena = sb("arena", [128, ARENA])
        K.xs = sb("xs", [128, GRP, D])
        K.xTs = sb("xTs", [128, GRP, DK, NODE_P])
        K.S = sb("S", [128, NT, 6])
        K.t1, K.t2, K.t3, K.std, K.rstd, K.nmr = (sb(n, [128, NT]) for n in ("t1", "t2", "t3", "std", "rstd", "nmr"))
        K.node, K.lane, K.inlane, K.cnt_le, K.cnt_lt = (sb(n, [128, NT]) for n in ("node", "lane", "inlane", "cnt_le", "cnt_lt"))
        K.q2sum, K.k2sum, K.q4sum, K.kscale, K.qscale = (sb(n, [128, NT]) for n in ("q2sum", "k2sum", "q4sum", "kscale", "qscale"))
        K.nrm, K.junk, K.neutral = sb("nrm", [128, 8]), sb("junk", [128, D]), sb("neutral", [1, D])
        K.zeros, K.ys = sb("zeros", [128, D]), sb("ys", [128, GRP, D])
        K.ranki = sb("ranki", [128, NT, E8], I32)
        K.slots, K.slot_ys = dram("slots", [SLOT_BLOCKS * BLOCK, D]), dram("slot_ys", [SLOT_BLOCKS * BLOCK, D])
        K.slots_zeroed = sem("slots_zeroed")
        K.htab = dram("htab", [N * E8, D])
        K.index1 = dram("index1", [LANES, STEPS + RING - TAIL], I32)
        K.out3 = out.rearrange("(p t) d -> p t d", t=NT)
        K.index_sb = sb("index_sb", [128, RING], I32)
        K.nodei, K.lane_i, K.end_i = (sb(n, [128, NT], I32) for n in ("nodei", "lane_i", "end_i"))
        K.goes_on, K.first_i = sb("goes_on", [128, 4]), sb("first_i", [128, 1], I32)
        K.parti = sb("parti", [128, 1], I32)
        K.zero, K.eps = sb("zero", [128, 1]), sb("eps", [128, 1])
        K.ones, K.ident = sb("ones", [128, 128]), sb("ident", [128, 128])
        K.edge_rows = sb("edge_rows_sb", [128, 2, LANES])
        K.lane_keep, K.lane_pen = sb("lane_keep", [128, LANES]), sb("lane_pen", [128, LANES])
        K.wB, K.wphi, K.wtheta = (sb(n, [128, DK, D]) for n in ("wB", "wphi", "wtheta"))
        K.PS = ctx.enter_context(nc.psum_tensor("PS", [128, 8, 512], F32))
        K.pT = lambda u: K.PS[:, u % 4, 0:DK * NODE_P].rearrange("p (k n) -> p k n", k=DK)
        K.pB = lambda u: K.PS[:NODE_P, 4 + u % 3, 0:D]
        K.landed = [sem(f"landed{s}") for s in range(RING)]
        K.landed_total = [16 * GRP if s < GRP else 0 for s in range(RING)]
        K.dve_own, K.waits_passed = sem("dve_own"), sem("waits_passed")
        K.dstf_dram = dram("dstf_dram", [LANES, STEPS])
        K.cnt_dram = dram("cnt_dram", [N + 1])
        K.btab2 = dram("btab", [N, D])
        K.btab = K.btab2.rearrange("(p t) d -> p t d", t=NT)
        wk = lambda name: ins[name].rearrange("(k p) n -> p k n", p=128)
        K.early_loads = [(K.wphi[:], wk("phi_wT")), (K.wtheta[:], wk("theta_wT"))]
        K.hist = dram("hist", [LANES * STEPS + 1, D])
        K.hist3 = K.hist[0:LANES * STEPS, :].rearrange("(p k) d -> p k d", k=STEPS)
        K.in_src = ins["src"]
        stages = (setup, gather0_mix0, ends0, experts0, relations, gather1_mix1, ends1, experts1)
        for stage in stages:
            own_sems = []

            def stage_sem(name):
                own_sems.append(sem(name))
                return own_sems[-1]
            stage(nc, K, stage_sem)
            if stage is not experts1:
                nc.clear_and_free_semaphores(own_sems)
                nc.all_engine_barrier()


def laid_out(inputs):
    import numpy as np
    a = {k: np.ascontiguousarray(v) for k, v in inputs.items()}
    lanes = lambda e, fill: np.concatenate([e, np.full(LANES * STEPS - EDGES, fill, e.dtype)]).reshape(LANES, STEPS)
    staged = lambda e: np.pad(e, ((0, 0), (0, RING - TAIL)))
    out = {
        "x": a["x"], "src": staged(lanes(a["src"], 0)), "dst": lanes(a["dst"], N), "etype": staged(lanes(a["edge_type_8"], 0)),
        "theta_wT": a["L0_gnn_theta_w"].T, "phi_wT": a["L0_gnn_phi_w"].T,
        "theta_b": a["L0_gnn_theta_b"].reshape(1, D), "phi_b": a["L0_gnn_phi_b"].reshape(1, D),
        "mix0_qk": a["L0_mix_W_qkv"][:, :2 * D], "mix0_v": a["L0_mix_W_qkv"][:, 2 * D:],
        "mix0_vT": a["L0_mix_W_qkv"][:, 2 * D:].T, "mix0_b": a["L0_mix_b_qkv"].reshape(1, 3 * D),
        "mix0_bvT": a["L0_mix_b_qkv"][2 * D:].reshape(DK, 128).T,
        "mix0_out": a["L0_mix_W_out"], "mix0_bout": a["L0_mix_b_out"].reshape(1, D),
        "ffn0_Wr": a["L0_ffn_Wr"], "ffn0_br": a["L0_ffn_br"].reshape(1, E8),
        "basis": a["L1_gnn_basis"].reshape(4 * D, D), "comp": a["L1_gnn_comp"].reshape(1, 32), "loop_w": a["L1_gnn_loop_w"],
        "h_bias": a["L1_gnn_h_bias"].reshape(1, D),
        "mix1_qkv": a["L1_mix_W_qkv"], "mix1_out": a["L1_mix_W_out"], "mix1_bout": a["L1_mix_b_out"].reshape(1, D),
        "ffn1_Wr": a["L1_ffn_Wr"], "ffn1_br": a["L1_ffn_br"].reshape(1, E8),
        "gamma_beta0": np.concatenate([a["L0_ffn_gamma"], a["L0_ffn_beta"]]).reshape(1, 2 * D),
        "gamma_beta1": np.concatenate([a["L1_gnn_ln_gamma"], a["L1_gnn_ln_beta"]]).reshape(1, 2 * D),
        "gamma_beta2": np.concatenate([a["L1_ffn_gamma"], a["L1_ffn_beta"]]).reshape(1, 2 * D),
    }
    for n in (0, 1):
        out[f"ffn{n}_W1"] = a[f"L{n}_ffn_W1"].reshape(E8, DK, 128, F).transpose(0, 2, 1, 3).reshape(E8 * 128, DK * F)
        out[f"ffn{n}_W2"] = a[f"L{n}_ffn_W2"].reshape(E8, FK, 128, D).transpose(0, 2, 1, 3).reshape(E8 * 128, FK * D)
        out[f"ffn{n}_b1"] = a[f"L{n}_ffn_b1"].reshape(E8, FK, 128).transpose(0, 2, 1).reshape(E8 * 128, FK)
    out["ffn0_b2"], out["ffn1_b2"] = a["L0_ffn_b2"], a["L1_ffn_b2"].reshape(1, E8 * D)
    return {k: np.ascontiguousarray(v) for k, v in out.items()}


def kernel(**inputs):
    import numpy as np
    import concourse.bacc as bacc
    from concourse.bass_utils import run_bass_kernel_spmd

    nc = bacc.Bacc("TRN2", target_bir_lowering=False, num_devices=1)
    arrays = laid_out(inputs)
    aps = {k: nc.dram_tensor(f"in_{k}_dram", v.shape, mybir.dt.from_np(v.dtype), kind="ExternalInput").ap() for k, v in arrays.items()}
    out = nc.dram_tensor("out_dram", (N, D), F32, kind="ExternalOutput").ap()
    program(nc, out, aps)
    got = run_bass_kernel_spmd(nc, [{f"in_{k}_dram": v for k, v in arrays.items()}], core_ids=[0])
    return got.results[0]["out_dram"]
```

```python
import concourse.bass as bass
from concourse import mybir
from contextlib import ExitStack

F32 = mybir.dt.float32
I32 = mybir.dt.int32
U32 = mybir.dt.uint32
ALU = mybir.AluOpType
ACT = mybir.ActivationFunctionType
AX = mybir.AxisListType.X

N, D = 3125, 256
NODE_P, NT = 125, 25
GRP = 5
NG = NT // GRP
DK = D // 128
EDGES = 103125
LANES = 128
RING = 16
HB = 4
STEPS = 808
TAIL = STEPS % RING
ROUNDS = STEPS // RING
EMPTY = LANES * STEPS
E8, F = 8, 512
FK = F // 128
BLOCK = 128
TURN = 8
RING_T = 4
ROW = D + 1
SLOT_BLOCKS = (2 * N + E8 * (BLOCK - 1)) // BLOCK
BIG = 1e30
ARENA = 19968
LN_EPS = 1e-5
assert NODE_P * NT == N and LANES * STEPS > EDGES and TAIL == RING // 2
assert SLOT_BLOCKS % TURN == 0 and TURN == 2 * RING_T


class Own:

    def __init__(self, eng, sem):
        self.eng, self.sem, self.done = eng, sem, 0

    def step(self, ins):
        ins.then_inc(self.sem, 1)
        self.done = self.done + 1

    def settle(self):
        self.eng.wait_ge(self.sem, self.done)

    def link(self, ins):
        self.step(ins)
        self.settle()

    def loop(self, i, start, per):
        self.base, self.per = self.done, per
        self.done = (i - start) * per + self.base

    def left(self, turns):
        self.done = self.base + turns * self.per


def free(g, u, slots):
    before = slots if u >= slots else GRP - max(w for w in range(GRP) if w % slots == u) + u
    return g * GRP + u + 1 + GRP - before


class Names:
    pass


def hold(eng, K, sem, value):
    eng.wait_ge(sem, value).then_inc(K.waits_passed, 1)


def variances(nc, K, own, tiles, n, act_asks):
    S, P = K.S[:NODE_P, tiles, :], NODE_P
    t1, t2, t3 = K.t1[:P, 0:n], K.t2[:P, 0:n], K.t3[:P, 0:n]
    own.link(nc.vector.tensor_tensor(t1, S[:, :, 1], S[:, :, 4], ALU.add))
    own.link(nc.vector.tensor_tensor(t2, S[:, :, 1], S[:, :, 4], ALU.subtract))
    own.link(nc.vector.tensor_tensor(t3, S[:, :, 2], S[:, :, 5], ALU.add))
    own.link(nc.vector.tensor_tensor(t2, t2, t2, ALU.mult))
    own.link(nc.vector.tensor_scalar(t2, t2, 0.25, LN_EPS, ALU.mult, ALU.add))
    nc.vector.scalar_tensor_tensor(t3, t3, 1.0 / D, t2, ALU.mult, ALU.add).then_inc(act_asks, 1)


def scales(nc, K, v, own, tiles, n, act_gives, given):
    P = NODE_P
    hold(v, K, act_gives, given)
    own.link(nc.vector.reciprocal(K.rstd[:P, tiles], K.std[:P, 0:n]))
    own.link(nc.vector.scalar_tensor_tensor(K.nmr[:P, tiles], K.t1[:P, 0:n], -0.5, K.rstd[:P, tiles], ALU.mult, ALU.mult))


def norm_stats(nc, K, v, own, act_asks, act_gives):
    variances(nc, K, own, slice(0, NT), NT, act_asks)
    scales(nc, K, v, own, slice(0, NT), NT, act_gives, 1)


def setup(nc, K, sem):
    loaded_x = [sem(f"loaded_x{g}") for g in range(NG)]
    loaded_w, loaded_e = sem("loaded_w"), sem("loaded_e")
    ident_zero, ident_done, consts = sem("ident_zero"), sem("ident_done"), sem("consts")
    stats_asks, stats_gives = sem("stats_asks"), sem("stats_gives")
    xs_ready, xt_psum, xt_free, xt_copied = (sem(n) for n in ("xs_ready", "xt_psum", "xt_free", "xt_copied"))
    b_psum, b_free, b_stored = sem("b_psum"), sem("b_free"), sem("b_stored")
    wdiff, edge_diag, edge_rows, lanes_of = sem("wdiff"), sem("edge_diag"), sem("edge_rows"), sem("lanes_of")
    dstf_ready, dstf_stored, cnt_used = sem("dstf_ready"), sem("dstf_stored"), sem("cnt_used")
    P = NODE_P
    PS, A = K.PS, K.arena
    Ball = A[:P, 0:NT * D].rearrange("p (t d) -> p t d", d=D)
    cmp_ = A[:P, NT * D:NT * D + NT * LANES].rearrange("p (t l) -> p t l", l=LANES)
    dsti = A[:, 2 * NT * D:2 * NT * D + STEPS].bitcast(I32)
    diag = A[:, 2 * NT * D + STEPS:2 * NT * D + STEPS + 256].rearrange("p (a l) -> p a l", a=2)
    dstf = K.keep
    cg = K.arena[:P, 2 * NT * D + STEPS + 256:2 * NT * D + STEPS + 256 + GRP * STEPS].rearrange("p (s k) -> p s k", s=GRP)

    with nc.Block() as block:
        @block.sync
        def _(sp):
            sp.dma_start(dsti, K.in_dst).then_inc(loaded_e, 16)
            for g in range(NG):
                tiles = slice(g * GRP, (g + 1) * GRP)
                sp.dma_start(K.X[:P, tiles, :], K.in_x.rearrange("(p t) d -> p t d", t=NT)[:, tiles, :]).then_inc(loaded_x[g], 16)
            for dst, src in K.early_loads:
                sp.dma_start(dst, src).then_inc(loaded_w, 16)
            sp.wait_ge(dstf_ready, 1)
            sp.dma_start(K.dstf_dram, dstf[:]).then_inc(dstf_stored, 16)
            for g in range(NG):
                sp.wait_ge(b_free, GRP * (g + 1) + GRP)
                sp.dma_start(K.btab[:, g * GRP:(g + 1) * GRP, :], Ball[:, g * GRP:(g + 1) * GRP, :]).then_inc(b_stored, 16)
            stage_first_indices(nc, K, sp, K.in_src)
            sp.wait_ge(b_stored, 16 * NG)

        @block.gpsimd
        def _(pool):
            nc.gpsimd.memset(K.ident[:], 0.0).then_inc(ident_zero, 1)
            pool.wait_ge(ident_zero, 1)
            nc.gpsimd.affine_select(out=K.ident[:], in_=K.ident[:], compare_op=ALU.not_equal, fill=1.0, base=0,
                                    pattern=[[-1, 128]], channel_multiplier=1).then_inc(ident_done, 1)
            nc.gpsimd.iota(K.nodei[:P], pattern=[[1, NT]], base=0, channel_multiplier=NT).then_inc(consts, 1)
            nc.gpsimd.iota(K.parti[:], pattern=[[0, 1]], base=0, channel_multiplier=1).then_inc(consts, 1)
            nc.gpsimd.memset(K.zero[:], 0.0).then_inc(consts, 1)
            nc.gpsimd.memset(K.ones[:], 1.0).then_inc(consts, 1)
            pool.wait_ge(lanes_of, 1)
            pool.wait_ge(dstf_stored, 16)
            for t in range(NT):
                if t >= GRP:
                    pool.wait_ge(cnt_used, t - GRP + 1)
                nc.gpsimd.indirect_dma_start(cg[:, t % GRP, :], None, K.dstf_dram,
                                             bass.IndirectOffsetOnAxis(ap=K.lane_i[:P, t:t + 1], axis=0)
                                             ).then_inc(K.landed[t % GRP], 16)

        @block.scalar
        def _(act):
            act.wait_ge(stats_asks, 1)
            nc.scalar.activation(K.std[:P], K.t3[:P], ACT.Sqrt).then_inc(stats_gives, 1)
            act.sem_inc(xt_free, GRP)
            act.sem_inc(b_free, GRP)
            with act.Fori(0, NG) as g:
                for u in range(GRP):
                    hold(act, K, xt_psum, g * GRP + u + 1)
                    nc.scalar.copy(K.xTs[:, u], K.pT(u)).then_inc(xt_copied, 1)
                    nc.scalar.copy(K.XT[:, :, bass.ds((g * GRP + u) * P, P)], K.pT(u)).then_inc(xt_free, 1)
                for u in range(GRP):
                    hold(act, K, b_psum, g * GRP + u + 1)
                    nc.scalar.copy(Ball[:, bass.ds(g * GRP + u, 1), :], K.pB(u)).then_inc(b_free, 1)

        @block.tensor
        def _(pe):
            pe.wait_ge(ident_done, 1)
            pe.wait_ge(consts, 4)
            pe.wait_ge(edge_diag, 1)
            nc.tensor.matmul(PS[:, 7, 0:256], K.ones[:, 0:128], diag.rearrange("p a l -> p (a l)"),
                             start=True, stop=True).then_inc(edge_rows, 1)
            pe.wait_ge(wdiff, 1)
            with pe.Fori(0, NG) as g:
                for u in range(GRP):
                    pe.wait_ge(xs_ready, g * GRP + u + 1)
                    pe.wait_ge(xt_free, free(g, u, 4))
                    for k in range(DK):
                        last = nc.tensor.transpose(K.pT(u)[:, k, :], K.xs[:P, u, k * 128:(k + 1) * 128], K.ident[:P, :P])
                    last.then_inc(xt_psum, 1)
                for u in range(GRP):
                    pe.wait_ge(xt_copied, g * GRP + u + 1)
                    pe.wait_ge(b_free, free(g, u, 3))
                    for k in range(DK):
                        last = nc.tensor.matmul(K.pB(u), K.xTs[:, u, k, :], K.wB[:, k, :], start=k == 0, stop=k == DK - 1)
                    last.then_inc(b_psum, 1)

        @block.vector
        def _(v):
            own = K.own_v = Own(v, K.dve_own)
            v.wait_ge(loaded_e, 16)
            own.link(nc.vector.tensor_copy(dstf[:], dsti))
            v.sem_inc(dstf_ready, 1)
            v.wait_ge(ident_done, 1)
            own.link(nc.vector.tensor_scalar(diag[:, 0, :], K.ident[:], dstf[:, 0:1], None, ALU.mult))
            nc.vector.tensor_scalar(diag[:, 1, :], K.ident[:], dstf[:, STEPS - 1:STEPS], None, ALU.mult).then_inc(edge_diag, 1)
            v.wait_ge(consts, 4)
            own.link(nc.vector.tensor_copy(K.node[:P], K.nodei[:P]))
            v.wait_ge(edge_rows, 1)
            own.link(nc.vector.tensor_copy(K.edge_rows[:].rearrange("p a l -> p (a l)"), PS[:, 7, 0:256]))
            own.link(nc.vector.tensor_tensor(cmp_, K.edge_rows[:P, 1:2, :].broadcast_to([P, NT, LANES]),
                                             K.node[:P].unsqueeze(2).broadcast_to([P, NT, LANES]), ALU.is_le))
            own.link(nc.vector.tensor_reduce(K.lane[:P], cmp_, AX, ALU.add))
            nc.vector.tensor_copy(K.lane_i[:P], K.lane[:P]).then_inc(lanes_of, 1)
            v.wait_ge(loaded_w, 16 * len(K.early_loads))
            nc.vector.tensor_tensor(K.wB[:], K.wphi[:], K.wtheta[:], ALU.subtract).then_inc(wdiff, 1)
            for g in range(NG):
                v.wait_ge(loaded_x[g], 16)
                for t in range(g * GRP, (g + 1) * GRP):
                    own.step(nc.vector.bn_stats(K.S[:P, t, :], K.X[:P, t, :]))
            own.settle()
            norm_stats(nc, K, v, own, stats_asks, stats_gives)
            with v.Fori(0, NG) as g:
                normalise(K, nc, v, g, xt_free, xs_ready)
                for u in range(GRP):
                    hold(v, K, K.landed[u], 16 * g + 16)
                    nc.vector.tensor_scalar(cg[:, u, :], cg[:, u, :], K.node[:P, bass.ds(g * GRP + u, 1)], None,
                                            ALU.is_le, ALU.add,
                                            accum_out=K.inlane[:P, bass.ds(g * GRP + u, 1)]).then_inc(cnt_used, 1)
            v.wait_ge(cnt_used, NT)
            own.link(nc.vector.scalar_tensor_tensor(K.cnt_le[:P], K.lane[:P], float(STEPS), K.inlane[:P], ALU.mult, ALU.add))



def lane_factors(nc, K, own):
    dstf = K.keep
    own.link(nc.vector.tensor_scalar(K.pen[:], dstf[:], dstf[:, 0:1], None, ALU.is_equal, ALU.add, accum_out=K.goes_on[:, 2:3]))
    own.link(nc.vector.tensor_copy(K.goes_on[:, 3:4], K.parti[:]))
    own.link(nc.vector.scalar_tensor_tensor(K.goes_on[:, 3:4], K.goes_on[:, 3:4], float(STEPS), K.goes_on[:, 2:3], ALU.mult, ALU.add))
    own.link(nc.vector.tensor_scalar(K.first_i[:], K.goes_on[:, 3:4], -1.0, None, ALU.add))
    own.link(nc.vector.tensor_tensor(K.pen[:, 1:STEPS], dstf[:, 1:STEPS], dstf[:, 0:STEPS - 1], ALU.is_equal))
    own.link(nc.vector.tensor_copy(K.keep[:, 1:STEPS], K.pen[:, 1:STEPS]))
    own.link(nc.vector.memset(K.keep[:, 0:1], 0.0))
    own.link(nc.vector.tensor_scalar(K.pen[:], K.keep[:], BIG, -BIG, ALU.mult, ALU.add))
    own.link(nc.vector.memset(K.lane_keep[:], 0.0))
    own.link(nc.vector.tensor_tensor(K.lane_keep[:, 1:LANES], K.edge_rows[:, 0, 1:LANES], K.edge_rows[:, 1, 0:LANES - 1], ALU.is_equal))
    own.link(nc.vector.tensor_tensor(K.lane_pen[:], K.lane_keep[:], K.ident[:], ALU.mult))
    own.link(nc.vector.tensor_reduce(K.goes_on[:, 0:1], K.lane_pen[:], AX, ALU.add))
    own.link(nc.vector.tensor_scalar(K.goes_on[:, 1:2], K.goes_on[:, 0:1], BIG, -BIG, ALU.mult, ALU.add))
    own.link(nc.vector.tensor_tensor(K.lane_pen[:], K.edge_rows[:, 0, :], K.edge_rows[:, 1, :], ALU.is_equal))
    own.link(nc.vector.tensor_tensor(K.lane_keep[:], K.lane_keep[:], K.lane_pen[:], ALU.mult))
    own.link(nc.vector.tensor_scalar(K.lane_pen[:], K.lane_keep[:], BIG, -BIG, ALU.mult, ALU.add))


def end_rows(nc, K, own):
    t2, t3 = K.t2[:NODE_P], K.t3[:NODE_P]
    own.link(nc.vector.tensor_tensor(t3, K.cnt_lt[:NODE_P], K.cnt_le[:NODE_P], ALU.is_equal))
    own.link(nc.vector.tensor_scalar(t2, K.cnt_le[:NODE_P], -1.0, float(EMPTY + 1), ALU.mult, ALU.add))
    own.link(nc.vector.tensor_tensor(t2, t2, t3, ALU.mult))
    own.link(nc.vector.scalar_tensor_tensor(t2, K.cnt_le[:NODE_P], -1.0, t2, ALU.add, ALU.add))
    own.link(nc.vector.tensor_copy(K.end_i[:NODE_P], t2))



class Pass:

    def __init__(self, K, sem, name, table, index, factor, op0, op1, lane_factor, neutral):
        self.table, self.index, self.factor = table, index, factor
        self.op0, self.op1, self.lane_factor, self.neutral = op0, op1, lane_factor, neutral
        self.base = K.landed_total
        self.folded = sem(name + "_folded")
        self.staged_base = K.staged_total
        K.staged_total += 16 * (ROUNDS + 1)
        self.written = [sem(f"{name}_written{b}") for b in range(RING // HB)]


def gather_rounds(eng, one):
    one(0, RING, True)
    with eng.Fori(1, ROUNDS) as i:
        one(i, RING, False)
    one(ROUNDS, TAIL, False)


def stage_index(nc, K, sp, index, i, h):
    half = RING // 2
    sp.dma_start(K.index_sb[:, h * half:(h + 1) * half], index[:, bass.ds(i * RING + h * half, half)]).then_inc(K.index_staged[h], 16)


def stage_first_indices(nc, K, sp, index):
    for h in range(2):
        stage_index(nc, K, sp, index, 0, h)


def gather_sync(nc, K, sp, L):
    def one(i, steps, first):
        for b in range(steps // HB):
            sp.wait_ge(L.folded, i * RING + HB * (b + 1))
            sp.dma_start(K.hist3[:, bass.ds(i * RING + b * HB, HB), :], K.G[:, b * HB:(b + 1) * HB, :]
                         ).then_inc(L.written[b], 16)
            if steps == RING and b % 2 == 1:
                stage_index(nc, K, sp, L.index, i + 1, b // 2)
    gather_rounds(sp, one)


def gather_pool(nc, K, pool, L):
    def one(i, steps, first):
        for s in range(steps):
            if s % (RING // 2) == 0:
                hold(pool, K, K.index_staged[s // (RING // 2)], i * 16 + 16 + L.staged_base)
            if s % HB == 0 and not first:
                hold(pool, K, L.written[s // HB], i * 16)
                hold(pool, K, L.folded, (i - 1) * RING + s + HB + 1)
            if first and s == RING - 1:
                pool.wait_ge(L.folded, 1)
            nc.gpsimd.indirect_dma_start(K.G[:, s, :], None, L.table,
                                         bass.IndirectOffsetOnAxis(ap=K.index_sb[:, s:s + 1], axis=0)
                                         ).then_inc(K.landed[s], 16)
    gather_rounds(pool, one)


def gather_fold(nc, K, v, L, i, steps, first, beside=None):
    for s in range(steps):
        hold(v, K, K.landed[s], i * 16 + 16 + L.base[s])
        if not (first and s == 0):
            v.wait_ge(L.folded, i * RING + s)
        nc.vector.scalar_tensor_tensor(K.G[:, s, :], K.G[:, (s - 1) % RING, :], L.factor[:, bass.ds(i * RING + s, 1)],
                                       K.G[:, s, :], L.op0, L.op1).then_inc(L.folded, 1)
        if beside:
            beside(s)


BESIDE = 36


CARRY_SEMS = "trail_up scanned trail_back first_landed fixed neutral_set neutral_stored".split()
FIX = RING // 2


def carry_tensor(nc, K, pe, L, c):
    pe.wait_ge(L.folded, STEPS)
    for k in range(DK):
        last = nc.tensor.transpose(K.PS[:, 0, k * 128:(k + 1) * 128], K.G[:, TAIL - 1, k * 128:(k + 1) * 128], K.ident[:])
    last.then_inc(c.trail_up, 1)
    pe.wait_ge(c.scanned, DK)
    for k in range(DK):
        last = nc.tensor.transpose(K.PS[:, 1, k * 128:(k + 1) * 128], K.trail[:, k, 0:LANES], K.ident[:])
    last.then_inc(c.trail_back, 1)


def carry_vector(nc, K, v, own, L, c):
    own.link(nc.vector.memset(K.neutral[:], L.neutral))
    v.sem_inc(c.neutral_set, 1)
    own.link(nc.vector.memset(K.trail[:, :, 0:1], 0.0))
    v.wait_ge(c.trail_up, 1)
    for k in range(DK):
        nc.vector.tensor_tensor_scan(K.trail[:, k, 1:1 + LANES], L.lane_factor[:], K.PS[:, 0, k * 128:(k + 1) * 128], 0.0,
                                     L.op0, L.op1).then_inc(c.scanned, 1)
    v.wait_ge(c.trail_back, 1)
    own.link(nc.vector.tensor_scalar(K.junk[:], K.PS[:, 1, 0:D], K.goes_on[:, 0:1],
                                     K.goes_on[:, 1:2] if L.neutral else 0.0, ALU.mult, ALU.add))
    v.wait_ge(c.first_landed, 1)
    nc.vector.tensor_tensor(K.G[:, FIX, :], K.G[:, FIX, :], K.junk[:], L.op1).then_inc(c.fixed, 1)


def carry_pool(nc, K, pool, L, c):
    for b in range(RING // HB):
        pool.wait_ge(L.written[b], 16 * (ROUNDS + (b < TAIL // HB)))
    pool.wait_ge(L.folded, STEPS)
    index = bass.IndirectOffsetOnAxis(ap=K.first_i[:, 0:1], axis=0)
    nc.gpsimd.indirect_dma_start(K.G[:, FIX, :], None, K.hist, index).then_inc(K.landed[FIX], 16)
    pool.wait_ge(K.landed[FIX], L.base[FIX] + 16 * (ROUNDS + 1))
    pool.sem_inc(c.first_landed, 1)
    pool.wait_ge(c.fixed, 1)
    nc.gpsimd.indirect_dma_start(K.hist, index, K.G[:, FIX, :], None).then_inc(K.landed[FIX], 16)
    pool.wait_ge(K.landed[FIX], L.base[FIX] + 16 * (ROUNDS + 2))


def carry_sync(nc, K, sp, L, c):
    sp.wait_ge(c.neutral_set, 1)
    sp.dma_start(K.hist[EMPTY:EMPTY + 1, :], K.neutral[0:1, :]).then_inc(c.neutral_stored, 16)
    sp.wait_ge(c.neutral_stored, 16)
    for h in range(2):
        sp.wait_ge(K.index_staged[h], L.staged_base + 16 * (ROUNDS + 1))


def carry_names(sem, prefix):
    c = Names()
    (c.trail_up, c.scanned, c.trail_back, c.first_landed, c.fixed, c.neutral_set, c.neutral_stored) = (
        sem(prefix + n) for n in CARRY_SEMS)
    return c


def gather0_mix0(nc, K, sem):
    L = Pass(K, sem, "max", K.btab2, K.in_src, K.pen, ALU.add, ALU.max, K.lane_pen, -BIG)
    names = """loaded_m centred x_staged qk_psum qk_free q2_ready q2T_psum q2T_free stats_done roots r_ready
               v_psum v_free vk_ready kv_done kv_copied norm_root kvw_psum acc_free
               end_weights q_staged ae_psum ae_free mix_added p1_psum p1_free cnt_stored cnt_back""".split()
    (loaded_m, centred, x_staged, qk_psum, qk_free, q2_ready, q2T_psum, q2T_free, stats_done, roots, r_ready,
     v_psum, v_free, vk_ready, kv_done, kv_copied, norm_root, kvw_psum, acc_free,
     end_weights, q_staged, ae_psum, ae_free, mix_added, p1_psum, p1_free, cnt_stored, cnt_back) = (
        sem("m0_" + n) for n in names)
    c = carry_names(sem, "c0_")
    P, PS, A = NODE_P, K.PS, K.arena
    K2 = A[:P, 0:NT * D].rearrange("p (t d) -> p t d", d=D)
    K.dst_part = K2
    at = NT * D
    Q2T = K.Q2T = A[:, at:at + DK * N].rearrange("p (k n) -> p k n", k=DK)
    at += DK * N

    def piece(n):
        nonlocal at
        at += n
        return A[:, at - n:at]
    wqk = piece(DK * 512).rearrange("p (k n) -> p k n", k=DK)
    wv, wvT, wout = (piece(DK * D).rearrange("p (k n) -> p k n", k=DK) for _ in range(3))
    KVW = piece(DK * D).rearrange("p (k n) -> p k n", k=DK)
    wE = piece(DK * 512).rearrange("p (k n) -> p k n", k=DK)
    kvT = piece(DK * D).rearrange("p (k n) -> p k n", k=DK)
    K.trail = piece(DK * (1 + LANES)).rearrange("p (k n) -> p k n", k=DK)
    K.rowE = piece(512)[0:1, :]
    rowqkv = piece(768)[0:1, :]
    rowb = piece(512)[0:1, :]
    rowo = piece(256)[0:1, :]
    bvT = piece(2)
    assert at <= ARENA
    wk = lambda name: K.ins[name].rearrange("(k p) n -> p k n", p=128)
    loads = [(wqk, wk("mix0_qk")), (wv, wk("mix0_v")), (wvT, wk("mix0_vT")), (wout, wk("mix0_out")),
             (rowqkv, K.ins["mix0_b"]), (rowb[:, 0:256], K.ins["theta_b"]), (rowb[:, 256:512], K.ins["phi_b"]),
             (rowo, K.ins["mix0_bout"]), (bvT, K.ins["mix0_bvT"])]

    with nc.Block() as block:
        @block.sync
        def _(sp):
            for dst, src in loads:
                sp.dma_start(dst, src).then_inc(loaded_m, 16)
            sp.dma_start(K.cnt_dram[1:N + 1].rearrange("(p t) -> p t", t=NT), K.cnt_le[:P]).then_inc(cnt_stored, 16)
            sp.dma_start(K.cnt_dram[0:1].rearrange("(a b) -> a b", a=1), K.zero[0:1, 0:1]).then_inc(cnt_stored, 16)
            sp.wait_ge(cnt_stored, 32)
            sp.dma_start(K.cnt_lt[:P], K.cnt_dram[0:N].rearrange("(p t) -> p t", t=NT)).then_inc(cnt_back, 16)
            gather_sync(nc, K, sp, L)
            carry_sync(nc, K, sp, L, c)

        @block.gpsimd
        def _(pool):
            gather_pool(nc, K, pool, L)
            carry_pool(nc, K, pool, L, c)

        @block.scalar
        def _(act):
            act.sem_inc(qk_free, GRP)
            act.sem_inc(q2T_free, GRP)
            act.sem_inc(v_free, GRP)
            with act.Fori(0, NG) as g:
                for u in range(GRP):
                    nc.scalar.copy(K.xTs[:, u], K.XT[:, :, bass.ds((g * GRP + u) * P, P)]).then_inc(x_staged, 1)
                for u in range(GRP):
                    t = g * GRP + u
                    hold(act, K, qk_psum, t + 1)
                    nc.scalar.activation(K.xs[:P, u], PS[:P, u, 0:D], ACT.Square,
                                         accum_out=K.q2sum[:P, bass.ds(t, 1)]).then_inc(q2_ready, 1)
                    nc.scalar.activation(K2[:, bass.ds(t, 1), :], PS[:P, u:u + 1, D:2 * D], ACT.Square,
                                         accum_out=K.k2sum[:P, bass.ds(t, 1)]).then_inc(qk_free, 1)
                    hold(act, K, q2_ready, t + 1)
                    nc.scalar.activation(K.junk[:P], K.xs[:P, u], ACT.Square,
                                         accum_out=K.q4sum[:P, bass.ds(t, 1)]).then_inc(stats_done, 1)
                for u in range(GRP):
                    t = g * GRP + u
                    hold(act, K, q2T_psum, t + 1)
                    nc.scalar.copy(Q2T[:, :, bass.ds(t * P, P)],
                                   PS[:, 5 + u % 3, 0:DK * P].rearrange("p (k n) -> p k n", k=DK)).then_inc(q2T_free, 1)
            act.wait_ge(stats_done, NT)
            nc.scalar.activation(K.std[:P], K.q4sum[:P], ACT.Sqrt).then_inc(roots, 1)
            act.wait_ge(r_ready, 1)
            with act.Fori(0, NG) as g:
                for u in range(GRP):
                    nc.scalar.copy(K.xTs[:, u], K.XT[:, :, bass.ds((g * GRP + u) * P, P)]).then_inc(x_staged, 1)
                for u in range(GRP):
                    t = g * GRP + u
                    hold(act, K, v_psum, t + 1)
                    hold(act, K, acc_free, t + 1)
                    nc.scalar.activation(K.xs[:P, u], PS[:P, u % 3, 0:D], ACT.Copy,
                                         scale=K.kscale[:P, bass.ds(t, 1)]).then_inc(v_free, 1)
                    nc.scalar.activation(K.ys[:P, u], K2[:, bass.ds(t, 1), :].rearrange("p a d -> p (a d)"), ACT.Square,
                                         scale=K.kscale[:P, bass.ds(t, 1)]).then_inc(vk_ready, 1)
            act.wait_ge(kv_copied, 2)
            nc.scalar.activation(K.nrm[:, 2:4], K.nrm[:, 0:2], ACT.Sqrt).then_inc(norm_root, 1)
            act.wait_ge(acc_free, NT + GRP)
            act.sem_inc(ae_free, GRP)
            with act.Fori(0, NG) as g:
                for u in range(GRP):
                    t = g * GRP + u
                    hold(act, K, ae_free, t + 1)
                    hold(act, K, p1_free, t + 1)
                    cols = bass.ds(t * P, P)
                    nc.scalar.copy(K.xTs[:, u], K.XT[:, :, cols]).then_inc(x_staged, 1)
                    nc.scalar.copy(K.ys[:, u, 0:DK * P].rearrange("p (k n) -> p k n", k=DK), K.Q2T[:, :, cols]).then_inc(q_staged, 1)
                for u in range(GRP):
                    t = g * GRP + u
                    hold(act, K, mix_added, t + 1)
                    nc.scalar.copy(tile_of(K.dst_part, t), PS[:P, u, 0:D]).then_inc(ae_free, 1)

        @block.tensor
        def _(pe):
            pe.wait_ge(centred, 1)
            with pe.Fori(0, NG) as g:
                for u in range(GRP):
                    t = g * GRP + u
                    pe.wait_ge(x_staged, t + 1)
                    pe.wait_ge(qk_free, t + 1)
                    for k in range(DK):
                        nc.tensor.matmul(PS[:P, u, :], K.xTs[:, u, k, :], wqk[:, k, :], start=k == 0, stop=False)
                    nc.tensor.matmul(PS[:P, u, :], K.ones[0:1, 0:P], rowqkv[:, 0:512], start=False, stop=True).then_inc(qk_psum, 1)
                for u in range(GRP):
                    t = g * GRP + u
                    pe.wait_ge(q2_ready, t + 1)
                    pe.wait_ge(q2T_free, free(g, u, 3))
                    for k in range(DK):
                        last = nc.tensor.transpose(PS[:, 5 + u % 3, k * P:(k + 1) * P], K.xs[:P, u, k * 128:(k + 1) * 128], K.ident[:P, :P])
                    last.then_inc(q2T_psum, 1)
            pe.wait_ge(q2T_free, NT + GRP)
            pe.sem_inc(acc_free, GRP)
            for bank in (5, 6):
                nc.tensor.matmul(PS[:, bank, :], K.zeros[:], wqk[:, 0, :], start=True, stop=False)
            with pe.Fori(0, NG) as g:
                for u in range(GRP):
                    t = g * GRP + u
                    pe.wait_ge(x_staged, t + 1 + NT)
                    pe.wait_ge(v_free, free(g, u, 3))
                    for k in range(DK):
                        nc.tensor.matmul(PS[:P, u % 3, 0:D], K.xTs[:, u, k, :], wv[:, k, :], start=k == 0, stop=False)
                    nc.tensor.matmul(PS[:P, u % 3, 0:D], K.ones[0:1, 0:P], rowqkv[:, 512:768], start=False, stop=True).then_inc(v_psum, 1)
                for u in range(GRP):
                    t = g * GRP + u
                    pe.wait_ge(vk_ready, t + 1)
                    for k in range(DK):
                        nc.tensor.matmul(PS[:, 5, k * D:(k + 1) * D], K.xs[:P, u, k * 128:(k + 1) * 128],
                                         K2[:, bass.ds(t, 1), :].rearrange("p a d -> p (a d)"), start=False, stop=False)
                        last = nc.tensor.matmul(PS[:, 6, k:k + 1], K.ys[:P, u, k * 128:(k + 1) * 128], K.ones[:P, 0:1],
                                                start=False, stop=False)
                    last.then_inc(acc_free, 1)
            for bank in (5, 6):
                last = nc.tensor.matmul(PS[:, bank, :], K.zeros[:], wqk[:, 0, :], start=False, stop=True)
            last.then_inc(kv_done, 1)
            for k in range(DK):
                for d in range(DK):
                    nc.tensor.matmul(PS[:, 3, k * D:(k + 1) * D], wvT[:, d, k * 128:(k + 1) * 128], wout[:, d, :], start=d == 0, stop=d == DK - 1)
            for d in range(DK):
                nc.tensor.matmul(PS[0:1, 4, 0:D], bvT[:, d:d + 1], wout[:, d, :], start=d == 0, stop=d == DK - 1)
            pe.wait_ge(kv_copied, 2)
            pe.wait_ge(v_free, NT + GRP)
            for k in range(DK):
                for d in range(DK):
                    last = nc.tensor.matmul(PS[:, 7, k * D:(k + 1) * D], kvT[:, d, k * 128:(k + 1) * 128], wout[:, d, :], start=d == 0, stop=d == DK - 1)
            last.then_inc(kvw_psum, 1)
            pe.wait_ge(end_weights, 1)
            with pe.Fori(0, NG) as g:
                for u in range(GRP):
                    t = g * GRP + u
                    pe.wait_ge(x_staged, t + 1 + 2 * NT)
                    pe.wait_ge(ae_free, t + 1)
                    for k in range(DK):
                        nc.tensor.matmul(PS[:P, u, :], K.xTs[:, u, k, :], wE[:, k, :], start=k == 0, stop=False)
                    nc.tensor.matmul(PS[:P, u, :], K.ones[0:1, 0:P], K.rowE, start=False, stop=True).then_inc(ae_psum, 1)
                for u in range(GRP):
                    pe.wait_ge(q_staged, g * GRP + u + 1)
                    pe.wait_ge(p1_free, free(g, u, 3))
                    for k in range(DK):
                        last = nc.tensor.matmul(PS[:P, 5 + u % 3, 0:D], K.ys[:, u, k * P:(k + 1) * P], KVW[:, k, :],
                                                start=k == 0, stop=k == DK - 1)
                    last.then_inc(p1_psum, 1)
            pe.wait_ge(ae_free, NT + GRP)
            carry_tensor(nc, K, pe, L, c)

        @block.vector
        def _(v):
            own = K.own_v
            own.eng = v
            own.link(nc.vector.memset(K.zeros[:], 0.0))
            own.link(nc.vector.memset(K.G[:, RING - 1, :], 0.0))
            lane_factors(nc, K, own)
            gather_fold(nc, K, v, L, 0, RING, True)
            v.wait_ge(cnt_back, 16)
            end_rows(nc, K, own)
            v.wait_ge(loaded_m, 16 * len(loads))
            for which in range(2):
                for w, n, p in [(wqk[:, k, which * D:(which + 1) * D], k, 128) for k in range(DK)] + [(rowqkv[:, which * D:(which + 1) * D], 2, 1)]:
                    own.link(nc.vector.tensor_reduce(K.nrm[:p, 4:5], w, AX, ALU.add))
                    own.link(nc.vector.tensor_scalar(K.nrm[:p, 5:6], K.nrm[:p, 4:5], -1.0 / D, None, ALU.mult))
                    own.link(nc.vector.tensor_scalar(w, w, K.nrm[:p, 5:6], None, ALU.add))
            v.sem_inc(centred, 1)
            with v.Fori(1, 12) as i:
                gather_fold(nc, K, v, L, i, RING, False)
            v.wait_ge(roots, 1)
            own.link(nc.vector.tensor_scalar(K.kscale[:P], K.k2sum[:P], 1e-7, None, ALU.add))
            nc.vector.reciprocal(K.kscale[:P], K.kscale[:P]).then_inc(r_ready, 1)
            own.link(nc.vector.tensor_scalar(K.q2sum[:P], K.q2sum[:P], 1e-7, None, ALU.add))
            own.link(nc.vector.reciprocal(K.q2sum[:P], K.q2sum[:P]))
            own.link(nc.vector.tensor_tensor(K.t1[:P], K.std[:P], K.q2sum[:P], ALU.mult))
            own.link(nc.vector.tensor_scalar(K.t1[:P], K.t1[:P], 1e-12, None, ALU.max))
            own.link(nc.vector.reciprocal(K.t1[:P], K.t1[:P]))
            own.link(nc.vector.scalar_tensor_tensor(K.qscale[:P], K.q2sum[:P], N ** -0.5, K.t1[:P], ALU.mult, ALU.mult))
            with v.Fori(12, BESIDE) as i:
                gather_fold(nc, K, v, L, i, RING, False)
            v.wait_ge(kv_done, 1)
            nc.vector.tensor_copy(kvT.rearrange("p k n -> p (k n)"), PS[:, 5, :]).then_inc(kv_copied, 1)
            nc.vector.tensor_copy(K.nrm[:, 0:2], PS[:, 6, 0:2]).then_inc(kv_copied, 1)
            v.wait_ge(norm_root, 1)
            own.link(nc.vector.tensor_scalar(K.nrm[:, 2:4], K.nrm[:, 2:4], 1e-12, None, ALU.max))
            own.link(nc.vector.reciprocal(K.nrm[:, 2:4], K.nrm[:, 2:4]))
            v.wait_ge(kvw_psum, 1)
            for k in range(DK):
                own.link(nc.vector.tensor_scalar(KVW[:, k, :], PS[:, 7, k * D:(k + 1) * D], K.nrm[:, 2 + k:3 + k], None, ALU.mult))
                own.link(nc.vector.tensor_copy(wE[:, k, 0:D], K.wtheta[:, k, :]))
                own.link(nc.vector.tensor_copy(wE[:, k, D:2 * D], PS[:, 3, k * D:(k + 1) * D]))
            own.link(nc.vector.tensor_tensor(K.rowE[:, 0:D], rowb[:, 0:D], rowb[:, D:2 * D], ALU.add))
            own.link(nc.vector.tensor_tensor(K.rowE[:, D:2 * D], PS[0:1, 4, 0:D], rowo, ALU.add))
            v.sem_inc(end_weights, 1)
            v.sem_inc(p1_free, GRP)
            with v.Fori(0, NG) as g:
                def constant_part(s):
                    u, X = s // 3, K.X[:P]
                    if s % 3 == 0 and u < GRP:
                        t = g * GRP + u
                        v.wait_ge(ae_psum, t + 1)
                        nc.vector.tensor_tensor(tile_of(X, t), tile_of(X, t), PS[:P, u, D:2 * D], ALU.add).then_inc(mix_added, 1)

                def attention_part(s):
                    u, X = s // 3, K.X[:P]
                    if s % 3 == 0 and u < GRP:
                        t = g * GRP + u
                        v.wait_ge(p1_psum, t + 1)
                        v.wait_ge(mix_added, t + 1)
                        nc.vector.scalar_tensor_tensor(tile_of(X, t), PS[:P, 5 + u % 3, 0:D], col(K.qscale, t), tile_of(X, t),
                                                       ALU.mult, ALU.add).then_inc(p1_free, 1)
                gather_fold(nc, K, v, L, g * 2 + BESIDE, RING, False, constant_part)
                gather_fold(nc, K, v, L, g * 2 + BESIDE + 1, RING, False, attention_part)
            with v.Fori(BESIDE + 2 * NG, ROUNDS) as i:
                gather_fold(nc, K, v, L, i, RING, False)
            gather_fold(nc, K, v, L, ROUNDS, TAIL, False)
            carry_vector(nc, K, v, own, L, c)
    for s in range(RING):
        K.landed_total[s] += 16 * (ROUNDS + (s < TAIL) + 2 * (s == FIX))


def gather_ends(nc, K, pool, m_used):
    for t in range(NT):
        u = t % GRP
        if t >= GRP:
            pool.wait_ge(m_used, t - GRP + 1)
        nc.gpsimd.indirect_dma_start(K.G[:NODE_P, u, :], None, K.hist,
                                     bass.IndirectOffsetOnAxis(ap=K.end_i[:NODE_P, t:t + 1], axis=0)
                                     ).then_inc(K.landed[u], 16)


def ends_taken(K):
    for s in range(GRP):
        K.landed_total[s] += 16 * NG


def tile_of(buf, t):
    return buf[:, bass.ds(t, 1), :].rearrange("p a d -> p (a d)")


def col(buf, t):
    return buf[:NODE_P, bass.ds(t, 1)]


def ends0(nc, K, sem):
    m_used, summed = sem("e0_m_used"), sem("e0_summed")
    P, G, X = NODE_P, K.G, K.X[:NODE_P]
    base = list(K.landed_total)
    with nc.Block() as block:
        @block.gpsimd
        def _(pool):
            gather_ends(nc, K, pool, m_used)

        @block.vector
        def _(v):
            own = K.own_v
            own.eng = v
            with v.Fori(0, NG) as g:
                own.loop(g, 0, GRP)
                for u in range(GRP):
                    t = g * GRP + u
                    hold(v, K, K.landed[u], g * 16 + 16 + base[u])
                    nc.vector.tensor_tensor(K.xs[:P, u], G[:P, u, :], tile_of(K.dst_part, t), ALU.add).then_inc(m_used, 1)
                for u in range(GRP):
                    t = g * GRP + u
                    hold(v, K, m_used, t + 1)
                    nc.vector.scalar_tensor_tensor(tile_of(X, t), K.xs[:P, u], 0.0, tile_of(X, t), ALU.max, ALU.add).then_inc(summed, 1)
                for u in range(GRP):
                    t = g * GRP + u
                    hold(v, K, summed, t + 1)
                    own.step(nc.vector.bn_stats(K.S[:P, bass.ds(t, 1), :], tile_of(X, t)))
            own.left(NG)
            own.settle()
    ends_taken(K)


def transposes(K, nc, pe, g, ready, xt_psum, xt_free, ring):
    for u in range(GRP):
        pe.wait_ge(ready, g * GRP + u + 1)
        pe.wait_ge(xt_free, free(g, u, ring))
        for k in range(DK):
            last = nc.tensor.transpose(K.PS[:, u % ring, k * NODE_P:(k + 1) * NODE_P], K.xs[:NODE_P, u, k * 128:(k + 1) * 128],
                                       K.ident[:NODE_P, :NODE_P])
        last.then_inc(xt_psum, 1)


def normalise(K, nc, v, g, xt_free, xs_ready):
    for u in range(GRP):
        t = g * GRP + u
        hold(v, K, xt_free, t + 1)
        nc.vector.tensor_scalar(K.xs[:NODE_P, u], tile_of(K.X[:NODE_P], t), col(K.rstd, t), col(K.nmr, t),
                                ALU.mult, ALU.add).then_inc(xs_ready, 1)


def add_normed_scalar(nc, K, act, a, stats_ready, normed):
    act.wait_ge(stats_ready, 1)
    with act.Fori(0, NG) as g:
        for u in range(GRP):
            t = g * GRP + u
            nc.scalar.activation(tile_of(a, t), tile_of(a, t), ACT.Identity, scale=col(K.rstd, t), bias=col(K.nmr, t)).then_inc(normed, 1)


def add_normed_vector(nc, K, v, own, a, gamma, normed):
    P, X = NODE_P, K.X[:NODE_P]
    gamma_group = gamma[:P].unsqueeze(1).broadcast_to([P, GRP, D])
    with v.Fori(0, NG) as g:
        own.loop(g, 0, 2 + GRP)
        tiles = bass.ds(g * GRP, GRP)
        hold(v, K, normed, g * GRP + GRP)
        own.step(nc.vector.tensor_tensor(a[:, tiles, :], a[:, tiles, :], gamma_group, ALU.mult))
        hold(v, K, own.sem, own.done)
        own.step(nc.vector.tensor_tensor(X[:, tiles, :], X[:, tiles, :], a[:, tiles, :], ALU.add))
        hold(v, K, own.sem, own.done)
        for u in range(GRP):
            own.step(nc.vector.bn_stats(K.S[:P, bass.ds(g * GRP + u, 1), :], tile_of(X, g * GRP + u)))
    own.left(NG)
    own.settle()


def experts0(nc, K, sem):
    names = """loaded asks gives xs_ready xt_psum xt_free mean_ready logits_psum exp_asks exp_gives index_ready weights_ready
               h_psum h_ready y_psum y_free asks_a gives_a asks_x gives_x loaded_next comp_psum""".split()
    (loaded, asks, gives, xs_ready, xt_psum, xt_free, mean_ready, logits_psum, exp_asks, exp_gives, index_ready, weights_ready,
     h_psum, h_ready, y_psum, y_free, asks_a, gives_a, asks_x, gives_x, loaded_next, comp_psum) = (sem("f0_" + n) for n in names)
    P, PS, A, XT = NODE_P, K.PS, K.arena, K.XT
    at = 0

    def piece(n):
        nonlocal at
        at += n
        return A[:, at - n:at]
    a = piece(NT * D)[:P].rearrange("p (t d) -> p t d", d=D)
    W1 = [piece(DK * F).rearrange("p (k f) -> p k f", k=DK) for _ in range(2)]
    W2 = [piece(FK * D).rearrange("p (f d) -> p f d", f=FK) for _ in range(2)]
    b1 = [piece(FK) for _ in range(2)]
    b2 = [piece(D)[:P] for _ in range(2)]
    HR = 5
    hs = [piece(FK * P).rearrange("p (f n) -> p f n", f=FK) for _ in range(HR)]
    gb = piece(2 * D)
    wr = piece(DK * E8).rearrange("p (k e) -> p k e", k=DK)
    br = piece(E8)[0:1, :]
    spread = piece(DK * 128).rearrange("p (k n) -> p k n", k=DK)
    means = piece(DK * NT).rearrange("p (k t) -> p k t", k=DK)
    mean = piece(DK)
    lg, ex, top = piece(E8), piece(E8), piece(E8)
    m1, m2, m3 = piece(1), piece(1), piece(1)
    wts = piece(2)
    topi = piece(E8).bitcast(U32)
    ef, ix = piece(2), piece(2)
    rowi, expi = piece(2).bitcast(I32), piece(2).bitcast(I32)
    partf = piece(1)
    K.relW = A[:, ARENA - DK * E8 * D:ARENA].rearrange("p (k n) -> p k n", k=DK)
    assert at <= ARENA - DK * E8 * D
    IC = STEPS + RING - TAIL
    Gf = K.G[:].rearrange("p s d -> p (s d)")
    basis = Gf[:, 0:4 * DK * D].rearrange("p (b k n) -> p b k n", b=4, k=DK)
    K.srcf = srcf = Gf[:, 4 * DK * D:4 * DK * D + IC]
    comp, comp_row = Gf[:, 4 * DK * D + IC:4 * DK * D + IC + 32], Gf[0:1, 4 * DK * D + IC + 32:4 * DK * D + IC + 64]
    typf = K.ys[:].rearrange("p s d -> p (s d)")[:, 0:IC]
    ins = K.ins
    loads_next = [(basis[:, b], ins["basis"][b * D:(b + 1) * D, :].rearrange("(k p) n -> p k n", p=128)) for b in range(4)]
    loads_next += [(comp_row, ins["comp"]), (srcf.bitcast(I32), ins["src"]), (typf.bitcast(I32), ins["etype"])]
    loads = [(gb, ins["gamma_beta0"].broadcast_to([128, 2 * D])), (wr, ins["ffn0_Wr"].rearrange("(k p) e -> p k e", p=128)),
             (br, ins["ffn0_br"])]
    base = list(K.landed_total)
    CAP = -(-N * 5 // (4 * E8))
    with nc.Block() as block:
        @block.sync
        def _(sp):
            for dst, src in loads:
                sp.dma_start(dst, src).then_inc(loaded, 16)
            for dst, src in loads_next:
                sp.dma_start(dst, src).then_inc(loaded_next, 16)

        @block.gpsimd
        def _(pool):
            pool.wait_ge(index_ready, 1)
            s = 0
            for e in range(2):
                for dst, table, index, parts in ((W1[e].rearrange("p k f -> p (k f)"), ins["ffn0_W1"], rowi, 128),
                                                 (W2[e].rearrange("p f d -> p (f d)"), ins["ffn0_W2"], rowi, 128),
                                                 (b1[e], ins["ffn0_b1"], rowi, 128), (b2[e], ins["ffn0_b2"], expi, P)):
                    nc.gpsimd.indirect_dma_start(dst, None, table, bass.IndirectOffsetOnAxis(ap=index[:parts, e:e + 1], axis=0)
                                                 ).then_inc(K.landed[s], 16)
                    s += 1

        @block.scalar
        def _(act):
            act.wait_ge(asks, 1)
            nc.scalar.activation(K.std[:P], K.t3[:P], ACT.Sqrt).then_inc(gives, 1)
            act.sem_inc(xt_free, GRP)
            with act.Fori(0, NG) as g:
                for u in range(GRP):
                    t = g * GRP + u
                    hold(act, K, xt_psum, t + 1)
                    for k in range(DK):
                        last = nc.scalar.activation(XT[:, k, bass.ds(t * P, P)], PS[:, u % 4, k * P:(k + 1) * P], ACT.Copy,
                                                    accum_out=means[:, k, bass.ds(t, 1)])
                    last.then_inc(xt_free, 1)
            for n in range(3):
                act.wait_ge(exp_asks, n + 1)
                src, dst = ((lg, ex), (lg, ex), (m2, m3))[n]
                nc.scalar.activation(dst, src, ACT.Exp).then_inc(exp_gives, 1)
            act.wait_ge(weights_ready, 1)

            def root(asks_, gives_, g):
                act.wait_ge(asks_, g + 1)
                nc.scalar.activation(K.std[:P, 0:GRP], K.t3[:P, 0:GRP], ACT.Sqrt).then_inc(gives_, 1)

            def group(g, first):
                for u in range(GRP):
                    for e in range(2):
                        j = 2 * u + e
                        act.wait_ge(h_psum, g * (2 * GRP) + j + 1)
                        if not (first and u < 2):
                            act.wait_ge(y_psum, g * GRP + u - 1)
                        for f in range(FK):
                            last = nc.scalar.activation(hs[j % HR][:, f, :], PS[:, j % HR, f * P:(f + 1) * P], ACT.Gelu,
                                                        bias=b1[e][:, f:f + 1])
                        last.then_inc(h_ready, 1)
                    if u == 0 and not first:
                        root(asks_a, gives_a, g - 1)
                    if u == 2 and not first:
                        root(asks_x, gives_x, g - 1)
            group(0, True)
            with act.Fori(1, NG) as g:
                group(g, False)
            root(asks_a, gives_a, NG - 1)
            root(asks_x, gives_x, NG - 1)

        @block.tensor
        def _(pe):
            pe.wait_ge(loaded, 16 * len(loads))
            with pe.Fori(0, NG) as g:
                transposes(K, nc, pe, g, xs_ready, xt_psum, xt_free, 4)
            pe.wait_ge(loaded_next, 16 * len(loads_next))
            nc.tensor.matmul(PS[:, 5, 0:32], K.ones[0:1, :], comp_row, start=True, stop=True).then_inc(comp_psum, 1)
            pe.wait_ge(mean_ready, 1)
            for k in range(DK):
                nc.tensor.matmul(PS[:, 6, 0:E8], spread[:, k, :], wr[:, k, :], start=k == 0, stop=False)
            nc.tensor.matmul(PS[:, 6, 0:E8], K.ones[0:1, :], br, start=False, stop=True).then_inc(logits_psum, 1)
            pe.wait_ge(weights_ready, 1)

            def hidden(g, u):
                for e in range(2):
                    j = 2 * u + e
                    pe.wait_ge(h_ready, g * (2 * GRP) + j + 1)
                    for f in range(FK):
                        for k in range(DK):
                            last = nc.tensor.matmul(PS[:, j % HR, f * P:(f + 1) * P], W1[e][:, k, f * 128:(f + 1) * 128],
                                                    XT[:, k, bass.ds((g * GRP + u) * P, P)], start=k == 0, stop=k == DK - 1)
                    last.then_inc(h_psum, 1)

            def output(g, u):
                pe.wait_ge(h_ready, g * (2 * GRP) + 2 * u + 2 + HR)
                pe.wait_ge(y_free, free(g, u, 3))
                for e in range(2):
                    for f in range(FK):
                        last = nc.tensor.matmul(PS[:P, 5 + u % 3, 0:D], hs[(2 * u + e) % HR][:, f, :], W2[e][:, f, :],
                                                start=e == 0 and f == 0, stop=e == 1 and f == FK - 1)
                last.then_inc(y_psum, 1)
            pe.sem_inc(h_ready, HR)
            with pe.Fori(0, NG) as g:
                for u in range(GRP):
                    hidden(g, u)
                    if u:
                        output(g, u - 1)
                output(g, GRP - 1)

        @block.vector
        def _(v):
            own = K.own_v
            own.eng = v
            link = own.link
            norm_stats(nc, K, v, own, asks, gives)
            link(nc.vector.tensor_copy(partf, K.parti[:]))
            with v.Fori(0, NG) as g:
                normalise(K, nc, v, g, xt_free, xs_ready)
            v.wait_ge(xt_free, NT + GRP)
            link(nc.vector.tensor_reduce(mean, means, AX, ALU.add))
            link(nc.vector.tensor_scalar(mean, mean, 1.0 / N, None, ALU.mult))
            for k in range(DK):
                link(nc.vector.tensor_scalar(spread[:, k, :], K.ones[:], mean[:, k:k + 1], None, ALU.mult))
            v.wait_ge(comp_psum, 1)
            link(nc.vector.tensor_copy(comp, PS[:, 5, 0:32]))
            v.sem_inc(mean_ready, 1)
            v.wait_ge(logits_psum, 1)

            def softmax(n, src):
                link(nc.vector.tensor_reduce(m1, src, AX, ALU.max))
                link(nc.vector.tensor_scalar(lg, src, m1, None, ALU.subtract))
                v.sem_inc(exp_asks, 1)
                v.wait_ge(exp_gives, n)
                link(nc.vector.tensor_reduce(m1, ex, AX, ALU.add))
                link(nc.vector.reciprocal(m1, m1))
                link(nc.vector.tensor_scalar(ex, ex, m1, None, ALU.mult))
            softmax(1, PS[:, 6, 0:E8])
            link(nc.vector.tensor_scalar(top, ex, float(N), None, ALU.mult))
            link(nc.vector.reciprocal(top, top))
            link(nc.vector.tensor_scalar(top, top, float(CAP), 1.0, ALU.mult, ALU.min))
            link(nc.vector.tensor_tensor(lg, ex, top, ALU.mult))
            softmax(2, lg)
            link(nc.vector.max(top, ex))
            link(nc.vector.max_index(topi, top, ex))
            link(nc.vector.tensor_copy(ef, topi[:, 0:2]))
            link(nc.vector.tensor_copy(expi, ef))
            link(nc.vector.tensor_scalar(ix, ef, 128.0, partf, ALU.mult, ALU.add))
            link(nc.vector.tensor_copy(rowi, ix))
            v.sem_inc(index_ready, 1)
            link(nc.vector.tensor_tensor(m2, top[:, 1:2], top[:, 0:1], ALU.subtract))
            v.sem_inc(exp_asks, 1)
            v.wait_ge(exp_gives, 3)
            link(nc.vector.tensor_scalar(m1, m3, 1.0, None, ALU.add))
            link(nc.vector.reciprocal(wts[:, 0:1], m1))
            link(nc.vector.tensor_tensor(wts[:, 1:2], wts[:, 0:1], m3, ALU.mult))
            for s in range(8):
                v.wait_ge(K.landed[s], base[s] + 16)
            for e in range(2):
                link(nc.vector.tensor_scalar(W2[e], W2[e], wts[:, e:e + 1], None, ALU.mult))
                link(nc.vector.tensor_scalar(b2[e], b2[e], wts[:P, e:e + 1], None, ALU.mult))
            link(nc.vector.tensor_tensor(b2[0], b2[0], b2[1], ALU.add))
            v.sem_inc(weights_ready, 1)
            v.sem_inc(y_free, GRP)
            for b in range(4):
                for r in range(E8):
                    w, f = K.relW[:, :, r * D:(r + 1) * D], comp[:, r * 4 + b:r * 4 + b + 1]
                    if b == 0:
                        own.step(nc.vector.tensor_scalar(w, basis[:, b], f, None, ALU.mult))
                    else:
                        own.step(nc.vector.scalar_tensor_tensor(w, basis[:, b], f, w, ALU.mult, ALU.add))
                own.settle()
            v.wait_ge(loaded_next, 16 * len(loads_next))
            link(nc.vector.tensor_copy(srcf, srcf.bitcast(I32)))
            link(nc.vector.tensor_copy(typf, typf.bitcast(I32)))
            link(nc.vector.scalar_tensor_tensor(srcf, srcf, float(E8), typf, ALU.mult, ALU.add))
            link(nc.vector.tensor_copy(srcf.bitcast(I32), srcf))
            group_rows = lambda r: r.unsqueeze(1).broadcast_to([P, GRP, D])

            def experts_sum(g, first):
                tiles = bass.ds(g * GRP, GRP)
                for u in range(GRP):
                    t = g * GRP + u
                    own.step(nc.vector.tensor_scalar(tile_of(a, t), tile_of(K.X[:P], t), col(K.rstd, t), col(K.nmr, t), ALU.mult, ALU.add))
                hold(v, K, own.sem, own.done)
                own.step(nc.vector.tensor_tensor(a[:, tiles, :], a[:, tiles, :], group_rows(b2[0]), ALU.add))
                own.step(nc.vector.tensor_tensor(K.X[:P, tiles, :], K.X[:P, tiles, :], group_rows(gb[:P, D:2 * D]), ALU.add))
                if not first:
                    normed_sum(g - 1)
                for u in range(GRP):
                    t = g * GRP + u
                    hold(v, K, own.sem, own.done)
                    hold(v, K, y_psum, t + 1)
                    nc.vector.tensor_tensor(tile_of(a, t), tile_of(a, t), PS[:P, 5 + u % 3, 0:D], ALU.add).then_inc(y_free, 1)
                for u in range(GRP):
                    t = g * GRP + u
                    hold(v, K, y_free, t + 1 + GRP)
                    own.step(nc.vector.bn_stats(K.S[:P, bass.ds(t, 1), :], tile_of(a, t)))
                own.settle()
                variances(nc, K, own, tiles, GRP, asks_a)

            def normed_sum(g):
                tiles = bass.ds(g * GRP, GRP)
                scales(nc, K, v, own, tiles, GRP, gives_a, g + 1)
                for u in range(GRP):
                    t = g * GRP + u
                    own.step(nc.vector.tensor_scalar(tile_of(a, t), tile_of(a, t), col(K.rstd, t), col(K.nmr, t), ALU.mult, ALU.add))
                hold(v, K, own.sem, own.done)
                own.step(nc.vector.tensor_tensor(a[:, tiles, :], a[:, tiles, :], group_rows(gb[:P, 0:D]), ALU.mult))
                hold(v, K, own.sem, own.done)
                own.step(nc.vector.tensor_tensor(K.X[:P, tiles, :], K.X[:P, tiles, :], a[:, tiles, :], ALU.add))
                hold(v, K, own.sem, own.done)
                for u in range(GRP):
                    t = g * GRP + u
                    own.step(nc.vector.bn_stats(K.S[:P, bass.ds(t, 1), :], tile_of(K.X[:P], t)))
                own.settle()
                variances(nc, K, own, tiles, GRP, asks_x)
                scales(nc, K, v, own, tiles, GRP, gives_x, g + 1)
            at_first = own.done
            experts_sum(0, True)
            per_sum = own.done - at_first
            per_normed = 2 + GRP + 2 + GRP + 5 + 2
            with v.Fori(1, NG) as g:
                own.loop(g, 1, per_sum + per_normed)
                experts_sum(g, False)
            own.left(NG - 1)
            normed_sum(NG - 1)
    for s in range(8):
        K.landed_total[s] += 16


def relations(nc, K, sem):
    names = "empty_ready xs_ready xt_psum xt_free x_staged act_free dve_free act_full index_stored staged_free".split()
    (empty_ready, xs_ready, xt_psum, xt_free, x_staged, act_free, dve_free, act_full, index_stored, staged_free) = (
        sem("r_" + n) for n in names)
    chunk_psum = [sem(f"r_chunk_psum{c}") for c in range(4)]
    stored = [sem(f"r_stored{u}") for u in range(GRP)]
    P, PS, A, XT = NODE_P, K.PS, K.arena, K.XT
    RW = E8 * D
    W = K.relW
    H = A[:P, 0:GRP * RW].rearrange("p (s n) -> p s n", s=GRP)
    assert GRP * RW <= ARENA - DK * RW
    empty = K.ys[:].rearrange("p s d -> p (s d)")[:, 0:RING_T * ROW].rearrange("p (s d) -> p s d", d=ROW)

    def groups(eng, group):
        group(0, True, False)
        with eng.Fori(1, NG - 1) as g:
            group(g, False, False)
        group(NG - 1, False, True)

    with nc.Block() as block:
        @block.sync
        def _(sp):
            sp.wait_ge(empty_ready, RING_T)
            for s in range(RING_T):
                sp.dma_start(K.slots.rearrange("(a s p) d -> p a s d", s=RING_T, p=BLOCK)[:, :, s, :],
                             empty[:, s:s + 1, :].broadcast_to([BLOCK, SLOT_BLOCKS // RING_T, ROW])).then_inc(K.slots_empty, 16)
            sp.dma_start(K.index1, K.srcf.bitcast(I32)).then_inc(index_stored, 16)
            with sp.Fori(0, NG) as g:
                for u in range(GRP):
                    t = g * GRP + u
                    sp.wait_ge(act_full, t + 1)
                    sp.wait_ge(dve_free, 1 + t)
                    sp.dma_start(K.htab.rearrange("(p t r) d -> p t (r d)", t=NT, r=E8)[:, bass.ds(t, 1), :].rearrange("p a n -> p (a n)"),
                                 H[:, u, :]).then_inc(stored[u], 16)
            for u in range(GRP):
                sp.wait_ge(stored[u], 16 * NG)
            sp.wait_ge(index_stored, 16)
            stage_first_indices(nc, K, sp, K.index1)

        @block.scalar
        def _(act):
            def staged(t, u):
                hold(act, K, xt_psum, t + 1)
                pt = PS[:, u % 2, 0:DK * P].rearrange("p (k n) -> p k n", k=DK)
                nc.scalar.copy(K.xTs[:, u], pt).then_inc(x_staged, 1)
                nc.scalar.copy(XT[:, :, bass.ds(t * P, P)], pt).then_inc(xt_free, 1)

            def group(g, first, last):
                for u in range(GRP):
                    t = g * GRP + u
                    if not first:
                        act.wait_ge(stored[u], g * 16)
                    for c in range(2):
                        act.wait_ge(chunk_psum[c], t + 1)
                        copied = nc.scalar.copy(H[:, u, c * 512:(c + 1) * 512], PS[:P, 2 + c, :])
                        copied.then_inc(act_free if c == 0 else act_full, 1)
                    if not last:
                        act.wait_ge(chunk_psum[3], t + 1)
                        staged(t + GRP, u)
            for u in range(GRP):
                staged(u, u)
            groups(act, group)

        @block.tensor
        def _(pe):
            def transposed(t, u, start):
                pe.wait_ge(xs_ready, t + 1)
                if not start:
                    pe.wait_ge(xt_free, t if u == 0 else t - 1)
                for k in range(DK):
                    last_k = nc.tensor.transpose(PS[:, u % 2, k * P:(k + 1) * P], K.xs[:P, u, k * 128:(k + 1) * 128], K.ident[:P, :P])
                last_k.then_inc(xt_psum, 1)

            def group(g, first, last):
                for u in range(GRP):
                    t = g * GRP + u
                    pe.wait_ge(x_staged, t + 1)
                    for c in range(4):
                        if not (first and u == 0):
                            pe.wait_ge((act_free, act_full, staged_free, dve_free)[c], t)
                        for k in range(DK):
                            last_k = nc.tensor.matmul(PS[:P, 2 + c, :], K.xTs[:, u, k, :], W[:, k, c * 512:(c + 1) * 512], start=k == 0, stop=k == DK - 1)
                        last_k.then_inc(chunk_psum[c], 1)
                    if not last:
                        transposed(t + GRP, u, False)
            for u in range(GRP):
                transposed(u, u, u < 2)
            groups(pe, group)

        @block.vector
        def _(v):
            def normalised(t, u):
                nc.vector.tensor_scalar(K.xs[:P, u], tile_of(K.X[:P], t), col(K.rstd, t), col(K.nmr, t), ALU.mult, ALU.add).then_inc(xs_ready, 1)

            def group(g, first, last):
                for u in range(GRP):
                    t = g * GRP + u
                    if not last:
                        hold(v, K, xt_psum, t + 1)
                        normalised(t + GRP, u)
                    if not first:
                        v.wait_ge(stored[u], g * 16)
                    for c in (2, 3):
                        v.wait_ge(chunk_psum[c], t + 1)
                        nc.vector.tensor_copy(H[:, u, c * 512:(c + 1) * 512], PS[:P, 2 + c, :]).then_inc(staged_free if c == 2 else dve_free, 1)
            for u in range(GRP):
                normalised(u, u)
            own = K.own_v
            own.eng = v
            own.link(nc.vector.memset(empty, 0.0))
            own.link(nc.vector.tensor_copy(K.nrm[:, 4:5], K.parti[:]))
            for s in range(RING_T):
                nc.vector.tensor_scalar(empty[:, s, D:ROW].bitcast(I32), K.nrm[:, 4:5], float(2 * N + s * BLOCK), None, ALU.add).then_inc(empty_ready, 1)
            groups(v, group)


def gather1_mix1(nc, K, sem):
    L = Pass(K, sem, "sum", K.htab, K.index1, K.keep, ALU.mult, ALU.add, K.lane_keep, 0.0)
    names = """loaded x_staged kq_psum kq_free v_psum v_free max_ready exp_ready kT_psum kT_free acc_free ctx_done
               ctx_ready ctxT_psum ctxT_ready w_psum end_weights q_staged ae_psum ae_free mix_added""".split()
    (loaded, x_staged, kq_psum, kq_free, v_psum, v_free, max_ready, exp_ready, kT_psum, kT_free, acc_free, ctx_done,
     ctx_ready, ctxT_psum, ctxT_ready, w_psum, end_weights, q_staged, ae_psum, ae_free, mix_added) = (
        sem("m1_" + n) for n in names)
    c = carry_names(sem, "c1_")
    P, PS, A, XT = NODE_P, K.PS, K.arena, K.XT
    HEADS, HD = 4, 32
    at = 0

    def piece(n):
        nonlocal at
        at += n
        return A[:, at - n:at]
    KQ = piece(2 * N).rearrange("p (a n) -> p a n", a=2)
    V = piece(NT * 128)[:P].rearrange("p (t e) -> p t e", e=128)
    wqkv = piece(DK * 384).rearrange("p (k n) -> p k n", k=DK)
    wout, Wmix, ctx, ctxT, mask = piece(D), piece(D), piece(128), piece(128), piece(128)
    Wloop = piece(DK * D).rearrange("p (k n) -> p k n", k=DK)
    row1, beta_row = piece(2 * D)[0:1, :], piece(D)[0:1, :]
    K.trail = piece(DK * (1 + LANES)).rearrange("p (k n) -> p k n", k=DK)
    kmax, ksum, kfac = piece(1), piece(NT), piece(1)
    K.own_part = piece(NT * D)[:P].rearrange("p (t d) -> p t d", d=D)
    assert at <= ARENA
    ins = K.ins
    loads = [(wqkv, ins["mix1_qkv"].rearrange("(k p) n -> p k n", p=128)), (wout, ins["mix1_out"]),
             (Wloop, ins["loop_w"].rearrange("(k p) n -> p k n", p=128)), (row1[:, 0:D], ins["h_bias"]),
             (row1[:, D:2 * D], ins["mix1_bout"]), (beta_row, ins["gamma_beta1"][:, D:2 * D])]
    with nc.Block() as block:
        @block.sync
        def _(sp):
            for dst, src in loads:
                sp.dma_start(dst, src).then_inc(loaded, 16)
            gather_sync(nc, K, sp, L)
            carry_sync(nc, K, sp, L, c)

        @block.gpsimd
        def _(pool):
            gather_pool(nc, K, pool, L)
            carry_pool(nc, K, pool, L, c)

        @block.scalar
        def _(act):
            act.sem_inc(kq_free, GRP)
            act.sem_inc(v_free, GRP)
            act.sem_inc(kT_free, GRP)
            with act.Fori(0, NG) as g:
                for u in range(GRP):
                    nc.scalar.copy(K.xTs[:, u], XT[:, :, bass.ds((g * GRP + u) * P, P)]).then_inc(x_staged, 1)
                for u in range(GRP):
                    t = g * GRP + u
                    hold(act, K, kq_psum, t + 1)
                    nc.scalar.copy(KQ[:, :, bass.ds(t * P, P)], PS[:, u, 0:2 * P].rearrange("p (a n) -> p a n", a=2)).then_inc(kq_free, 1)
                    hold(act, K, v_psum, t + 1)
                    nc.scalar.copy(tile_of(V, t), PS[:P, 5 + u % 3, 0:128]).then_inc(v_free, 1)
            act.wait_ge(max_ready, 1)
            with act.Fori(0, NG) as g:
                for u in range(GRP):
                    t = g * GRP + u
                    hold(act, K, kT_free, t + 1)
                    nc.scalar.activation(K.ys[:, u, 0:P], KQ[:, 1, bass.ds(t * P, P)], ACT.Exp, bias=kmax,
                                         accum_out=ksum[:, bass.ds(t, 1)]).then_inc(exp_ready, 1)
                for u in range(GRP):
                    t = g * GRP + u
                    act.wait_ge(kT_psum, t + 1)
                    act.wait_ge(acc_free, t + 1)
                    nc.scalar.copy(K.xs[:P, u, 0:128], PS[:P, u % 3, 0:128]).then_inc(kT_free, 1)
            act.sem_inc(ae_free, GRP)
            with act.Fori(0, NG) as g:
                for u in range(GRP):
                    t = g * GRP + u
                    hold(act, K, ae_free, t + 1)
                    nc.scalar.copy(K.xTs[:, u], XT[:, :, bass.ds(t * P, P)]).then_inc(x_staged, 1)
                    nc.scalar.copy(K.ys[:, u, 128:128 + P], KQ[:, 0, bass.ds(t * P, P)]).then_inc(q_staged, 1)
                for u in range(GRP):
                    t = g * GRP + u
                    hold(act, K, mix_added, t + 1)
                    nc.scalar.copy(tile_of(K.own_part, t), PS[:P, u, 0:D]).then_inc(ae_free, 1)

        @block.tensor
        def _(pe):
            pe.wait_ge(loaded, 16 * len(loads))
            with pe.Fori(0, NG) as g:
                for u in range(GRP):
                    t = g * GRP + u
                    pe.wait_ge(x_staged, t + 1)
                    pe.wait_ge(kq_free, t + 1)
                    for a in range(2):
                        for k in range(DK):
                            last = nc.tensor.matmul(PS[:, u, a * P:(a + 1) * P], wqkv[:, k, a * 128:(a + 1) * 128],
                                                    K.xTs[:, u, k, :], start=k == 0, stop=k == DK - 1)
                    last.then_inc(kq_psum, 1)
                    pe.wait_ge(v_free, free(g, u, 3))
                    for k in range(DK):
                        last = nc.tensor.matmul(PS[:P, 5 + u % 3, 0:128], K.xTs[:, u, k, :], wqkv[:, k, 256:384], start=k == 0, stop=k == DK - 1)
                    last.then_inc(v_psum, 1)
            pe.wait_ge(kq_free, NT + GRP)
            pe.sem_inc(acc_free, GRP)
            nc.tensor.matmul(PS[:, 4, 0:128], K.zeros[:], K.ones[:], start=True, stop=False)
            with pe.Fori(0, NG) as g:
                for u in range(GRP):
                    t = g * GRP + u
                    pe.wait_ge(exp_ready, t + 1)
                    pe.wait_ge(kT_free, free(g, u, 3))
                    nc.tensor.transpose(PS[:P, u % 3, 0:128], K.ys[:, u, 0:P], K.ident[:]).then_inc(kT_psum, 1)
                for u in range(GRP):
                    t = g * GRP + u
                    pe.wait_ge(kT_free, t + 1 + GRP)
                    nc.tensor.matmul(PS[:, 4, 0:128], K.xs[:P, u, 0:128], tile_of(V, t), start=False, stop=False).then_inc(acc_free, 1)
            nc.tensor.matmul(PS[:, 4, 0:128], K.zeros[:], K.ones[:], start=False, stop=True).then_inc(ctx_done, 1)
            pe.wait_ge(ctx_ready, 1)
            nc.tensor.transpose(PS[:, 5, 0:128], ctx, K.ident[:]).then_inc(ctxT_psum, 1)
            pe.wait_ge(ctxT_ready, 1)
            nc.tensor.matmul(PS[:, 6, 0:D], ctxT, wout, start=True, stop=True).then_inc(w_psum, 1)
            pe.wait_ge(end_weights, 1)
            with pe.Fori(0, NG) as g:
                for u in range(GRP):
                    t = g * GRP + u
                    pe.wait_ge(ae_free, t + 1)
                    nc.tensor.matmul(PS[:P, u, :], K.ones[0:1, 0:P], row1, start=True, stop=False)
                    pe.wait_ge(x_staged, t + 1 + NT)
                    for k in range(DK):
                        nc.tensor.matmul(PS[:P, u, 0:D], K.xTs[:, u, k, :], Wloop[:, k, :], start=False, stop=False)
                    pe.wait_ge(q_staged, t + 1)
                    nc.tensor.matmul(PS[:P, u, D:2 * D], K.ys[:, u, 128:128 + P], Wmix, start=False, stop=True).then_inc(ae_psum, 1)
            pe.wait_ge(ae_free, NT + GRP)
            carry_tensor(nc, K, pe, L, c)

        @block.vector
        def _(v):
            own = K.own_v
            own.eng = v
            link = own.link
            link(nc.vector.memset(K.G[:, RING - 1, :], 0.0))
            link(nc.vector.memset(mask, 0.0))
            for h in range(HEADS):
                link(nc.vector.memset(mask[h * HD:(h + 1) * HD, h * HD:(h + 1) * HD], 1.0))
            gather_fold(nc, K, v, L, 0, RING, True)
            with v.Fori(1, 12) as i:
                gather_fold(nc, K, v, L, i, RING, False)
            v.wait_ge(kq_free, NT + GRP)
            link(nc.vector.tensor_reduce(kmax, KQ[:, 1, :], AX, ALU.max))
            nc.vector.tensor_scalar(kmax, kmax, -1.0, None, ALU.mult).then_inc(max_ready, 1)
            with v.Fori(12, BESIDE) as i:
                gather_fold(nc, K, v, L, i, RING, False)
            v.wait_ge(ctx_done, 1)
            nc.vector.tensor_tensor(ctx, PS[:, 4, 0:128], mask, ALU.mult).then_inc(ctx_ready, 1)
            v.wait_ge(kT_free, NT + GRP)
            link(nc.vector.tensor_reduce(kfac, ksum, AX, ALU.add))
            link(nc.vector.reciprocal(kfac, kfac))
            link(nc.vector.tensor_scalar(kfac, kfac, HD ** -0.5, None, ALU.mult))
            v.wait_ge(ctxT_psum, 1)
            nc.vector.tensor_copy(ctxT, PS[:, 5, 0:128]).then_inc(ctxT_ready, 1)
            v.wait_ge(w_psum, 1)
            link(nc.vector.tensor_scalar(Wmix, PS[:, 6, 0:D], kfac, None, ALU.mult))
            for k in range(DK):
                w = Wloop[:, k, k * 128:(k + 1) * 128]
                link(nc.vector.tensor_tensor(w, w, K.ident[:], ALU.add))
            link(nc.vector.tensor_tensor(row1[:, D:2 * D], row1[:, D:2 * D], beta_row, ALU.add))
            v.sem_inc(end_weights, 1)
            with v.Fori(0, NG) as g:
                def mix_part(s):
                    u, X = s // 3, K.X[:P]
                    if s % 3 == 0 and u < GRP:
                        t = g * GRP + u
                        v.wait_ge(ae_psum, t + 1)
                        nc.vector.tensor_tensor(tile_of(X, t), tile_of(X, t), PS[:P, u, D:2 * D], ALU.add).then_inc(mix_added, 1)
                gather_fold(nc, K, v, L, g + BESIDE, RING, False, mix_part)
            with v.Fori(BESIDE + NG, ROUNDS) as i:
                gather_fold(nc, K, v, L, i, RING, False)
            gather_fold(nc, K, v, L, ROUNDS, TAIL, False)
            carry_vector(nc, K, v, own, L, c)
    for s in range(RING):
        K.landed_total[s] += 16 * (ROUNDS + (s < TAIL) + 2 * (s == FIX))


def ends1(nc, K, sem):
    names = "loaded m_used gelu_done asks gives stats_ready normed".split()
    loaded, m_used, gelu_done, asks, gives, stats_ready, normed = (sem("e1_" + n) for n in names)
    P, G, a = NODE_P, K.G, K.own_part
    base = list(K.landed_total)
    gamma = K.wphi[:, 0, :]
    with nc.Block() as block:
        @block.sync
        def _(sp):
            sp.dma_start(gamma, K.ins["gamma_beta1"][:, 0:D].broadcast_to([128, D])).then_inc(loaded, 16)

        @block.gpsimd
        def _(pool):
            gather_ends(nc, K, pool, m_used)

        @block.scalar
        def _(act):
            with act.Fori(0, NG) as g:
                for u in range(GRP):
                    t = g * GRP + u
                    hold(act, K, m_used, t + 1)
                    nc.scalar.activation(tile_of(a, t), K.xs[:P, u], ACT.Gelu).then_inc(gelu_done, 1)
            act.wait_ge(asks, 1)
            nc.scalar.activation(K.std[:P], K.t3[:P], ACT.Sqrt).then_inc(gives, 1)
            add_normed_scalar(nc, K, act, a, stats_ready, normed)

        @block.vector
        def _(v):
            own = K.own_v
            own.eng = v
            v.wait_ge(loaded, 16)
            v.sem_inc(gelu_done, GRP)
            with v.Fori(0, NG) as g:
                own.loop(g, 0, GRP)
                for u in range(GRP):
                    t = g * GRP + u
                    hold(v, K, K.landed[u], g * 16 + 16 + base[u])
                    hold(v, K, gelu_done, t + 1)
                    nc.vector.tensor_tensor(K.xs[:P, u], G[:P, u, :], tile_of(a, t), ALU.add).then_inc(m_used, 1)
                for u in range(GRP):
                    t = g * GRP + u
                    hold(v, K, gelu_done, t + 1 + GRP)
                    own.step(nc.vector.bn_stats(K.S[:P, bass.ds(t, 1), :], tile_of(a, t)))
            own.left(NG)
            own.settle()
            norm_stats(nc, K, v, own, asks, gives)
            v.sem_inc(stats_ready, 1)
            add_normed_vector(nc, K, v, own, a, gamma, normed)
    ends_taken(K)


def experts1(nc, K, sem):
    names = """loaded loaded_big consts asks gives xs_ready xt_psum xt_free br_psum lg_psum lg_free rows_kept
               exp_asks exp_gives picks_ready prefix_psum slots_ready rowT_ready w1_ready h_psum h_ready y_psum y_out
               first_added out_ready out_stored ids_ready""".split()
    (loaded, loaded_big, consts, asks, gives, xs_ready, xt_psum, xt_free, br_psum, lg_psum, lg_free, rows_kept,
     exp_asks, exp_gives, picks_ready, prefix_psum, slots_ready, rowT_ready, w1_ready, h_psum, h_ready, y_psum, y_out,
     first_added, out_ready, out_stored, ids_ready) = (sem("f1_" + n) for n in names)
    rows_in = [sem(f"f1_rows_in{u}") for u in range(TURN)]
    stored = [sem(f"f1_stored{u}") for u in range(TURN)]
    ys_in = [sem(f"f1_ys_in{g}") for g in range(NG)]
    P, PS = NODE_P, K.PS

    def pieces(buf):
        at = [0]

        def piece(n):
            at[0] += n
            assert at[0] <= buf.shape[1]
            return buf[:, at[0] - n:at[0]]
        return piece
    per_node = lambda a: a[:P].rearrange("p (t e) -> p t e", e=E8)
    piece = pieces(K.arena)
    W1_WORDS = DK * F + FK
    W1 = piece(E8 * W1_WORDS).rearrange("p (e n) -> p e n", e=E8)
    W2 = piece(E8 * FK * D).rearrange("p (e n) -> p e n", e=E8)
    b2 = piece(E8 * D).rearrange("p (e d) -> p e d", e=E8)
    wr = piece(DK * E8).rearrange("p (k e) -> p k e", k=DK)
    br, brB = piece(E8)[0:1, :], piece(E8)[:P]
    lgs, rank, pick1, pick2 = (per_node(piece(NT * E8)) for _ in range(4))
    block_cmp = piece(SLOT_BLOCKS * E8)[0:1].rearrange("p (j e) -> p j e", e=E8)
    piece = pieces(K.keep)
    PAD = 16
    scan = [piece((PAD + NT) * E8)[:P].rearrange("p (t e) -> p t e", e=E8) for _ in range(2)]
    rowf = piece(128)
    piece = pieces(K.pen)
    before, rowi = piece(128), piece(128).bitcast(I32)
    pos, picked = per_node(piece(NT * E8)), per_node(piece(NT * E8))
    EPAD = 4
    escan = [piece(EPAD + E8)[:P] for _ in range(2)]
    count, base_row, partf = piece(E8)[:P], piece(E8)[:P], piece(1)
    slotf = piece(NT)[:P]
    slot_i = K.ranki[:].rearrange("p t e -> p (t e)")[:P, 0:2 * NT].rearrange("p (k t) -> p k t", k=2)
    expert_f, expert_i = K.lane_pen[0:1, 0:SLOT_BLOCKS], K.edge_rows[0:1, 0, 0:SLOT_BLOCKS].bitcast(I32)
    gamma_beta = K.wphi[:].rearrange("p k n -> p (k n)")
    rows_node = K.XTraw[:P].rearrange("p (t d) -> p t d", d=ROW)
    ids = rows_node[:, :, D].bitcast(I32)
    rows = [K.XTraw[:, s * ROW:(s + 1) * ROW] for s in range(TURN)]
    ys_node = K.arena[:P, 0:2 * NT * D].rearrange("p (k t d) -> p k t d", k=2, d=D)
    G = K.G[:].rearrange("p s d -> p (s d)")
    w1 = [G[:, s * W1_WORDS:(s + 1) * W1_WORDS] for s in range(2)]
    hs = [G[:, 2 * W1_WORDS + s * F:2 * W1_WORDS + (s + 1) * F] for s in range(2)]
    xT = [K.xTs[:].rearrange("p u k n -> p (u k n)")[:, s * D:(s + 1) * D] for s in range(RING_T)]
    m1, m2, mi, ee = K.t1[:P], K.t2[:P], K.t3[:P], K.std[:P]
    scattered = K.landed[RING - 1]
    scattered_base = K.landed_total[RING - 1]
    ins = K.ins
    loads = [(wr, ins["ffn1_Wr"].rearrange("(k p) e -> p k e", p=128)), (br, ins["ffn1_br"]),
             (gamma_beta, ins["gamma_beta2"].broadcast_to([128, 2 * D]))]
    big = [(W1[:, :, 0:DK * F], ins["ffn1_W1"].rearrange("(e p) n -> p e n", p=128)),
           (W1[:, :, DK * F:W1_WORDS], ins["ffn1_b1"].rearrange("(e p) n -> p e n", p=128)),
           (W2, ins["ffn1_W2"].rearrange("(e p) n -> p e n", p=128)),
           (b2.rearrange("p e d -> p (e d)"), ins["ffn1_b2"].broadcast_to([128, E8 * D]))]
    spread = lambda c: c.unsqueeze(2).broadcast_to([P, NT, E8])
    spread_rows = lambda r: r.unsqueeze(1).broadcast_to([P, NT, E8])
    spread_group = lambda r: r[:P].unsqueeze(1).broadcast_to([P, GRP, D])

    def groups(eng, one):
        with eng.Fori(0, NG // 2) as h:
            one(h * 2, K.xs)
            one(h * 2 + 1, K.ys)
        one(NG - 1, K.xs)
    block_of = lambda table, j: table[bass.ds(j * BLOCK, BLOCK), :]
    TURNS = SLOT_BLOCKS // TURN

    def turns(eng, one):
        one(0, True, False)
        with eng.Fori(1, TURNS - 1) as i:
            one(i, False, False)
        one(TURNS - 1, False, True)

    with nc.Block() as block:
        @block.sync
        def _(sp):
            for dst, src in loads:
                sp.dma_start(dst, src).then_inc(loaded, 16)
            for dst, src in big:
                sp.dma_start(dst, src).then_inc(loaded_big, 16)
            sp.wait_ge(scattered, scattered_base + 16 * 2 * NT)
            for u in range(TURN):
                sp.dma_start(rows[u], block_of(K.slots, u)).then_inc(rows_in[u], 16)
            with sp.Fori(1, TURNS) as i:
                for u in range(TURN):
                    sp.wait_ge(stored[u], i * 16)
                    sp.dma_start(rows[u], block_of(K.slots, i * TURN + u)).then_inc(rows_in[u], 16)
            for u in range(TURN):
                sp.wait_ge(stored[u], 16 * TURNS)
            for g in range(NG):
                for k in range(2):
                    sp.dma_start(ys_node[:, k, g * GRP:(g + 1) * GRP, :],
                                 K.node_ys[k * N:(k + 1) * N, :].rearrange("(p t) d -> p t d", t=NT)[:, g * GRP:(g + 1) * GRP, :]
                                 ).then_inc(ys_in[g], 16)
            for g in range(NG):
                sp.wait_ge(out_ready, GRP * (g + 1))
                sp.dma_start(K.out3[:, g * GRP:(g + 1) * GRP, :], K.X[:P, g * GRP:(g + 1) * GRP, :]).then_inc(out_stored, 16)
            sp.wait_ge(out_stored, 16 * NG)

        @block.gpsimd
        def _(pool):
            nc.gpsimd.iota(K.ranki[:P], pattern=[[0, NT], [-1, E8]], base=E8, channel_multiplier=0).then_inc(consts, 1)
            nc.gpsimd.iota(rowi, pattern=[[1, 128]], base=0, channel_multiplier=0).then_inc(consts, 1)
            pool.wait_ge(rows_kept, NG)
            pool.wait_ge(K.slots_empty, 16 * RING_T)
            for k in range(2):
                pool.wait_ge(slots_ready, k + 1)
                pool.wait_ge(ids_ready, k + 1)
                for t in range(NT):
                    nc.gpsimd.indirect_dma_start(K.slots, bass.IndirectOffsetOnAxis(ap=slot_i[:, k, t:t + 1], axis=0),
                                                 rows_node[:, t, :], None).then_inc(scattered, 16)
            with pool.Fori(0, TURNS) as i:
                for u in range(TURN):
                    hold(pool, K, y_out, i * TURN + u + 1)
                    nc.gpsimd.indirect_dma_start(K.node_ys, bass.IndirectOffsetOnAxis(ap=rows[u][:, D:ROW].bitcast(I32), axis=0),
                                                 K.ys[:, u % RING_T, :], None).then_inc(stored[u], 16)

        @block.scalar
        def _(act):
            act.wait_ge(asks, 1)
            nc.scalar.activation(K.std[:P], K.t3[:P], ACT.Sqrt).then_inc(gives, 1)
            act.sem_inc(xt_free, GRP)

            def front(g, buf):
                for u in range(GRP):
                    t = g * GRP + u
                    act.wait_ge(lg_psum, t + 1)
                    act.wait_ge(xt_psum, t + 1 + GRP)
                    nc.scalar.copy(K.xTs[:, u].rearrange("p k n -> p (k n)"), PS[:, u % 4, 0:DK * P]).then_inc(xt_free, 1)
                hold(act, K, xs_ready, g + 1)
                nc.scalar.copy(rows_node[:, bass.ds(g * GRP, GRP), 0:D], buf[:P]).then_inc(rows_kept, 1)
            groups(act, front)
            act.wait_ge(exp_asks, 1)
            nc.scalar.activation(ee, m2, ACT.Exp).then_inc(exp_gives, 1)
            act.wait_ge(lg_free, NT + GRP)

            def transposed(j, u):
                act.wait_ge(xt_psum, NT + GRP + j + 1)
                nc.scalar.copy(xT[u % RING_T], PS[:, u % 2, 0:D]).then_inc(rowT_ready, 1)

            def one(i, first, last):
                for u in range(TURN):
                    j = i * TURN + u
                    if first and u == 0:
                        transposed(0, 0)
                    if not (last and u == TURN - 1):
                        transposed(j + 1, u + 1)
                    act.wait_ge(h_psum, j + 1)
                    if not (first and u < 2):
                        act.wait_ge(y_psum, j - 1)
                    for f in range(FK):
                        last_f = nc.scalar.activation(hs[u % 2][:, f * 128:(f + 1) * 128], PS[:, 2 + u % 2, f * 128:(f + 1) * 128], ACT.Gelu,
                                                      bias=w1[u % 2][:, DK * F + f:DK * F + f + 1])
                    last_f.then_inc(h_ready, 1)
            turns(act, one)

        @block.tensor
        def _(pe):
            pe.wait_ge(loaded, 16 * len(loads))
            nc.tensor.matmul(PS[:, 7, 0:E8], K.ones[0:1, :], br, start=True, stop=True).then_inc(br_psum, 1)
            pe.sem_inc(xt_psum, GRP)
            pe.sem_inc(lg_psum, GRP)

            def front(g, buf):
                pe.wait_ge(xs_ready, g + 1)
                for u in range(GRP):
                    pe.wait_ge(xt_free, free(g, u, 4))
                    for k in range(DK):
                        last_k = nc.tensor.transpose(PS[:, u % 4, k * P:(k + 1) * P], buf[:P, u, k * 128:(k + 1) * 128], K.ident[:P, :P])
                    last_k.then_inc(xt_psum, 1)
                for u in range(GRP):
                    t = g * GRP + u
                    pe.wait_ge(xt_free, t + 1 + GRP)
                    pe.wait_ge(lg_free, free(g, u, 3))
                    for k in range(DK):
                        last_k = nc.tensor.matmul(PS[:P, 4 + u % 3, 0:E8], K.xTs[:, u, k, :], wr[:, k, :], start=k == 0, stop=k == DK - 1)
                    last_k.then_inc(lg_psum, 1)
            groups(pe, front)
            pe.wait_ge(picks_ready, 1)
            nc.tensor.matmul(PS[:P, 7, 0:NT * E8], before[:P, 0:P], picked.rearrange("p t e -> p (t e)"), start=True, stop=True)
            nc.tensor.matmul(PS[:P, 7, NT * E8:2 * NT * E8], K.ones[:P, 0:P], picked.rearrange("p t e -> p (t e)"),
                             start=True, stop=True).then_inc(prefix_psum, 1)
            pe.wait_ge(slots_ready, 3)

            def transposed(i, u):
                s = u % TURN
                pe.wait_ge(rows_in[s], 16 * (i + 1 + u // TURN))
                if i is not None and not (isinstance(i, int) and i * TURN + u < 2):
                    pe.wait_ge(rowT_ready, i * TURN + u - 1)
                for k in range(DK):
                    last_k = nc.tensor.transpose(PS[:, u % 2, k * 128:(k + 1) * 128], rows[s][:, k * 128:(k + 1) * 128], K.ident[:])
                last_k.then_inc(xt_psum, 1)

            def output(j, u):
                e = pe.value_load(expert_i[0:1, bass.ds(j, 1)], min_val=0, max_val=E8 - 1)
                pe.wait_ge(h_ready, j + 1)
                if not (isinstance(j, int) and j < 2):
                    pe.wait_ge(y_out, j - 1)
                for f in range(FK):
                    last_f = nc.tensor.matmul(PS[:, 4 + u % 2, 0:D], hs[u % 2][:, f * 128:(f + 1) * 128],
                                              W2[:, bass.ds(e, 1), f * D:(f + 1) * D].rearrange("p a d -> p (a d)"), start=f == 0, stop=f == FK - 1)
                last_f.then_inc(y_psum, 1)

            def one(i, first, last):
                if first:
                    transposed(0, 0)
                for u in range(TURN):
                    j = i * TURN + u
                    if not (last and u == TURN - 1):
                        transposed(i, u + 1)
                    pe.wait_ge(rowT_ready, j + 1)
                    pe.wait_ge(w1_ready, j + 1)
                    if not (first and u < 2):
                        pe.wait_ge(h_ready, j - 1)
                    for f in range(FK):
                        for k in range(DK):
                            last_k = nc.tensor.matmul(PS[:, 2 + u % 2, f * 128:(f + 1) * 128], w1[u % 2][:, k * F + f * 128:k * F + (f + 1) * 128],
                                                      xT[u % RING_T][:, k * 128:(k + 1) * 128], start=k == 0, stop=k == DK - 1)
                    last_k.then_inc(h_psum, 1)
                    if not (first and u == 0):
                        output(j - 1, u + 1)
            turns(pe, one)
            output(SLOT_BLOCKS - 1, SLOT_BLOCKS - 1)

        @block.vector
        def _(v):
            own = K.own_v
            own.eng = v
            link = own.link
            norm_stats(nc, K, v, own, asks, gives)
            v.wait_ge(br_psum, 1)
            link(nc.vector.tensor_copy(brB, PS[:P, 7, 0:E8]))
            v.wait_ge(consts, 2)
            nc.vector.tensor_copy(ids, K.nodei[:P]).then_inc(ids_ready, 1)
            link(nc.vector.tensor_copy(rank, K.ranki[:P]))
            link(nc.vector.tensor_copy(rowf, rowi))
            link(nc.vector.tensor_copy(partf, K.parti[:]))
            link(nc.vector.tensor_scalar(before, rowf, partf, None, ALU.is_gt))
            v.wait_ge(loaded, 16 * len(loads))
            v.sem_inc(lg_free, GRP)
            def logits(g):
                for u in range(GRP):
                    hold(v, K, lg_psum, g * GRP + u + 1 + GRP)
                    nc.vector.tensor_tensor(tile_of(lgs, g * GRP + u), PS[:P, 4 + u % 3, 0:E8], brB, ALU.add).then_inc(lg_free, 1)

            def front(g, buf, first):
                if not first:
                    v.wait_ge(xt_psum, g * GRP)
                    hold(v, K, rows_kept, g - 1)
                for u in range(GRP):
                    t = g * GRP + u
                    own.step(nc.vector.tensor_scalar(buf[:P, u], tile_of(K.X[:P], t), col(K.rstd, t), col(K.nmr, t), ALU.mult, ALU.add))
                own.settle()
                own.link(nc.vector.tensor_tensor(buf[:P], buf[:P], spread_group(gamma_beta[:, 0:D]), ALU.mult))
                nc.vector.tensor_tensor(buf[:P], buf[:P], spread_group(gamma_beta[:, D:2 * D]), ALU.add).then_inc(xs_ready, 1)
            front(0, K.xs, True)
            front(1, K.ys, True)
            with v.Fori(1, NG // 2) as h:
                own.loop(h, 1, 2 * (GRP + 1))
                logits(h * 2 - 2)
                front(h * 2, K.xs, False)
                logits(h * 2 - 1)
                front(h * 2 + 1, K.ys, False)
            own.left(NG // 2 - 1)
            logits(NG - 3)
            front(NG - 1, K.xs, False)
            logits(NG - 2)
            logits(NG - 1)
            v.wait_ge(lg_free, NT + GRP)

            def largest(m, pick):
                link(nc.vector.tensor_reduce(m, lgs, AX, ALU.max))
                link(nc.vector.tensor_tensor(pick, lgs, spread(m), ALU.is_equal))
                link(nc.vector.tensor_tensor(pick, pick, rank, ALU.mult))
                link(nc.vector.tensor_reduce(mi, pick, AX, ALU.max))
                link(nc.vector.tensor_tensor(pick, rank, spread(mi), ALU.is_equal))
            largest(m1, pick1)
            link(nc.vector.scalar_tensor_tensor(lgs, pick1, -BIG, lgs, ALU.mult, ALU.add))
            largest(m2, pick2)
            nc.vector.tensor_tensor(picked, pick1, pick2, ALU.add).then_inc(picks_ready, 1)
            link(nc.vector.tensor_tensor(m2, m2, m1, ALU.subtract))
            v.sem_inc(exp_asks, 1)
            v.wait_ge(exp_gives, 1)
            link(nc.vector.tensor_scalar(m1, ee, 1.0, None, ALU.add))
            link(nc.vector.reciprocal(m1, m1))
            link(nc.vector.tensor_tensor(m2, m1, ee, ALU.mult))
            for b in scan:
                link(nc.vector.memset(b[:, 0:PAD, :], 0.0))
            for b in escan:
                link(nc.vector.memset(b[:, 0:EPAD], 0.0))
            v.wait_ge(prefix_psum, 1)
            in_tile = PS[:P, 7, NT * E8:2 * NT * E8].rearrange("p (t e) -> p t e", e=E8)
            link(nc.vector.tensor_copy(scan[0][:, PAD:, :], in_tile))
            for n, step in enumerate((1, 2, 4, 8, 16)):
                a, b = scan[n % 2], scan[(n + 1) % 2]
                link(nc.vector.tensor_tensor(b[:, PAD:, :], a[:, PAD:, :], a[:, PAD - step:PAD + NT - step, :], ALU.add))
            upto = scan[1]
            link(nc.vector.tensor_copy(count, upto[:, PAD + NT - 1, :]))
            link(nc.vector.tensor_scalar(slotf, rowf[:P, 0:NT], float(BLOCK), None, ALU.mult))
            link(nc.vector.tensor_tensor(lgs, spread_rows(count), spread(slotf), ALU.is_gt))
            link(nc.vector.tensor_reduce(escan[0][:, EPAD:], lgs.rearrange("p t e -> p e t"), AX, ALU.add))
            link(nc.vector.tensor_copy(count, escan[0][:, EPAD:]))
            for n, step in enumerate((1, 2, 4)):
                a, b = escan[n % 2], escan[(n + 1) % 2]
                link(nc.vector.tensor_tensor(b[:, EPAD:], a[:, EPAD:], a[:, EPAD - step:EPAD + E8 - step], ALU.add))
            blocks_upto = escan[1][:, EPAD:]
            link(nc.vector.tensor_tensor(base_row, blocks_upto, count, ALU.subtract))
            link(nc.vector.tensor_scalar(base_row, base_row, float(BLOCK), None, ALU.mult))
            link(nc.vector.tensor_tensor(pos, upto[:, PAD:, :], in_tile, ALU.subtract))
            link(nc.vector.tensor_tensor(pos, pos, PS[:P, 7, 0:NT * E8].rearrange("p (t e) -> p t e", e=E8), ALU.add))
            link(nc.vector.tensor_tensor(pos, pos, spread_rows(base_row), ALU.add))
            for k, pick in enumerate((pick1, pick2)):
                link(nc.vector.tensor_tensor(pick, pick, pos, ALU.mult))
                link(nc.vector.tensor_reduce(slotf, pick, AX, ALU.add))
                nc.vector.tensor_copy(slot_i[:, k, :], slotf).then_inc(slots_ready, 1)
                v.wait_ge(slots_ready, k + 1)
            link(nc.vector.tensor_tensor(block_cmp, blocks_upto[0:1].unsqueeze(1).broadcast_to([1, SLOT_BLOCKS, E8]),
                                         rowf[0:1, 0:SLOT_BLOCKS].unsqueeze(2).broadcast_to([1, SLOT_BLOCKS, E8]), ALU.is_le))
            link(nc.vector.tensor_reduce(expert_f, block_cmp, AX, ALU.add))
            link(nc.vector.tensor_scalar(expert_f, expert_f, float(E8 - 1), None, ALU.min))
            nc.vector.tensor_copy(expert_i, expert_f).then_inc(slots_ready, 1)
            v.wait_ge(scattered, scattered_base + 16 * NT)
            nc.vector.tensor_scalar(ids, K.node[:P], float(N), None, ALU.add).then_inc(ids_ready, 1)
            v.wait_ge(slots_ready, 3)
            v.wait_ge(loaded_big, 16 * len(big))

            def expert_of(j):
                return v.value_load(expert_i[0:1, bass.ds(j, 1)], min_val=0, max_val=E8 - 1)

            def weights(j, u):
                e = expert_of(j)
                nc.vector.tensor_copy(w1[u % 2], W1[:, bass.ds(e, 1), :].rearrange("p a n -> p (a n)")).then_inc(w1_ready, 1)

            def result(i, u):
                e = expert_of(i * TURN + u)
                hold(v, K, y_psum, i * TURN + u + 1)
                if u >= RING_T:
                    hold(v, K, stored[u - RING_T], i * 16 + 16)
                elif not (isinstance(i, int) and i == 0):
                    hold(v, K, stored[u + RING_T], i * 16)
                nc.vector.tensor_tensor(K.ys[:, u % RING_T, :], PS[:, 4 + u % 2, 0:D], b2[:, bass.ds(e, 1), :].rearrange("p a d -> p (a d)"),
                                        ALU.add).then_inc(y_out, 1)

            def one(i, first, last):
                if first:
                    weights(0, 0)
                for u in range(TURN):
                    j = i * TURN + u
                    if not (last and u == TURN - 1):
                        if not (first and u == 0):
                            hold(v, K, h_ready, j)
                        weights(j + 1, u + 1)
                    if u:
                        result(i, u - 1)
                    elif not first:
                        result(i - 1, TURN - 1)
            turns(v, one)
            result(TURNS - 1, TURN - 1)
            for g in range(NG):
                v.wait_ge(ys_in[g], 32)
                for k, (weight, done) in enumerate(((m1, first_added), (m2, out_ready))):
                    for t in range(g * GRP, (g + 1) * GRP):
                        if k:
                            v.wait_ge(first_added, t + 1)
                        nc.vector.scalar_tensor_tensor(K.X[:P, t, :], ys_node[:, k, t, :], weight[:, t:t + 1], K.X[:P, t, :],
                                                       ALU.mult, ALU.add).then_inc(done, 1)


def program(nc, out, ins):
    K = Names()
    ctx = ExitStack()
    with ctx:
        def sb(name, shape, dt=F32):
            return ctx.enter_context(nc.sbuf_tensor(name, shape, dt))

        def sem(name):
            return nc.alloc_semaphore(name)

        def dram(name, shape, dt=F32):
            return nc.dram_tensor(name, shape, dt).ap()

        K.ins = ins
        K.in_x, K.in_dst = ins["x"], ins["dst"]
        K.X = sb("X", [128, NT, D])
        K.XTraw = sb("XT", [128, NT * ROW])
        K.XT = K.XTraw[:, 0:DK * N].rearrange("p (k n) -> p k n", k=DK)
        K.G = sb("G", [128, RING, D])
        K.keep = sb("keep", [128, STEPS])
        K.pen = sb("pen", [128, STEPS])
        K.arena = sb("arena", [128, ARENA])
        K.xs = sb("xs", [128, GRP, D])
        K.xTs = sb("xTs", [128, GRP, DK, NODE_P])
        K.S = sb("S", [128, NT, 6])
        K.t1, K.t2, K.t3, K.std, K.rstd, K.nmr = (sb(n, [128, NT]) for n in ("t1", "t2", "t3", "std", "rstd", "nmr"))
        K.node, K.lane, K.inlane, K.cnt_le, K.cnt_lt = (sb(n, [128, NT]) for n in ("node", "lane", "inlane", "cnt_le", "cnt_lt"))
        K.q2sum, K.k2sum, K.q4sum, K.kscale, K.qscale = (sb(n, [128, NT]) for n in ("q2sum", "k2sum", "q4sum", "kscale", "qscale"))
        K.nrm, K.junk, K.neutral = sb("nrm", [128, 8]), sb("junk", [128, D]), sb("neutral", [1, D])
        K.zeros, K.ys = sb("zeros", [128, 128]), sb("ys", [128, GRP, D])
        K.ranki = sb("ranki", [128, NT, E8], I32)
        K.slots, K.node_ys = dram("slots", [SLOT_BLOCKS * BLOCK, ROW]), dram("node_ys", [2 * N + RING_T * BLOCK, D])
        K.slots_empty = sem("slots_empty")
        K.htab = dram("htab", [N * E8, D])
        K.index1 = dram("index1", [LANES, STEPS + RING - TAIL], I32)
        K.out3 = out.rearrange("(p t) d -> p t d", t=NT)
        K.index_sb = sb("index_sb", [128, RING], I32)
        K.nodei, K.lane_i, K.end_i = (sb(n, [128, NT], I32) for n in ("nodei", "lane_i", "end_i"))
        K.goes_on, K.first_i = sb("goes_on", [128, 4]), sb("first_i", [128, 1], I32)
        K.parti = sb("parti", [128, 1], I32)
        K.zero = sb("zero", [128, 1])
        K.ones, K.ident = sb("ones", [128, 128]), sb("ident", [128, 128])
        K.edge_rows = sb("edge_rows_sb", [128, 2, LANES])
        K.lane_keep, K.lane_pen = sb("lane_keep", [128, LANES]), sb("lane_pen", [128, LANES])
        K.wB, K.wphi, K.wtheta = (sb(n, [128, DK, D]) for n in ("wB", "wphi", "wtheta"))
        K.PS = ctx.enter_context(nc.psum_tensor("PS", [128, 8, 512], F32))
        K.pT = lambda u: K.PS[:, u % 4, 0:DK * NODE_P].rearrange("p (k n) -> p k n", k=DK)
        K.pB = lambda u: K.PS[:NODE_P, 4 + u % 3, 0:D]
        K.landed = [sem(f"landed{s}") for s in range(RING)]
        K.landed_total = [16 * GRP if s < GRP else 0 for s in range(RING)]
        K.index_staged, K.staged_total = [sem(f"index_staged{h}") for h in range(2)], 0
        K.dve_own, K.waits_passed = sem("dve_own"), sem("waits_passed")
        K.dstf_dram = dram("dstf_dram", [LANES, STEPS])
        K.cnt_dram = dram("cnt_dram", [N + 1])
        K.btab2 = dram("btab", [N, D])
        K.btab = K.btab2.rearrange("(p t) d -> p t d", t=NT)
        wk = lambda name: ins[name].rearrange("(k p) n -> p k n", p=128)
        K.early_loads = [(K.wphi[:], wk("phi_wT")), (K.wtheta[:], wk("theta_wT"))]
        K.hist = dram("hist", [LANES * STEPS + 1, D])
        K.hist3 = K.hist[0:LANES * STEPS, :].rearrange("(p k) d -> p k d", k=STEPS)
        K.in_src = ins["src"]
        stages = (setup, gather0_mix0, ends0, experts0, relations, gather1_mix1, ends1, experts1)
        for stage in stages:
            own_sems = []

            def stage_sem(name):
                own_sems.append(sem(name))
                return own_sems[-1]
            stage(nc, K, stage_sem)
            if stage is not experts1:
                nc.clear_and_free_semaphores(own_sems)
                nc.all_engine_barrier()


def laid_out(inputs):
    import numpy as np
    a = {k: np.ascontiguousarray(v) for k, v in inputs.items()}
    lanes = lambda e, fill: np.concatenate([e, np.full(LANES * STEPS - EDGES, fill, e.dtype)]).reshape(LANES, STEPS)
    staged = lambda e: np.pad(e, ((0, 0), (0, RING - TAIL)))
    out = {
        "x": a["x"], "src": staged(lanes(a["src"], 0)), "dst": lanes(a["dst"], N), "etype": staged(lanes(a["edge_type_8"], 0)),
        "theta_wT": a["L0_gnn_theta_w"].T, "phi_wT": a["L0_gnn_phi_w"].T,
        "theta_b": a["L0_gnn_theta_b"].reshape(1, D), "phi_b": a["L0_gnn_phi_b"].reshape(1, D),
        "mix0_qk": a["L0_mix_W_qkv"][:, :2 * D], "mix0_v": a["L0_mix_W_qkv"][:, 2 * D:],
        "mix0_vT": a["L0_mix_W_qkv"][:, 2 * D:].T, "mix0_b": a["L0_mix_b_qkv"].reshape(1, 3 * D),
        "mix0_bvT": a["L0_mix_b_qkv"][2 * D:].reshape(DK, 128).T,
        "mix0_out": a["L0_mix_W_out"], "mix0_bout": a["L0_mix_b_out"].reshape(1, D),
        "ffn0_Wr": a["L0_ffn_Wr"], "ffn0_br": a["L0_ffn_br"].reshape(1, E8),
        "basis": a["L1_gnn_basis"].reshape(4 * D, D), "comp": a["L1_gnn_comp"].reshape(1, 32), "loop_w": a["L1_gnn_loop_w"],
        "h_bias": a["L1_gnn_h_bias"].reshape(1, D),
        "mix1_qkv": a["L1_mix_W_qkv"], "mix1_out": a["L1_mix_W_out"], "mix1_bout": a["L1_mix_b_out"].reshape(1, D),
        "ffn1_Wr": a["L1_ffn_Wr"], "ffn1_br": a["L1_ffn_br"].reshape(1, E8),
        "gamma_beta0": np.concatenate([a["L0_ffn_gamma"], a["L0_ffn_beta"]]).reshape(1, 2 * D),
        "gamma_beta1": np.concatenate([a["L1_gnn_ln_gamma"], a["L1_gnn_ln_beta"]]).reshape(1, 2 * D),
        "gamma_beta2": np.concatenate([a["L1_ffn_gamma"], a["L1_ffn_beta"]]).reshape(1, 2 * D),
    }
    for n in (0, 1):
        out[f"ffn{n}_W1"] = a[f"L{n}_ffn_W1"].reshape(E8, DK, 128, F).transpose(0, 2, 1, 3).reshape(E8 * 128, DK * F)
        out[f"ffn{n}_W2"] = a[f"L{n}_ffn_W2"].reshape(E8, FK, 128, D).transpose(0, 2, 1, 3).reshape(E8 * 128, FK * D)
        out[f"ffn{n}_b1"] = a[f"L{n}_ffn_b1"].reshape(E8, FK, 128).transpose(0, 2, 1).reshape(E8 * 128, FK)
    out["ffn0_b2"], out["ffn1_b2"] = a["L0_ffn_b2"], a["L1_ffn_b2"].reshape(1, E8 * D)
    return {k: np.ascontiguousarray(v) for k, v in out.items()}


def kernel(**inputs):
    import numpy as np
    import concourse.bacc as bacc
    from concourse.bass_utils import run_bass_kernel_spmd

    nc = bacc.Bacc("TRN2", target_bir_lowering=False, num_devices=1)
    arrays = laid_out(inputs)
    aps = {k: nc.dram_tensor(f"in_{k}_dram", v.shape, mybir.dt.from_np(v.dtype), kind="ExternalInput").ap() for k, v in arrays.items()}
    out = nc.dram_tensor("out_dram", (N, D), F32, kind="ExternalOutput").ap()
    program(nc, out, aps)
    got = run_bass_kernel_spmd(nc, [{f"in_{k}_dram": v for k, v in arrays.items()}], core_ids=[0])
    return got.results[0]["out_dram"]
```
